# Optimizing a Trainium2 kernel written in Bass

```python
import numpy as np
import jax
import jax.numpy as jnp

def _softmax(x, axis=-1):
    return jax.nn.softmax(x, axis=axis)

def _gelu(x):
    return jax.nn.gelu(x, approximate=True)

def _silu(x):
    return jax.nn.silu(x)

def _sigmoid(x):
    return jax.nn.sigmoid(x)

def _layernorm(x, axis=-1, eps=1e-05):
    m = jnp.mean(x, axis=axis, keepdims=True)
    v = jnp.var(x, axis=axis, keepdims=True)
    return (x - m) / jnp.sqrt(v + eps)

def _scatter_add(tgt, idx, src, axis=0):
    return tgt.at[idx].add(src)

def _segment_sum(src, seg, n):
    return jax.ops.segment_sum(src, seg, n)
kernel_name = 'mk_vit_tower_d1_tok_img1024_r4_df1b41'

def setup_inputs(seed: int=0):
    np.random.seed(seed)
    _w = jnp.asarray

    def _rec_inputs():
        import jax
        import jax.numpy as jnp
        _rk = jax.random.key(seed)
        x = -0.000392918 + 0.999932 * jax.random.normal(jax.random.fold_in(_rk, 1), (16, 256, 256, 1), jnp.float32)
        return x
    x = _rec_inputs()

    def _L0_tok_setup():
        import jax, jax.numpy as jnp
        import numpy as np
        INV_SQRT2 = 0.7071067811865476
        LEVEL = 3

        def _split(x, axis):
            ax = axis % x.ndim
            sl0 = [slice(None)] * x.ndim
            sl0[ax] = slice(0, None, 2)
            sl1 = [slice(None)] * x.ndim
            sl1[ax] = slice(1, None, 2)
            x0, x1 = (x[tuple(sl0)], x[tuple(sl1)])
            return ((x0 + x1) * INV_SQRT2, (x0 - x1) * INV_SQRT2)

        def _merge(lo, hi, axis):
            ax = axis % lo.ndim
            e = (lo + hi) * INV_SQRT2
            o = (lo - hi) * INV_SQRT2
            s = jnp.stack([e, o], axis=ax + 1)
            shape = list(lo.shape)
            shape[ax] *= 2
            return s.reshape(shape)

        def _dwt2(x):
            lo, hi = _split(x, -1)
            a, h = _split(lo, -2)
            v, d = _split(hi, -2)
            return (a, h, v, d)

        def _idwt2(a, h, v, d):
            lo = _merge(a, h, -2)
            hi = _merge(v, d, -2)
            return _merge(lo, hi, -1)
        key = jax.random.key(seed)
        ks = jax.random.split(key, 8)
        B, H, W = (16, 256, 256)
        x = jax.random.normal(ks[0], (B, H, W, 1), dtype=jnp.float32)
        na = H // 8 * (W // 8)
        n2 = H // 4 * (W // 4)
        n1 = H // 2 * (W // 2)
        scale = 0.02
        Wa = jax.random.normal(ks[1], (na, 1), dtype=jnp.float32) * scale
        ba = jnp.zeros((1,), jnp.float32)
        Wd1 = jax.random.normal(ks[2], (3 * na, 3), dtype=jnp.float32) * scale
        bd1 = jnp.zeros((3,), jnp.float32)
        Wd2 = jax.random.normal(ks[3], (3 * n2, 3), dtype=jnp.float32) * scale
        bd2 = jnp.zeros((3,), jnp.float32)
        Wd3 = jax.random.normal(ks[4], (3 * n1, 3), dtype=jnp.float32) * scale
        bd3 = jnp.zeros((3,), jnp.float32)
        return {'x': x, 'Wa': Wa, 'ba': ba, 'Wd1': Wd1, 'bd1': bd1, 'Wd2': Wd2, 'bd2': bd2, 'Wd3': Wd3, 'bd3': bd3}
    _L0_tok_all = _L0_tok_setup()
    _L0_tok_in = {k: v for k, v in _L0_tok_all.items() if k in ('Wa', 'ba', 'Wd1', 'bd1', 'Wd2', 'bd2', 'Wd3', 'bd3')}
    del _L0_tok_all

    def _L0_attn_setup():
        import jax, jax.numpy as jnp
        import numpy as np
        B, S, D, K = (4, 2048, 256, 16)
        TEMPERATURE = 1.0

        def _affinities(tokens, centers, log_scales):
            t_sq = jnp.sum(tokens * tokens, axis=-1, keepdims=True)
            c_sq = jnp.sum(centers * centers, axis=-1)
            cross = jnp.einsum('bsd,kd->bsk', tokens, centers)
            dist_sq = jnp.maximum(t_sq - 2.0 * cross + c_sq, 0.0)
            scales = jnp.clip(jnp.exp(log_scales), 0.1, 2.0)
            aff = jnp.exp(-0.5 * dist_sq / (scales * scales))
            aff = aff ** (1.0 / TEMPERATURE)
            return aff / (jnp.sum(aff, axis=-1, keepdims=True) + 1e-08)
        key = jax.random.key(seed)
        k0, k1, k2, k3 = jax.random.split(key, 4)
        token_embeddings = jax.random.normal(k0, (B, S, D), dtype=jnp.float32)
        splat_centers = jax.random.normal(k1, (K, D), dtype=jnp.float32) * 0.02
        splat_log_scales = jnp.full((K,), jnp.log(0.5), dtype=jnp.float32)
        lim = float(np.sqrt(6.0 / (D + D)))
        W_v = jax.random.uniform(k2, (D, D), minval=-lim, maxval=lim, dtype=jnp.float32)
        W_o = jax.random.uniform(k3, (D, D), minval=-lim, maxval=lim, dtype=jnp.float32)
        return {'token_embeddings': token_embeddings, 'splat_centers': splat_centers, 'splat_log_scales': splat_log_scales, 'W_v': W_v, 'W_o': W_o}
    _L0_attn_all = _L0_attn_setup()
    _L0_attn_in = {k: v for k, v in _L0_attn_all.items() if k in ('splat_centers', 'splat_log_scales', 'W_v', 'W_o')}
    del _L0_attn_all

    def _L0_ffn_setup():
        import jax, jax.numpy as jnp
        import numpy as np
        B, S, D, H, E, F, K = (2, 256, 256, 16, 8, 1024, 2)
        EPS = 1e-05

        def _layernorm(x, g, b):
            mu = jnp.mean(x, axis=-1, keepdims=True)
            var = jnp.mean(jnp.square(x - mu), axis=-1, keepdims=True)
            return (x - mu) * jax.lax.rsqrt(var + EPS) * g + b
        key = jax.random.key(seed)
        ks = jax.random.split(key, 12)
        w = lambda k, shape: jax.random.normal(k, shape, dtype=jnp.float32) * 0.02
        return {'x': jax.random.normal(ks[0], (B, S, D), dtype=jnp.float32), 'ln1_g': jnp.ones((D,), jnp.float32), 'ln1_b': jnp.zeros((D,), jnp.float32), 'ln2_g': jnp.ones((D,), jnp.float32), 'ln2_b': jnp.zeros((D,), jnp.float32), 'Wq': w(ks[1], (D, D)), 'Wk': w(ks[2], (D, D)), 'Wv': w(ks[3], (D, D)), 'Wo': w(ks[4], (D, D)), 'Wg': w(ks[5], (D, E)), 'W1': w(ks[6], (E, D, F)), 'b1': jnp.zeros((E, F), jnp.float32), 'W2': w(ks[7], (E, F, D)), 'b2': jnp.zeros((E, D), jnp.float32)}
    _L0_ffn_all = _L0_ffn_setup()
    _L0_ffn_in = {k: v for k, v in _L0_ffn_all.items() if k in ('ln1_g', 'ln1_b', 'ln2_g', 'ln2_b', 'Wq', 'Wk', 'Wv', 'Wo', 'Wg', 'W1', 'b1', 'W2', 'b2')}
    del _L0_ffn_all
    return {'x': x, 'L0_tok_Wa': _L0_tok_in['Wa'], 'L0_tok_ba': _L0_tok_in['ba'], 'L0_tok_Wd1': _L0_tok_in['Wd1'], 'L0_tok_bd1': _L0_tok_in['bd1'], 'L0_tok_Wd2': _L0_tok_in['Wd2'], 'L0_tok_bd2': _L0_tok_in['bd2'], 'L0_tok_Wd3': _L0_tok_in['Wd3'], 'L0_tok_bd3': _L0_tok_in['bd3'], 'L0_attn_splat_centers': _L0_attn_in['splat_centers'], 'L0_attn_splat_log_scales': _L0_attn_in['splat_log_scales'], 'L0_attn_W_v': _L0_attn_in['W_v'], 'L0_attn_W_o': _L0_attn_in['W_o'], 'L0_ffn_ln1_g': _L0_ffn_in['ln1_g'], 'L0_ffn_ln1_b': _L0_ffn_in['ln1_b'], 'L0_ffn_ln2_g': _L0_ffn_in['ln2_g'], 'L0_ffn_ln2_b': _L0_ffn_in['ln2_b'], 'L0_ffn_Wq': _L0_ffn_in['Wq'], 'L0_ffn_Wk': _L0_ffn_in['Wk'], 'L0_ffn_Wv': _L0_ffn_in['Wv'], 'L0_ffn_Wo': _L0_ffn_in['Wo'], 'L0_ffn_Wg': _L0_ffn_in['Wg'], 'L0_ffn_W1': _L0_ffn_in['W1'], 'L0_ffn_b1': _L0_ffn_in['b1'], 'L0_ffn_W2': _L0_ffn_in['W2'], 'L0_ffn_b2': _L0_ffn_in['b2']}

def reference(x, L0_tok_Wa, L0_tok_ba, L0_tok_Wd1, L0_tok_bd1, L0_tok_Wd2, L0_tok_bd2, L0_tok_Wd3, L0_tok_bd3, L0_attn_splat_centers, L0_attn_splat_log_scales, L0_attn_W_v, L0_attn_W_o, L0_ffn_ln1_g, L0_ffn_ln1_b, L0_ffn_ln2_g, L0_ffn_ln2_b, L0_ffn_Wq, L0_ffn_Wk, L0_ffn_Wv, L0_ffn_Wo, L0_ffn_Wg, L0_ffn_W1, L0_ffn_b1, L0_ffn_W2, L0_ffn_b2):
    import jax
    import jax.numpy as jnp

    def _L0_tok_ref(x, Wa, ba, Wd1, bd1, Wd2, bd2, Wd3, bd3):
        import jax, jax.numpy as jnp
        import numpy as np
        INV_SQRT2 = 0.7071067811865476
        LEVEL = 3

        def _split(x, axis):
            ax = axis % x.ndim
            sl0 = [slice(None)] * x.ndim
            sl0[ax] = slice(0, None, 2)
            sl1 = [slice(None)] * x.ndim
            sl1[ax] = slice(1, None, 2)
            x0, x1 = (x[tuple(sl0)], x[tuple(sl1)])
            return ((x0 + x1) * INV_SQRT2, (x0 - x1) * INV_SQRT2)

        def _merge(lo, hi, axis):
            ax = axis % lo.ndim
            e = (lo + hi) * INV_SQRT2
            o = (lo - hi) * INV_SQRT2
            s = jnp.stack([e, o], axis=ax + 1)
            shape = list(lo.shape)
            shape[ax] *= 2
            return s.reshape(shape)

        def _dwt2(x):
            lo, hi = _split(x, -1)
            a, h = _split(lo, -2)
            v, d = _split(hi, -2)
            return (a, h, v, d)

        def _idwt2(a, h, v, d):
            lo = _merge(a, h, -2)
            hi = _merge(v, d, -2)
            return _merge(lo, hi, -1)
        img = x[..., 0]
        B = img.shape[0]
        details = []
        cur = img
        for _ in range(LEVEL):
            cur, h, v, d = _dwt2(cur)
            details.append((h, v, d))
        aw = jax.nn.sigmoid(cur.reshape(B, -1) @ Wa + ba)
        rec = cur * aw[:, :, None]
        det_params = [(Wd1, bd1), (Wd2, bd2), (Wd3, bd3)]
        for (h, v, d), (Wd, bd) in zip(reversed(details), det_params):
            flat = jnp.stack([h, v, d], axis=1).reshape(B, -1)
            w = jax.nn.softmax(flat @ Wd + bd, axis=-1)
            rec = _idwt2(rec, h * w[:, 0, None, None], v * w[:, 1, None, None], d * w[:, 2, None, None])
        return rec

    def _L0_attn_ref(token_embeddings, splat_centers, splat_log_scales, W_v, W_o):
        import jax, jax.numpy as jnp
        import numpy as np
        B, S, D, K = (4, 2048, 256, 16)
        TEMPERATURE = 1.0

        def _affinities(tokens, centers, log_scales):
            t_sq = jnp.sum(tokens * tokens, axis=-1, keepdims=True)
            c_sq = jnp.sum(centers * centers, axis=-1)
            cross = jnp.einsum('bsd,kd->bsk', tokens, centers)
            dist_sq = jnp.maximum(t_sq - 2.0 * cross + c_sq, 0.0)
            scales = jnp.clip(jnp.exp(log_scales), 0.1, 2.0)
            aff = jnp.exp(-0.5 * dist_sq / (scales * scales))
            aff = aff ** (1.0 / TEMPERATURE)
            return aff / (jnp.sum(aff, axis=-1, keepdims=True) + 1e-08)
        aff = _affinities(token_embeddings, splat_centers, splat_log_scales)
        values = token_embeddings @ W_v
        splat_states = jnp.einsum('bsk,bsd->bkd', aff, values)
        token_outputs = jnp.einsum('bsk,bkd->bsd', aff, splat_states)
        return token_outputs @ W_o

    def _L0_ffn_ref(x, ln1_g, ln1_b, ln2_g, ln2_b, Wq, Wk, Wv, Wo, Wg, W1, b1, W2, b2):
        import jax, jax.numpy as jnp
        import numpy as np
        B, S, D, H, E, F, K = (2, 256, 256, 16, 8, 1024, 2)
        EPS = 1e-05

        def _layernorm(x, g, b):
            mu = jnp.mean(x, axis=-1, keepdims=True)
            var = jnp.mean(jnp.square(x - mu), axis=-1, keepdims=True)
            return (x - mu) * jax.lax.rsqrt(var + EPS) * g + b
        Bb, Ss, Dd = x.shape
        Dh = Dd // H
        h = _layernorm(x, ln1_g, ln1_b)
        q = (h @ Wq).reshape(Bb, Ss, H, Dh)
        k = (h @ Wk).reshape(Bb, Ss, H, Dh)
        v = (h @ Wv).reshape(Bb, Ss, H, Dh)
        scores = jnp.einsum('bqhd,bkhd->bhqk', q, k) / jnp.sqrt(jnp.float32(Dh))
        attn = jax.nn.softmax(scores, axis=-1)
        ctx = jnp.einsum('bhqk,bkhd->bqhd', attn, v).reshape(Bb, Ss, Dd)
        x = x + ctx @ Wo
        m = _layernorm(x, ln2_g, ln2_b)
        xt = m.reshape(-1, Dd)
        T = xt.shape[0]
        probs = jax.nn.softmax(xt @ Wg, axis=-1)
        wts, idx = jax.lax.top_k(probs, K)
        wts = wts / jnp.sum(wts, axis=-1, keepdims=True)
        h1 = jax.nn.gelu(jnp.einsum('td,edf->etf', xt, W1) + b1[:, None, :])
        ye = jnp.einsum('etf,efd->etd', h1, W2) + b2[:, None, :]
        sel = ye[idx, jnp.arange(T)[:, None], :]
        moe_out = jnp.sum(wts[..., None] * sel, axis=1).reshape(Bb, Ss, Dd)
        return x + moe_out
    h = _L0_tok_ref(x, L0_tok_Wa, L0_tok_ba, L0_tok_Wd1, L0_tok_bd1, L0_tok_Wd2, L0_tok_bd2, L0_tok_Wd3, L0_tok_bd3)
    h = h + _L0_attn_ref(_layernorm(h, axis=-1), L0_attn_splat_centers, L0_attn_splat_log_scales, L0_attn_W_v, L0_attn_W_o)
    h = h + _L0_ffn_ref(_layernorm(h, axis=-1), L0_ffn_ln1_g, L0_ffn_ln1_b, L0_ffn_ln2_g, L0_ffn_ln2_b, L0_ffn_Wq, L0_ffn_Wk, L0_ffn_Wv, L0_ffn_Wo, L0_ffn_Wg, L0_ffn_W1, L0_ffn_b1, L0_ffn_W2, L0_ffn_b2)
    return h

_drawn_inputs = setup_inputs


def setup_inputs(seed=0):
    import zlib

    import numpy as np

    out = dict(_drawn_inputs(seed))
    spreads = {'L0_tok_bd1': (0.0, 0.494),
     'L0_tok_bd2': (0.0, 0.654),
     'L0_tok_bd3': (0.0, 0.8),
     'L0_attn_splat_log_scales': (-0.6931471824645996, 0.2),
     'L0_ffn_ln1_g': (1.0, 0.6),
     'L0_ffn_ln1_b': (0.0, 0.8),
     'L0_ffn_ln2_g': (1.0, 0.6),
     'L0_ffn_ln2_b': (0.0, 1.198),
     'L0_ffn_b1': (0.0, 1.277),
     'L0_ffn_b2': (0.0, 0.505)}
    factors = {'L0_ffn_Wq': 8.0,
     'L0_ffn_Wk': 8.0,
     'L0_ffn_Wv': 5.248,
     'L0_ffn_Wo': 5.024,
     'L0_ffn_W1': 2.723}
    for name, (base, spread) in spreads.items():
        noise = np.random.default_rng([zlib.crc32(name.encode()), seed]).standard_normal(out[name].shape)
        drawn = base * np.exp(spread * noise) if base else spread * noise
        out[name] = jnp.asarray(drawn.astype(out[name].dtype))
    for name, factor in factors.items():
        out[name] = (out[name] * factor).astype(out[name].dtype)
    return out
```

```python
from contextlib import ExitStack

import concourse.bass as bass
from concourse import mybir

ALU = mybir.AluOpType
ACT = mybir.ActivationFunctionType
F32 = mybir.dt.float32
F16 = mybir.dt.float16
BF16 = mybir.dt.bfloat16
I32 = mybir.dt.int32
U32 = mybir.dt.uint32
AX = mybir.AxisListType

P = 128
B = 16
S = 256
D = 256
T = B * S
H, DH = 16, 16
K = 16
E, F = 8, 1024
NC = D // P
NS = S // P
FC = F // P
TT = 256
NT = 2 * T // TT + E - 1
NSLOT = NT * TT
NCOL = NSLOT // P
EPS = 1e-5
WS = 64.0

G4 = 4
NG = B // G4
RB = P // G4
RROWS = S // RB


class Count:

    def __init__(self, sem, per, unit=1, opened=True):
        self.sem, self.per, self.unit, self.opened = sem, per, unit, opened

    def open(self, eng):
        eng.sem_inc(self.sem, self.per * self.unit)

    def sig(self, ins):
        ins.then_inc(self.sem, self.unit)

    def wait(self, eng, i, n, alone=None):
        self.await_(eng, (i + self.opened) * (self.per * self.unit) + n * self.unit, alone)

    def wait_before(self, eng, i, n, alone=None):
        self.await_(eng, i * (self.per * self.unit) + n * self.unit, alone)

    def await_(self, eng, value, alone):
        eng.wait_ge(self.sem, value)
        if alone:
            eng.sem_inc(alone, 1)


class Chain:

    def __init__(self, sem, per):
        self.c, self.n = Count(sem, per), 0

    def start(self, eng, i):
        self.eng, self.i, self.n = eng, i, 0

    def link(self, ins, alone=None):
        self.n += 1
        self.c.sig(ins)
        self.c.wait(self.eng, self.i, self.n, alone)

    def end(self):
        assert self.n == self.c.per, (self.n, self.c.per)


def tower(nc, a, out, dbg=None, upto=9):
    with ExitStack() as ctx:
        build(nc, ctx, a, out, dbg, upto)


def build(nc, ctx, a, out, dbg, upto):
    def sb(name, shape, dt=F32):
        return ctx.enter_context(nc.sbuf_tensor(name, shape, dt))

    def sem(name):
        return ctx.enter_context(nc.semaphore(name))

    def dram(name, shape, dt):
        return nc.dram_tensor(name, shape, dt).ap()

    rec_dram = dram("rec_rows", [T, D], F32)
    h2_dram = dram("h2_rows", [T, D], F32)
    x4_dram = dram("x4_rows", [T, D], F32)
    m_dram = dram("m_rows", [T, 2 * D], F16)
    y_dram = dram("y_rows", [2 * T + NSLOT, D], F32)

    big = ctx.enter_context(nc.psum_tensor("big", [P, 2, 1024], F32))
    acc = ctx.enter_context(nc.psum_tensor("acc", [P, 4, 256], F32))
    px = ctx.enter_context(nc.psum_tensor("px", [P, 512], F32))
    py = ctx.enter_context(nc.psum_tensor("py", [P, 512], F32))

    expert_w = sb("expert_w", [P, 4, E * NC * F], F16)
    w1hi = expert_w[:, 0, :]
    w1lo = expert_w[:, 1, :].bitcast(BF16)
    w2hi = expert_w[:, 2, :]
    w2lo = expert_w[:, 3, :].bitcast(BF16)
    arena1 = expert_w[:, :, :].rearrange("p a b -> p (a b)").bitcast(F32)
    used = [0]

    def a1(n):
        used[0] += n
        assert used[0] <= 2 * E * NC * F
        return arena1[:, used[0] - n:used[0]]

    X = RROWS * D
    xin = [a1(X), a1(X)]
    rec = [a1(X), a1(X)]
    col_s, col_d = a1(X // 2), a1(X // 2)
    det = {1: a1(3 * X // 4), 2: a1(3 * X // 16), 3: a1(3 * X // 64)}
    app = {1: a1(X // 4), 2: a1(X // 16), 3: a1(X // 64)}
    wdet = {1: a1(9 * X // 4), 2: a1(9 * X // 16), 3: a1(9 * X // 64)}
    wapp = a1(X // 64)
    junk = a1(3 * X // 4)
    part = a1(10)
    bias10, rscale = a1(10), a1(10)
    z10, e10, w10, nw10 = a1(10), a1(10), a1(10), a1(10)
    s3, r3 = a1(3), a1(3)

    NWORK = 13920
    work = sb("work", [P, NWORK])
    at = [0]

    def wk(n):
        at[0] += n
        assert at[0] <= NWORK, at[0]
        return work[:, at[0] - n:at[0]]

    v3 = lambda t, n: t.rearrange("p (a b) -> p a b", a=n)
    h_t = v3(wk(512), 2)
    t0 = v3(wk(512), 2)
    t0T = v3(wk(512), 2)
    h2 = v3(wk(512), 2)
    x3 = wk(1024)
    hhT = v3(wk(512), 2)
    qst = v3(wk(1024).bitcast(F16), 8)
    kst = v3(wk(1024).bitcast(F16), 8)
    vext = wk(1024).rearrange("p (c h e) -> p c h e", c=NS, h=H)
    pt = wk(2048).rearrange("p (b r c q) -> p b r c q", b=2, r=2, c=NS)
    qk_hi = pt[:, 0].rearrange("p r c q -> p (r c q)")[:, 0:512].bitcast(F16)
    qk_lo = pt[:, 0].rearrange("p r c q -> p (r c q)")[:, 512:1024].bitcast(F16)
    ctxn = v3(wk(1024), 4)
    x4 = v3(wk(512), 2)
    m = v3(wk(512), 2)
    mhl = v3(wk(512).bitcast(F16), 2)
    mT = v3(wk(512), 2)
    wraw = wk(1024)
    mid = at[0]
    st = wk(12).rearrange("p (t n) -> p t n", t=NS)
    mv = wk(4).rearrange("p (t n) -> p t n", t=NS)
    var, rstd = wk(2), wk(2)
    stc = wk(12).rearrange("p (t n) -> p t n", t=NS)
    mvc = wk(4).rearrange("p (t n) -> p t n", t=NS)
    varc, rstdc = wk(2), wk(2)
    tsq, affsum, affrec = wk(2), wk(2), wk(2)
    dist = v3(wk(32), 2)
    aff = v3(wk(32), 2)
    ut = v3(wk(32), 2)
    affT = wk(256)[0:K, :]
    zs = wk(256)[0:K, :]
    sqj = v3(wk(256).bitcast(BF16), 2)
    mx = v3(wk(32), 2)
    neghl = v3(wk(32).bitcast(F16), 2)
    negmT = wk(128).bitcast(F16)[0:32, :]

    ident = sb("ident", [P, P])
    ident16 = sb("ident16", [P, P], F16)
    blk = sb("blk", [P, P])
    ones = sb("ones", [P, P])
    tri = sb("tri", [P, P])
    halfneg = sb("halfneg", [P, 2])
    kone = sb("kone", [P, 1])
    sel = sb("sel", [P, 4, 4, 128], F16)
    selm = sb("selm", [32, 8, 2, 64], F16)
    csq_b = sb("csq_b", [P, 2, K])
    wq, wk_, wv = (sb(n, [P, NC, D]) for n in ("wq", "wk", "wv"))
    wop = sb("wop", [P, 4, D])
    wvo = sb("wvo", [P, NC, D])
    g1, b1 = sb("g1", [P, NC]), sb("b1ln", [P, NC])
    g2b, b2b = sb("g2b", [P, D]), sb("b2b", [P, D])
    wg = sb("wg", [P, NC, E])
    cT = sb("cT", [P, NC, K])
    lall = sb("lall", [P, 2 * B, E])

    at[0] = 0
    rt = lambda n: wk(n)
    NTL = 2 * B
    te3 = lambda t: t.rearrange("p (t e) -> p t e", e=E)
    mask1, mask2, cmask, cand, lrest, ra, rb_, rank = (rt(NTL * E) for _ in range(8))
    mx1, mx2, pick = rt(NTL), rt(NTL), rt(NTL)
    wts = sb("wts", [P, 2, NTL])
    pos = rt(2 * NTL)
    pos_i, posa_i, posb_i = (rt(2 * NTL).bitcast(I32) for _ in range(3))
    posa, posb = rt(2 * NTL), rt(2 * NTL)
    ntile, tbase, tend = rt(E), rt(E), rt(E)
    cmp = rt(E * 16)
    tcmp = rt(NT * E)
    tef = rt(NT)
    iota_i = rt(P).bitcast(I32)
    iota_f = rt(P)
    iota_h = rt(P // 2).bitcast(F16)
    iota_p = rt(1)
    iota_pi = rt(1).bitcast(I32)
    jstep = rt(16)
    slot_i = rt(NCOL).bitcast(I32)
    slot_f = rt(NCOL)
    hotb = rt(8 * P // 2).bitcast(F16).rearrange("p (n b) -> p n b", n=8)
    hota = rt(8 * NCOL).bitcast(F16).rearrange("p (n v a) -> p n v a", n=8, v=2)
    zero16 = rt(P).bitcast(F16)
    cols1 = rt(2 * NTL)
    minus_p = rt(NCOL)
    tok, emp, dest = rt(NCOL), rt(NCOL), rt(NCOL)
    tex = sb("tex", [1, NT], I32)
    src_idx, dst_idx = sb("src_idx", [P, NCOL], U32), sb("dst_idx", [P, NCOL], U32)
    gidx, sidx = sb("gidx", [P, 2], U32), sb("sidx", [P, 2], U32)
    at[0] = 0
    b2e = wk(E * D)
    b1e = wk(E * FC)
    xg = v3(wk(512).bitcast(F16), 2)
    xT_hi = v3(wk(256).bitcast(F16), 2)
    xT_lo = v3(wk(256).bitcast(BF16), 2)
    hf = v3(wk(2048), FC)
    h_hi = v3(wk(1024).bitcast(F16), FC)
    h_lo = v3(wk(1024).bitcast(BF16), FC)
    ys = v3(wk(512), 2)
    at[0] = 0
    comb = [[v3(wk(512), 2) for _ in range(5)] for _ in range(2)]
    ident_bf = sb("ident_bf", [P, P], BF16)

    img = lambda d: d.rearrange("(i t p) d -> i p t d", t=NS, p=P)

    passed_dve, passed_pool, passed_sp = sem("passed_dve"), sem("passed_pool"), sem("passed_sp")

    const_ld, const_pool, const_dve = sem("const_ld"), sem("const_pool"), sem("const_dve")
    prep_pe, prep_dve, prep_act = sem("prep_pe"), sem("prep_dve"), sem("prep_act")
    dwt_w_ld = sem("dwt_w_ld")

    x_ld = [sem("x_ld0"), sem("x_ld1")]
    dwt_chain = Chain(sem("dwt_chain"), 32)
    part_ready = Count(sem("part_ready"), 1)
    part_sum = Count(sem("part_sum"), 1)
    dwt_logits = Count(sem("dwt_logits"), 1)
    band_logit = Count(sem("band_logit"), 1)
    band_exp = Count(sem("band_exp"), 2)
    rec_ready = Count(sem("rec_ready"), 1)
    rec_stored = Count(sem("rec_stored"), 1, 16)

    C = {}

    def cnt(name, per=1, unit=1):
        C[name] = Count(sem(name), per, unit)
        return C[name]

    h_ld = cnt("h_ld", 1, 16)
    var_a, rstd_a = cnt("var_a", 3), cnt("rstd_a", 3)
    t0_ready, tsq_ready = cnt("t0_ready"), cnt("tsq_ready")
    px_written = cnt("px_written", 6)
    t0T_ready, dist_ready, aff_exp = cnt("t0T_ready"), cnt("dist_ready"), cnt("aff_exp")
    aff_ready, ut_ready, z_ready = cnt("aff_ready"), cnt("ut_ready"), cnt("z_ready")
    h2_ready, h2_stored = cnt("h2_ready"), cnt("h2_stored", 1, 16)
    hn_ready, hhT_ready = cnt("hn_ready"), cnt("hhT_ready")
    big_written = cnt("big_written", 24)
    big_hi = cnt("big_hi", 1)
    big_act = cnt("big_act", 12)
    big_dve = cnt("big_dve", 12)
    negm_ready, negmT_psum, negmT_ready = cnt("negm_ready"), cnt("negmT_psum"), cnt("negmT_ready")
    pv_done, ctx_ready = cnt("pv_done", 8), cnt("ctx_ready")
    py_written = cnt("py_written", 3)
    x4_ready, x4_stored = cnt("x4_ready"), cnt("x4_stored", 1, 16)
    var_c, rstd_c, m0_ready, m_ready = cnt("var_c"), cnt("rstd_c"), cnt("m0_ready"), cnt("m_ready")
    mhl_ready, mhl_stored = cnt("mhl_ready"), cnt("mhl_stored", 1, 16)
    mT_ready, logit_read = cnt("mT_ready"), cnt("logit_read")
    w_ld, w_hi, w_lo = cnt("w_ld", 2, 16), cnt("w_hi", 2), cnt("w_lo", 2)
    dve_a, dve_b, dve_c = Chain(sem("dve_a"), 12), Chain(sem("dve_b"), 3), Chain(sem("dve_c"), 2)
    pool_c = Chain(sem("pool_c"), 2)

    READER = ["A", "D", "A", "D", "A", "D"] + ["D"] * 8 + ["A", "D"] + ["A"] * 8
    assert len(READER) == 24
    order = [READER[:u].count(READER[u]) + 1 for u in range(24)]
    N_A, N_D = READER.count("A"), READER.count("D")
    assert (N_A, N_D) == (12, 12)

    def slot_free(i, u):
        before = C["big_act"] if READER[u - 2] == "A" else C["big_dve"]
        (before.wait if u >= 2 else before.wait_before)(nc.tensor, i, order[u - 2])

    tri_ready = sem("tri_ready")
    ROUTE_RANKS = 45
    img_done_act, img_done_pe = sem("img_done_act"), sem("img_done_pe")
    r_dve, r_pool, r_act, r_pe, r_ld = sem("r_dve"), sem("r_pool"), sem("r_act"), sem("r_pe"), sem("r_ld")
    hot_ready, hot_used = Count(sem("hot_ready"), 2), Count(sem("hot_used"), 2)
    route_done = sem("route_done")
    x_in = Count(sem("x_in"), 2, 16, opened=False)
    xT_psum, xT_hi_ready, xT_lo_ready = Count(sem("xT_psum"), 1), Count(sem("xT_hi_ready"), 1), Count(sem("xT_lo_ready"), 1)
    up_done, gelu_done, split_done = Count(sem("up_done"), 2), Count(sem("gelu_done"), 2), Count(sem("split_done"), 2)
    hi_chain = Count(sem("hi_chain"), 2)
    down_done, y_ready = Count(sem("down_done"), 1), Count(sem("y_ready"), 1)
    y_out = Count(sem("y_out"), 2, 16, opened=False)
    y_free = Count(sem("y_free"), 1)
    src_ready, dst_ready = Count(sem("src_ready"), 1), Count(sem("dst_ready"), 1)
    c_in = [Count(sem(f"c_in{k}"), 4, 16) for k in range(2)]
    c_sum, c_out, c_first = Count(sem("c_sum"), 2), [Count(sem(f"c_out{k}"), 1, 16) for k in range(2)], Count(sem("c_first"), 2)
    c_done, c_mid = Count(sem("c_done"), 2), Count(sem("c_mid"), 2)
    ROUTE_MASKS = 15

    def expert(eng, j):
        return eng.value_load(tex[0:1, bass.ds(j, 1)], min_val=0, max_val=E - 1)

    block = ctx.enter_context(nc.Block())

    @block.sync
    def _(sp):
        for c in (rec_stored, h_ld, h2_stored, x4_stored, mhl_stored, w_ld):
            c.open(sp)
        for lv, name, n in ((1, "L0_tok_Wd3", X // 4), (2, "L0_tok_Wd2", X // 16), (3, "L0_tok_Wd1", X // 64)):
            src = a[name].rearrange("(b r n) o -> r b (n o)", b=3, r=RB)
            dst = wdet[lv].rearrange("p (b n) -> p b n", b=3)
            for q in range(G4):
                sp.dma_start(dst[RB * q:RB * (q + 1)], src).then_inc(dwt_w_ld, 16)
        for q in range(G4):
            sp.dma_start(wapp[RB * q:RB * (q + 1)], a["L0_tok_Wa"].rearrange("(r n) o -> r (n o)", r=RB)).then_inc(dwt_w_ld, 16)
        for k, name in enumerate(("L0_tok_ba", "L0_tok_bd1", "L0_tok_bd2", "L0_tok_bd3")):
            dst = bias10[:, 0:1] if k == 0 else bias10[:, 3 * k - 2:3 * k + 1]
            sp.dma_start(dst, a[name].partition_broadcast(P)).then_inc(dwt_w_ld, 16)
        xg = a["x"].rearrange("(g b) (r h) w o -> g (b r) (h w o)", b=G4, r=RB)
        rg = rec_dram.rearrange("(g p h) d -> g p (h d)", g=NG, h=RROWS)

        def store_rec(g):
            rec_ready.wait(sp, g, 1)
            sp.dma_start(rg[g], rec[g % 2]).then_inc(rec_stored.sem, 16)

        for g in range(NG):
            if g >= 2:
                rec_ready.wait(sp, g, -1)
            sp.dma_start(xin[g % 2], xg[g]).then_inc(x_ld[g % 2], 16)
            if g >= 1:
                store_rec(g - 1)
        store_rec(NG - 1)

        rec_stored.wait(sp, NG - 1, 1)
        sp.wait_ge(prep_pe, 1)
        w1v = a["L0_ffn_W1"].rearrange("e (c p) f -> (e c) p f", p=P)
        w2v = a["L0_ffn_W2"].rearrange("e (n q p) d -> (e n) p q d", n=2, p=P)
        with sp.Fori(0, B) as i:
            h2_ready.wait_before(sp, i, 1, alone=passed_sp)
            sp.dma_start(h_t, img(rec_dram)[i]).then_inc(h_ld.sem, 16)
            w_lo.wait_before(sp, i, 2, alone=passed_sp)
            sp.dma_start(wraw, w1v[i]).then_inc(w_ld.sem, 16)
            h2_ready.wait(sp, i, 1, alone=passed_sp)
            sp.dma_start(img(h2_dram)[i], h2).then_inc(h2_stored.sem, 16)
            w_lo.wait(sp, i, 1, alone=passed_sp)
            sp.dma_start(wraw.rearrange("p (q d) -> p q d", q=4), w2v[i]).then_inc(w_ld.sem, 16)
            x4_ready.wait(sp, i, 1, alone=passed_sp)
            sp.dma_start(img(x4_dram)[i], x4).then_inc(x4_stored.sem, 16)
            mhl_ready.wait(sp, i, 1, alone=passed_sp)
            sp.dma_start(img(m_dram)[i], mhl).then_inc(mhl_stored.sem, 16)
        for c in (h2_stored, x4_stored, mhl_stored):
            c.wait(sp, B - 1, 1)
        sp.wait_ge(route_done, 1)
        for c in (*c_in, *c_out, y_free):
            c.open(sp)
        sp.dma_start(b2e, a["L0_ffn_b2"].rearrange("e d -> (e d)").partition_broadcast(P)).then_inc(r_ld, 16)
        sp.dma_start(b1e.rearrange("p (e c) -> p e c", e=E), a["L0_ffn_b1"].rearrange("e (c p) -> p e c", p=P),
                     allow_slow_non_contiguous=True).then_inc(r_ld, 16)
        with sp.Fori(0, NT) as j:
            y_out.wait(sp, j, 2)
            sp.sem_inc(y_free.sem, 1)
        y1v, y2v = img(y_dram[0:T]), img(y_dram[T:2 * T])
        with sp.Fori(0, B // 2) as r:
            for k in range(2):
                c_out[k].wait_before(sp, r, 1, alone=passed_sp)
                for buf, src in zip(comb[k], (img(h2_dram), img(x4_dram), y1v, y2v)):
                    sp.dma_start(buf, src[r * 2 + k]).then_inc(c_in[k].sem, 16)
            for k in range(2):
                c_done.wait(sp, r, k + 1, alone=passed_sp)
                sp.dma_start(out.rearrange("i (t p) d -> i p t d", p=P)[r * 2 + k], comb[k][4]).then_inc(c_out[k].sem, 16)
        for k in range(2):
            c_out[k].wait(sp, B // 2 - 1, 1)

    @block.gpsimd
    def _(pool):
        g = nc.gpsimd
        for c in (rstd_a, rstd_c, m_ready, mhl_ready, pool_c.c):
            c.open(pool)
        g.memset(ident[:], 0.0).then_inc(const_pool, 1)
        g.memset(blk[:], 0.0).then_inc(const_pool, 1)
        g.memset(ones[:], 1.0).then_inc(const_pool, 1)
        g.memset(halfneg[:], -0.5).then_inc(const_pool, 1)
        g.memset(wop[:], 0.0).then_inc(const_pool, 1)
        g.memset(vext, 1.0).then_inc(const_pool, 1)
        g.memset(sel[:], 0.0).then_inc(const_pool, 1)
        g.memset(selm[:], 0.0).then_inc(const_pool, 1)
        pool.wait_ge(const_pool, 8)
        g.affine_select(out=ident[:], in_=ident[:], compare_op=ALU.not_equal, fill=1.0, base=0,
                        pattern=[[-1, P]], channel_multiplier=1).then_inc(const_pool, 1)
        pool.wait_ge(const_pool, 9)
        g.affine_select(out=tri[:], in_=ones[:], compare_op=ALU.is_gt, fill=0.0, base=0,
                        pattern=[[1, P]], channel_multiplier=-1).then_inc(tri_ready, 1)
        pool.wait_ge(tri_ready, 1)
        for q in range(G4):
            g.memset(blk[RB * q:RB * (q + 1), RB * q:RB * (q + 1)], 1.0).then_inc(const_pool, 1)
        pool.wait_ge(const_pool, 9 + G4)
        n = 0
        for dst, src in (
            (wq[:], a["L0_ffn_Wq"].rearrange("(c p) n -> p c n", p=P)),
            (wk_[:], a["L0_ffn_Wk"].rearrange("(c p) n -> p c n", p=P)),
            (wv[:], a["L0_ffn_Wv"].rearrange("(c p) n -> p c n", p=P)),
            (wg[:], a["L0_ffn_Wg"].rearrange("(c p) n -> p c n", p=P)),
            (h_t, a["L0_attn_W_v"].rearrange("(c p) n -> p c n", p=P)),
            (t0, a["L0_attn_W_o"].rearrange("(c p) n -> p c n", p=P)),
            (zs, a["L0_attn_splat_centers"]),
            (affT[:, 0:1], a["L0_attn_splat_log_scales"].rearrange("(k o) -> k o", o=1)),
            (g1[:], a["L0_ffn_ln1_g"].rearrange("(c p) -> p c", p=P)),
            (b1[:], a["L0_ffn_ln1_b"].rearrange("(c p) -> p c", p=P)),
            (g2b[:], a["L0_ffn_ln2_g"].partition_broadcast(P)),
            (b2b[:], a["L0_ffn_ln2_b"].partition_broadcast(P)),
        ):
            pool.dma_start(dst, src, allow_slow_non_contiguous=True).then_inc(const_ld, 16)
            n += 1
        wo_rows = a["L0_ffn_Wo"].rearrange("(g j d) n -> j d g n", g=4, j=4)
        for j in range(4):
            pool.dma_start(wop[32 * j:32 * j + DH], wo_rows[j]).then_inc(const_ld, 16)
            n += 1
        assert n == 16

        with pool.Fori(0, B) as i:
            for ln in range(3):
                var_a.wait(pool, i, ln + 1)
                g.tensor_tensor(rstd, var, halfneg[:], ALU.pow).then_inc(rstd_a.sem, 1)
            var_c.wait(pool, i, 1)
            g.tensor_tensor(rstdc, varc, halfneg[:], ALU.pow).then_inc(rstd_c.sem, 1)
            pool_c.start(pool, i)
            m0_ready.wait(pool, i, 1)
            pool_c.link(g.tensor_tensor(m, m, g2b[:].unsqueeze(1).broadcast_to([P, NS, D]), ALU.mult))
            g.tensor_tensor(m, m, b2b[:].unsqueeze(1).broadcast_to([P, NS, D]), ALU.add).then_inc(m_ready.sem, 1)
            m_ready.wait(pool, i, 1)
            mhl_stored.wait_before(pool, i, 1, alone=passed_pool)
            pool_c.link(g.tensor_copy(mhl[:, :, 0:D], m))
            g.tensor_tensor(mhl[:, :, D:2 * D].bitcast(BF16), m, mhl[:, :, 0:D], ALU.subtract).then_inc(mhl_ready.sem, 1)
            pool_c.end()
        pool.wait_ge(img_done_pe, 1)
        pool.wait_ge(img_done_act, 1)
        mhl_stored.wait(pool, B - 1, 1)
        x4_stored.wait(pool, B - 1, 1)
        g.iota(iota_i, pattern=[[1, P]], base=0, channel_multiplier=0).then_inc(r_pool, 1)
        g.iota(iota_pi, pattern=[[0, 1]], base=0, channel_multiplier=1).then_inc(r_pool, 1)
        g.iota(slot_i, pattern=[[P, NCOL]], base=2 * T + P, channel_multiplier=1).then_inc(r_pool, 1)
        g.memset(zero16, 0.0).then_inc(r_pool, 1)
        for c in (src_ready, dst_ready):
            c.open(pool)

        def gather(j):
            xT_psum.wait_before(pool, j, 1)
            g.tensor_copy(gidx[:], src_idx[:, bass.ds(j * 2, 2)]).then_inc(src_ready.sem, 1)
            src_ready.wait(pool, j, 1, alone=passed_pool)
            for t in range(2):
                g.indirect_dma_start(xg[:, t, :], None, m_dram, bass.IndirectOffsetOnAxis(ap=gidx[:, t:t + 1], axis=0)).then_inc(x_in.sem, 16)

        def scatter(j):
            y_ready.wait(pool, j, 1)
            g.tensor_copy(sidx[:], dst_idx[:, bass.ds(j * 2, 2)]).then_inc(dst_ready.sem, 1)
            dst_ready.wait(pool, j, 1, alone=passed_pool)
            for t in range(2):
                g.indirect_dma_start(y_dram, bass.IndirectOffsetOnAxis(ap=sidx[:, t:t + 1], axis=0), ys[:, t, :], None).then_inc(y_out.sem, 16)

        pool.wait_ge(route_done, 1)
        for j in range(3):
            gather(j)
        with pool.Fori(0, NT - 3) as j:
            gather(j + 3)
            scatter(j)
        for j in range(NT - 3, NT):
            scatter(j)
        c_first.open(pool)
        with pool.Fori(0, B // 2) as r:
            for k in range(2):
                c_in[k].wait(pool, r, 4)
                c_out[k].wait_before(pool, r, 1)
                g.tensor_tensor(comb[k][4], comb[k][0], comb[k][1], ALU.add).then_inc(c_first.sem, 1)

    @block.scalar
    def _(act):
        s = nc.scalar
        for c in (band_exp, tsq_ready, t0T_ready, aff_exp, ut_ready, z_ready, hhT_ready, big_hi, big_act,
                  negmT_ready, mT_ready, logit_read, w_hi):
            c.open(act)
        act.wait_ge(const_ld, 256)
        s.activation(affT[:, 1:2], affT[:, 0:1], ACT.Exp).then_inc(prep_act, 1)
        s.activation(sqj[0:K, 0, :], zs, ACT.Square, accum_out=affT[:, 2:3]).then_inc(prep_act, 1)
        for g in range(NG):
            band_logit.wait(act, g, 1)
            s.activation(e10[:, 1:10], z10[:, 1:10], ACT.Exp).then_inc(band_exp.sem, 1)
            s.activation(e10[:, 0:1], z10[:, 0:1], ACT.Exp, scale=-1.0).then_inc(band_exp.sem, 1)

        def stage_a(i):
            t0_ready.wait(act, i, 1)
            for t in range(NS):
                last = s.activation(sqj[:, t, :], t0[:, t, :], ACT.Square, accum_out=tsq[:, t:t + 1])
            tsq_ready.sig(last)
            px_written.wait(act, i, 1)
            s.copy(t0T.rearrange("p a b -> p (a b)"), px[:]).then_inc(t0T_ready.sem, 1)
            dist_ready.wait(act, i, 1)
            s.activation(aff, dist, ACT.Exp).then_inc(aff_exp.sem, 1)
            px_written.wait(act, i, 3)
            s.copy(ut, px[:, 0:32].rearrange("p (a b) -> p a b", a=2))
            s.copy(affT, px[0:K, 256:512]).then_inc(ut_ready.sem, 1)
            px_written.wait(act, i, 4)
            s.copy(zs, px[0:K, 0:256]).then_inc(z_ready.sem, 1)
            px_written.wait(act, i, 6)
            big_written.wait_before(act, i, 2)
            for c in range(NC):
                last = s.activation(hhT[:, c, :], px[:, c * 256:(c + 1) * 256], ACT.Identity,
                                    bias=b1[:, c:c + 1], scale=g1[:, c:c + 1])
            hhT_ready.sig(last)

        def stage_w(i, n, plane):
            w_ld.wait(act, i, n)
            s.activation(plane[:, bass.ds(i * 1024, 1024)], wraw, ACT.Copy, scale=WS).then_inc(w_hi.sem, 1)

        def stage_b(i):
            big_written.wait(act, i, 1)
            s.copy(vext[:, :, :, 0:DH], big[:, 0, 0:512].rearrange("p (c h e) -> p c h e", c=NS, h=H)).then_inc(big_act.sem, 1)
            big_written.wait(act, i, 2)
            s.copy(qk_hi, big[:, 1, :]).then_inc(big_hi.sem, 1)
            big_written.wait(act, i, 3)
            s.activation(kst[:, 0:4].rearrange("p a b -> p (a b)"), big[:, 0, :], ACT.Identity, bias=kone[:, 0:1]).then_inc(big_act.sem, 1)
            big_written.wait(act, i, 5)
            s.copy(qst[:, 0:4].rearrange("p a b -> p (a b)"), big[:, 0, :]).then_inc(big_act.sem, 1)
            negmT_psum.wait(act, i, 1)
            s.copy(negmT, acc[0:32, 0, 0:128].bitcast(F16)).then_inc(negmT_ready.sem, 1)
            big_written.wait(act, i, 15)
            s.copy(qst[:, 0:4].rearrange("p a b -> p (a b)"), big[:, 0, :]).then_inc(big_act.sem, 1)
            for u in range(8):
                big_written.wait(act, i, 17 + u)
                if u < 2:
                    pv_done.wait_before(act, i, 7 + u)
                else:
                    pv_done.wait(act, i, u - 1)
                s.activation(pt[:, u % 2].rearrange("p r c q -> p (r c q)"), big[:, u % 2, :], ACT.Exp,
                             scale=float(DH) ** -0.5).then_inc(big_act.sem, 1)

        def stage_c(i):
            py_written.wait(act, i, 2)
            s.copy(mT.rearrange("p a b -> p (a b)"), py[:]).then_inc(mT_ready.sem, 1)
            py_written.wait(act, i, 3)
            s.copy(lall[:].rearrange("p t e -> p (t e)")[:, bass.ds(i * 2 * E, 2 * E)], py[:, 0:2 * E]).then_inc(logit_read.sem, 1)

        with act.Fori(0, B) as i:
            stage_a(i)
            stage_w(i, 1, w1hi)
            stage_b(i)
            stage_w(i, 2, w2hi)
            stage_c(i)
        logit_read.wait(act, B - 1, 1)
        w_hi.wait(act, B - 1, 2)
        act.sem_inc(img_done_act, 1)
        act.wait_ge(r_dve, ROUTE_MASKS)
        s.activation(wts[:, 1, :], mx2, ACT.Exp).then_inc(r_act, 1)
        act.wait_ge(route_done, 1)
        for c in (xT_hi_ready, gelu_done):
            c.open(act)
        act.wait_ge(r_ld, 32)

        def rows_in(j):
            xT_psum.wait(act, j, 1)
            up_done.wait_before(act, j, 2)
            s.activation(xT_hi.rearrange("p a b -> p (a b)"), px[:, 0:256].bitcast(F16), ACT.Copy).then_inc(xT_hi_ready.sem, 1)

        def hidden_half(j, e, half):
            up_done.wait(act, j, half + 1)
            split_done.wait_before(act, j, half + 1)
            for k in range(FC // 2):
                f = half * (FC // 2) + k
                last = s.activation(hf[:, f, :], big[:, half, k * TT:(k + 1) * TT], ACT.Gelu_apprx_tanh,
                                    bias=b1e[:, bass.ds(e * FC + f, 1)], scale=1.0 / WS)
            gelu_done.sig(last)

        def hidden(j):
            e = expert(act, j)
            hidden_half(j, e, 0)
            hidden_half(j, e, 1)

        rows_in(0)
        hidden(0)
        rows_in(1)
        with act.Fori(0, NT - 2) as j:
            hidden(j + 1)
            rows_in(j + 2)
        hidden(NT - 1)

    @block.vector
    def _(dve):
        v = nc.vector
        for c in (dwt_chain.c, dwt_logits, part_ready, band_logit, rec_ready, var_a, t0_ready, dist_ready, aff_ready, h2_ready,
                  hn_ready, big_dve, negm_ready, ctx_ready, x4_ready, var_c, m0_ready, w_lo, dve_a.c, dve_b.c, dve_c.c):
            c.open(dve)
        steps = [0]

        def step(ins):
            steps[0] += 1
            ins.then_inc(prep_dve, 1)
            dve.wait_ge(prep_dve, steps[0])

        step(v.memset(rscale[:, 0:4], 1.0 / 64))
        step(v.memset(rscale[:, 4:7], 1.0 / 16))
        step(v.memset(rscale[:, 7:10], 1.0 / 4))
        dve.wait_ge(dwt_w_ld, 16 * (4 * G4 + 4))

        def dwt_group(g):
            ch = dwt_chain
            ch.start(dve, g)
            rec_ready.wait_before(dve, g, 1)
            dve.wait_ge(x_ld[g % 2], 16 * (g // 2 + 1))
            cur = xin[g % 2]
            n = X
            rows, cols = RROWS, D
            for lv in (1, 2, 3):
                q = n // 4
                xv = cur.rearrange("p (r two) -> p r two", two=2)
                v.tensor_tensor(col_s[:, 0:n // 2], xv[:, :, 0], xv[:, :, 1], ALU.add)
                ch.link(v.tensor_tensor(col_d[:, 0:n // 2], xv[:, :, 0], xv[:, :, 1], ALU.subtract))
                w = cols // 2
                sv = col_s[:, 0:n // 2].rearrange("p (r two c) -> p r two c", two=2, c=w)
                dv = col_d[:, 0:n // 2].rearrange("p (r two c) -> p r two c", two=2, c=w)
                o = lambda t: t.rearrange("p (r c) -> p r c", c=w)
                v.tensor_tensor(o(app[lv]), sv[:, :, 0], sv[:, :, 1], ALU.add)
                v.tensor_tensor(o(det[lv][:, 0:q]), sv[:, :, 0], sv[:, :, 1], ALU.subtract)
                v.tensor_tensor(o(det[lv][:, q:2 * q]), dv[:, :, 0], dv[:, :, 1], ALU.add)
                ch.link(v.tensor_tensor(o(det[lv][:, 2 * q:3 * q]), dv[:, :, 0], dv[:, :, 1], ALU.subtract))
                cur, n, rows, cols = app[lv], q, rows // 2, w
            ch.link(v.tensor_tensor_reduce(junk[:, 0:X // 64], app[3], wapp, 0.125, 0.0, ALU.mult, ALU.add, part[:, 0:1]))
            for k, lv in ((1, 3), (4, 2), (7, 1)):
                n = 3 * X // 4 ** lv
                for o in range(3):
                    wv_o = wdet[lv].rearrange("p (n o) -> p n o", o=3)[:, :, o]
                    ins = v.tensor_tensor_reduce(junk[:, 0:n], det[lv], wv_o, 0.5 ** lv, 0.0, ALU.mult, ALU.add,
                                                 part[:, k + o:k + o + 1])
                    if (k, o) == (7, 2):
                        part_ready.sig(ins)
                    else:
                        ch.link(ins)
            part_sum.wait(dve, g, 1)
            v.tensor_tensor(z10, px[:, 0:10], bias10, ALU.add).then_inc(dwt_logits.sem, 1)
            dwt_logits.wait(dve, g, 1)
            z3 = z10[:, 1:10].rearrange("p (l o) -> p l o", o=3)
            ch.link(v.tensor_reduce(s3, z3, AX.X, ALU.max))
            v.tensor_tensor(z3, z3, s3.unsqueeze(2).broadcast_to([P, 3, 3]), ALU.subtract).then_inc(band_logit.sem, 1)
            band_exp.wait(dve, g, 2)
            e3 = e10[:, 1:10].rearrange("p (l o) -> p l o", o=3)
            ch.link(v.tensor_reduce(s3, e3, AX.X, ALU.add))
            ch.link(v.reciprocal(r3, s3))
            ch.link(v.tensor_tensor(w10[:, 1:10].rearrange("p (l o) -> p l o", o=3), e3, r3.unsqueeze(2).broadcast_to([P, 3, 3]), ALU.mult))
            ch.link(v.tensor_scalar(e10[:, 0:1], e10[:, 0:1], 1.0, None, ALU.add))
            ch.link(v.reciprocal(w10[:, 0:1], e10[:, 0:1]))
            ch.link(v.tensor_tensor(w10, w10, rscale, ALU.mult))
            ch.link(v.tensor_scalar(nw10, w10, -1.0, None, ALU.mult))
            ch.link(v.tensor_scalar(app[3], app[3], w10[:, 0:1], None, ALU.mult))
            low = app[3]
            for k, lv in ((1, 3), (4, 2), (7, 1)):
                n = X // 4 ** lv
                w = D // 2 ** lv
                hb, vb, db = (det[lv][:, j * n:(j + 1) * n].rearrange("p (r c) -> p r c", c=w) for j in range(3))
                lowv = low.rearrange("p (r c) -> p r c", c=w)
                sv = col_s[:, 0:2 * n].rearrange("p (r two c) -> p r two c", two=2, c=w)
                dv = col_d[:, 0:2 * n].rearrange("p (r two c) -> p r two c", two=2, c=w)
                v.scalar_tensor_tensor(sv[:, :, 0], hb, w10[:, k:k + 1], lowv, ALU.mult, ALU.add)
                v.scalar_tensor_tensor(sv[:, :, 1], hb, nw10[:, k:k + 1], lowv, ALU.mult, ALU.add)
                ch.link(v.tensor_scalar(vb, vb, w10[:, k + 1:k + 2], None, ALU.mult))
                v.scalar_tensor_tensor(dv[:, :, 0], db, w10[:, k + 2:k + 3], vb, ALU.mult, ALU.add)
                ch.link(v.scalar_tensor_tensor(dv[:, :, 1], db, nw10[:, k + 2:k + 3], vb, ALU.mult, ALU.add))
                if lv == 1:
                    if g >= 2:
                        rec_stored.wait(dve, g, -1)
                    dst = rec[g % 2]
                else:
                    dst = app[lv - 1]
                ov = dst.rearrange("p (n two) -> p n two", two=2)
                v.tensor_tensor(ov[:, :, 0], col_s[:, 0:2 * n], col_d[:, 0:2 * n], ALU.add)
                ins = v.tensor_tensor(ov[:, :, 1], col_s[:, 0:2 * n], col_d[:, 0:2 * n], ALU.subtract)
                if lv == 1:
                    rec_ready.sig(ins)
                else:
                    ch.link(ins)
                low = dst
            ch.end()

        for g in range(NG):
            dwt_group(g)

        dve.wait_ge(const_pool, 9 + G4)
        step(v.tensor_copy(ident16[:], ident[:]))
        src = ident16[:].rearrange("p (s r d) -> p s r d", s=4, r=2)
        stk = lambda n: sel[:, n].rearrange("p s (r b d) -> p s r b d", r=2, b=4)
        for n, b in ((0, 0), (0, 2), (1, 1), (2, 0), (2, 1), (3, 2)):
            for sl in range(4):
                step(v.tensor_copy(stk(n)[:, sl, :, b, :], src[:, sl]))
        for part_, base in ((0, 0), (1, 16)):
            step(v.tensor_copy(selm[:, :, :, 48 + part_], ident16[0:32, base:base + 16].rearrange("p (s r) -> p s r", r=2)))
        step(v.tensor_reduce(kone[:], ident[:].rearrange("p (r c) -> p r c", r=2)[:, :, 48:50], AX.XY, ALU.add))
        dve.wait_ge(prep_act, 2)
        step(v.tensor_scalar(affT[:, 1:2], affT[:, 1:2], 0.1, 2.0, ALU.max, ALU.min))
        step(v.tensor_tensor(affT[:, 3:4], affT[:, 1:2], affT[:, 1:2], ALU.mult))
        step(v.reciprocal(affT[:, 4:5], affT[:, 3:4]))
        step(v.tensor_scalar(affT[:, 4:5], affT[:, 4:5], -0.5, None, ALU.mult))
        step(v.tensor_scalar(affT[:, 16:32], ident[0:K, 0:K], affT[:, 2:3], None, ALU.mult))
        step(v.tensor_scalar(affT[:, 32:48], ident[0:K, 0:K], affT[:, 4:5], None, ALU.mult))
        v.memset(x4[:, 0, 0:1], 0.0).then_inc(const_dve, 1)
        dve.wait_ge(prep_pe, 1)
        step(v.tensor_copy(csq_b[:].rearrange("p a b -> p (a b)"), py[:, 0:32]))
        step(v.tensor_copy(cT[:].rearrange("p a b -> p (a b)"), py[:, 32:64]))
        v.tensor_copy(t0T.rearrange("p a b -> p (a b)"), px[:]).then_inc(const_dve, 1)
        dve.wait_ge(prep_pe, 2)
        v.tensor_copy(wvo[:].rearrange("p a b -> p (a b)"), py[:]).then_inc(const_dve, 1)
        dve.wait_ge(const_dve, 3)

        def stats(ch, src, st_, mv_, var_, ready):
            for t in range(NS):
                last = v.bn_stats(st_[:, t, :], src[:, t, :])
            ch.link(last, alone=passed_dve)
            for t in range(NS):
                last = v.bn_aggr(mv_[:, t, :], st_[:, t, :])
            ch.link(last)
            v.tensor_scalar(var_, mv_[:, :, 1], EPS, None, ALU.add).then_inc(ready.sem, 1)

        def normed(dst, src, mv_, rstd_):
            for t in range(NS):
                last = v.tensor_scalar(dst[:, t, :], src[:, t, :], mv_[:, t, 0:1], rstd_[:, t:t + 1], ALU.subtract, ALU.mult)
            return last

        def x3_of(i):
            return v3(x3[:, bass.ds((i % 2) * 512, 512)], 2)

        def stage_a(i):
            ch = dve_a
            ch.start(dve, i)
            h_ld.wait(dve, i, 1, alone=passed_dve)
            stats(ch, h_t, st, mv, var, var_a)
            rstd_a.wait(dve, i, 1)
            px_written.wait_before(dve, i, 6)
            t0_ready.sig(normed(t0, h_t, mv, rstd))
            px_written.wait(dve, i, 2)
            tsq_ready.wait(dve, i, 1)
            ch.link(v.scalar_tensor_tensor(dist, px[:, 0:32].rearrange("p (a b) -> p a b", a=2), -2.0,
                                           csq_b[:, 0:1, :].broadcast_to([P, NS, K]), ALU.mult, ALU.add))
            ch.link(v.tensor_tensor(dist, dist, tsq.unsqueeze(2).broadcast_to([P, NS, K]), ALU.add))
            v.scalar_tensor_tensor(dist, dist, 0.0, csq_b[:, 1:2, :].broadcast_to([P, NS, K]), ALU.max, ALU.mult).then_inc(dist_ready.sem, 1)
            aff_exp.wait(dve, i, 1)
            ch.link(v.tensor_reduce(affsum, aff, AX.X, ALU.add))
            ch.link(v.tensor_scalar(affsum, affsum, 1e-8, None, ALU.add))
            ch.link(v.reciprocal(affrec, affsum))
            v.tensor_tensor(aff, aff, affrec.unsqueeze(2).broadcast_to([P, NS, K]), ALU.mult).then_inc(aff_ready.sem, 1)
            px_written.wait(dve, i, 5)
            h2_stored.wait_before(dve, i, 1)
            v.tensor_tensor(h2.rearrange("p a b -> p (a b)"), h_t.rearrange("p a b -> p (a b)"), px[:], ALU.add).then_inc(h2_ready.sem, 1)
            h2_ready.wait(dve, i, 1, alone=passed_dve)
            stats(ch, h2, st, mv, var, var_a)
            rstd_a.wait(dve, i, 2)
            ch.link(normed(x3_of(i), h2, mv, rstd), alone=passed_dve)
            stats(ch, x3_of(i), st, mv, var, var_a)
            rstd_a.wait(dve, i, 3)
            hn_ready.sig(normed(t0, x3_of(i), mv, rstd))
            ch.end()

        def stage_w(i, n, hi, lo):
            w_hi.wait(dve, i, n)
            v.scalar_tensor_tensor(lo[:, bass.ds(i * 1024, 1024)], wraw, WS, hi[:, bass.ds(i * 1024, 1024)],
                                   ALU.mult, ALU.subtract).then_inc(w_lo.sem, 1)

        def stage_b(i):
            ch = dve_b
            ch.start(dve, i)
            big_hi.wait(dve, i, 1)
            v.tensor_tensor(qk_lo, big[:, 1, :], qk_hi, ALU.subtract).then_inc(big_dve.sem, 1)
            big_written.wait(dve, i, 4)
            v.tensor_scalar(kst[:, 4:8].rearrange("p a b -> p (a b)"), big[:, 1, :], kone[:, 0:1], None, ALU.add).then_inc(big_dve.sem, 1)
            big_written.wait(dve, i, 6)
            v.tensor_copy(qst[:, 4:8].rearrange("p a b -> p (a b)"), big[:, 1, :]).then_inc(big_dve.sem, 1)
            for u in range(8):
                big_written.wait(dve, i, 7 + u)
                v.tensor_reduce(mx[:, :, 2 * u:2 * u + 2].rearrange("p c r -> p r c"),
                                big[:, u % 2, :].rearrange("p (r c k) -> p r c k", r=2, c=NS), AX.X, ALU.max,
                                negate=True).then_inc(big_dve.sem, 1)
            big_dve.wait(dve, i, 11)
            ch.link(v.tensor_copy(neghl[:, :, 0:H], mx))
            v.tensor_tensor(neghl[:, :, H:2 * H], mx, neghl[:, :, 0:H], ALU.subtract).then_inc(negm_ready.sem, 1)
            big_written.wait(dve, i, 16)
            v.tensor_copy(qst[:, 4:8].rearrange("p a b -> p (a b)"), big[:, 1, :]).then_inc(big_dve.sem, 1)
            pv_done.wait(dve, i, 8)
            py_written.wait_before(dve, i, 1, alone=passed_dve)
            ch.link(v.stream_shuffle(ctxn.rearrange("p a b -> p (a b)"), acc[:].rearrange("p a b -> p (a b)"),
                                     [16 + k % 16 for k in range(32)]))
            ch.link(v.reciprocal(ctxn, ctxn))
            v.tensor_tensor(ctxn, acc[:], ctxn, ALU.mult).then_inc(ctx_ready.sem, 1)
            ch.end()

        def stage_c(i):
            ch = dve_c
            ch.start(dve, i)
            py_written.wait(dve, i, 1)
            x4_stored.wait_before(dve, i, 1)
            v.tensor_tensor(x4, x3_of(i), py[:].rearrange("p (a b) -> p a b", a=2), ALU.add).then_inc(x4_ready.sem, 1)
            x4_ready.wait(dve, i, 1, alone=passed_dve)
            stats(ch, x4, stc, mvc, varc, var_c)
            rstd_c.wait(dve, i, 1)
            py_written.wait_before(dve, i, 2)
            mhl_ready.wait_before(dve, i, 1)
            m0_ready.sig(normed(m, x4, mvc, rstdc))
            ch.end()

        with dve.Fori(0, B) as i:
            stage_a(i)
            stage_w(i, 1, w1hi, w1lo)
            stage_b(i)
            stage_w(i, 2, w2hi, w2lo)
            stage_c(i)

        m0_ready.wait(dve, B - 1, 1)
        dve.wait_ge(img_done_act, 1)
        dve.wait_ge(img_done_pe, 1)
        mhl_stored.wait(dve, B - 1, 1)
        x4_stored.wait(dve, B - 1, 1)
        dve.wait_ge(r_pool, 4)
        rsteps = [0]

        def rstep(ins):
            rsteps[0] += 1
            ins.then_inc(r_dve, 1)
            dve.wait_ge(r_dve, rsteps[0])

        row = lambda t: t.unsqueeze(2).broadcast_to([P, NTL, E])
        v.tensor_copy(iota_f, iota_i)
        v.tensor_copy(iota_p, iota_pi)
        v.tensor_copy(slot_f, slot_i)
        rstep(v.tensor_copy(ident_bf[:], ident[:]))
        experts = iota_f[:, 0:E].unsqueeze(1).broadcast_to([P, NTL, E])
        v.memset(minus_p, -float(P))
        v.tensor_scalar(cols1, iota_f[:, 0:2 * NTL], 1.0, None, ALU.add)
        v.tensor_scalar(jstep, iota_f[:, 0:16], float(TT), None, ALU.mult)
        rstep(v.tensor_copy(iota_h, iota_f))

        def choose(l, mx_, mask):
            rstep(v.tensor_reduce(mx_, l, AX.X, ALU.max))
            rstep(v.tensor_tensor(te3(cand), l, row(mx_), ALU.is_lt))
            rstep(v.scalar_tensor_tensor(te3(cand), te3(cand), 16.0, experts, ALU.mult, ALU.add))
            rstep(v.tensor_reduce(pick, te3(cand), AX.X, ALU.min))
            rstep(v.tensor_tensor(te3(mask), experts, row(pick), ALU.is_equal))

        choose(lall[:], mx1, mask1)
        rstep(v.scalar_tensor_tensor(te3(lrest), te3(mask1), -1e30, lall[:], ALU.mult, ALU.add))
        choose(te3(lrest), mx2, mask2)
        rstep(v.tensor_tensor(mx2, mx2, mx1, ALU.subtract))
        rstep(v.tensor_tensor(cmask, mask1, mask2, ALU.add))
        assert rsteps[0] == ROUTE_MASKS
        dve.wait_ge(r_act, 1)
        rstep(v.tensor_scalar(mx1, wts[:, 1, :], 1.0, None, ALU.add))
        rstep(v.reciprocal(wts[:, 0, :], mx1))
        rstep(v.tensor_tensor(wts[:, 1, :], wts[:, 1, :], wts[:, 0, :], ALU.mult))
        dve.wait_ge(r_pe, 1)
        rstep(v.tensor_copy(ra, py[:, 0:NTL * E]))
        x, y = ra, rb_
        for s_ in (1, 2, 4, 8, 16):
            v.tensor_tensor(te3(y)[:, s_:], te3(x)[:, s_:], te3(x)[:, :NTL - s_], ALU.add)
            rstep(v.tensor_copy(te3(y)[:, :s_], te3(x)[:, :s_]))
            x, y = y, x
        count = te3(x)[:, NTL - 1, :]
        rstep(v.tensor_tensor(rank, x, py[:, 0:NTL * E], ALU.subtract))
        rstep(v.tensor_tensor(rank, rank, px[:, 0:NTL * E], ALU.add))
        cm3 = cmp.rearrange("p (e j) -> p e j", e=E)
        rstep(v.tensor_tensor(cm3, count.unsqueeze(2).broadcast_to([P, E, 16]), jstep.unsqueeze(1).broadcast_to([P, E, 16]), ALU.is_gt))
        rstep(v.tensor_reduce(ntile, cm3, AX.X, ALU.add))
        sq = cmp[:, 0:E * E].rearrange("p (e j) -> p e j", e=E)
        ie = iota_f[:, 0:E]
        rstep(v.tensor_tensor(sq, ie.unsqueeze(2).broadcast_to([P, E, E]), ie.unsqueeze(1).broadcast_to([P, E, E]), ALU.is_gt))
        rstep(v.tensor_tensor(sq, sq, ntile.unsqueeze(1).broadcast_to([P, E, E]), ALU.mult))
        rstep(v.tensor_reduce(tbase, sq, AX.X, ALU.add))
        rstep(v.tensor_tensor(tend, tbase, ntile, ALU.add))
        t3 = tcmp.rearrange("p (j e) -> p j e", e=E)
        rstep(v.tensor_tensor(t3, tend.unsqueeze(1).broadcast_to([P, NT, E]), iota_f[:, 0:NT].unsqueeze(2).broadcast_to([P, NT, E]), ALU.is_le))
        rstep(v.tensor_reduce(tef, t3, AX.X, ALU.add))
        rstep(v.tensor_scalar(tef, tef, float(E - 1), None, ALU.min))
        rstep(v.tensor_copy(tex[:], tef[0:1, :]))
        rstep(v.tensor_scalar(tbase, tbase, float(TT), None, ALU.mult))
        rstep(v.tensor_tensor(te3(rank), te3(rank), tbase.unsqueeze(1).broadcast_to([P, NTL, E]), ALU.add))
        for k, mask in enumerate((mask1, mask2)):
            rstep(v.tensor_tensor(mask, mask, rank, ALU.mult))
            rstep(v.tensor_reduce(pos[:, k * NTL:(k + 1) * NTL], te3(mask), AX.X, ALU.add))
        rstep(v.tensor_copy(pos_i, pos))
        v.tensor_scalar(posb_i, pos_i, P - 1, None, ALU.bitwise_and)
        rstep(v.tensor_scalar(posa_i, pos_i, 7, None, ALU.logical_shift_right))
        v.tensor_copy(posa, posa_i)
        rstep(v.tensor_copy(posb, posb_i))
        assert rsteps[0] == ROUTE_RANKS, rsteps[0]
        hot_ready.open(dve)
        with dve.Fori(0, 2 * NTL // 8) as r:
            for half in range(2):
                hot_used.wait_before(dve, r, half + 1)
                for k in range(4):
                    n = 4 * half + k
                    col = r * 8 + n
                    v.tensor_scalar(hotb[:, n, :], iota_h, posb[:, bass.ds(col, 1)], None, ALU.is_equal)
                    v.tensor_scalar(hota[:, n, 0, :], iota_h[:, 0:NCOL], posa[:, bass.ds(col, 1)], iota_p, ALU.is_equal, ALU.mult)
                    last = v.tensor_scalar(hota[:, n, 1, :], iota_h[:, 0:NCOL], posa[:, bass.ds(col, 1)], cols1[:, bass.ds(col, 1)], ALU.is_equal, ALU.mult)
                hot_ready.sig(last)
        dve.wait_ge(r_pe, 2)
        rstep(v.scalar_tensor_tensor(tok, px[:, NCOL:2 * NCOL], float(P), minus_p, ALU.mult, ALU.add))
        rstep(v.tensor_tensor(tok, tok, px[:, 0:NCOL], ALU.add))
        rstep(v.tensor_scalar(emp, tok, -0.5, None, ALU.is_lt))
        rstep(v.tensor_tensor(emp, emp, slot_f, ALU.mult))
        rstep(v.tensor_tensor(dest, tok, emp, ALU.add))
        rstep(v.tensor_copy(dst_idx[:], dest))
        rstep(v.tensor_scalar(emp, tok, float(T), -float(T), ALU.is_ge, ALU.mult))
        rstep(v.tensor_tensor(tok, tok, emp, ALU.add))
        rstep(v.tensor_scalar(tok, tok, 0.0, None, ALU.max))
        v.tensor_copy(src_idx[:], tok).then_inc(route_done, 1)
        dve.wait_ge(route_done, 1)

        for c in (xT_lo_ready, split_done, y_ready, hi_chain):
            c.open(dve)
        dve.wait_ge(r_ld, 32)

        def split(j, half):
            sl = slice(half * (FC // 2), (half + 1) * (FC // 2))
            gelu_done.wait(dve, j, half + 1)
            down_done.wait_before(dve, j, 1)
            v.tensor_copy(h_hi[:, sl], hf[:, sl]).then_inc(hi_chain.sem, 1)
            hi_chain.wait(dve, j, half + 1)
            v.tensor_tensor(h_lo[:, sl], hf[:, sl], h_hi[:, sl], ALU.subtract).then_inc(split_done.sem, 1)

        def rows_in(j):
            xT_psum.wait(dve, j, 1)
            up_done.wait_before(dve, j, 2)
            v.tensor_copy(xT_lo.rearrange("p a b -> p (a b)"), py[:, 0:256].bitcast(BF16)).then_inc(xT_lo_ready.sem, 1)

        def rows_out(j, e):
            down_done.wait(dve, j, 1)
            y_free.wait_before(dve, j, 1)
            for t in range(2):
                last = v.scalar_tensor_tensor(ys[:, t, :], acc[:, 2 * t, :], 1.0 / WS, b2e[:, bass.ds(e * D, D)], ALU.mult, ALU.add)
            y_ready.sig(last)

        rows_in(0)
        rows_in(1)
        with dve.Fori(0, NT - 2) as j:
            split(j, 0)
            split(j, 1)
            rows_in(j + 2)
            rows_out(j, expert(dve, j))
        for j in (NT - 2, NT - 1):
            split(j, 0)
            split(j, 1)
            rows_out(j, expert(dve, j))

        c_done.open(dve)
        c_mid.open(dve)
        with dve.Fori(0, B // 2) as r:
            for k in range(2):
                c_first.wait(dve, r, k + 1)
                for n in range(2):
                    for t in range(NS):
                        o = comb[k][4][:, t, :]
                        last = v.scalar_tensor_tensor(o, comb[k][2 + n][:, t, :], wts[:, n, :][:, bass.ds(r * 4 + 2 * k + t, 1)], o, ALU.mult, ALU.add)
                    if n == 0:
                        c_mid.sig(last)
                        c_mid.wait(dve, r, k + 1)
                c_done.sig(last)

    @block.tensor
    def _(pe):
        t_ = nc.tensor
        for c in (part_sum, px_written, big_written, negmT_psum, pv_done, py_written):
            c.open(pe)
        pe.wait_ge(const_pool, 9 + G4)
        for g in range(NG):
            part_ready.wait(pe, g, 1)
            t_.matmul(px[:, 0:10], blk[:], part, start=True, stop=True).then_inc(part_sum.sem, 1)
        pe.wait_ge(const_dve, 1)
        dwt_logits.wait(pe, NG - 1, 1)
        t_.matmul(py[:, 0:32], ones[0:K, :], affT[:, 16:48], start=True, stop=True)
        for c in range(NC):
            t_.transpose(py[:, 32 + 16 * c:48 + 16 * c], zs[:, c * P:(c + 1) * P], ident[0:K, 0:K])
        for c in range(NC):
            for k in range(NC):
                last = t_.transpose(px[:, k * 256 + c * P:k * 256 + (c + 1) * P], h_t[:, c, k * P:(k + 1) * P], ident[:])
        last.then_inc(prep_pe, 1)
        pe.wait_ge(const_dve, 2)
        for c in range(NC):
            for k in range(NC):
                last = t_.matmul(py[:, c * 256:(c + 1) * 256], t0T[:, k, c * P:(c + 1) * P], t0[:, k, :], start=(k == 0), stop=(k == NC - 1))
        last.then_inc(prep_pe, 1)
        pe.wait_ge(const_dve, 3)

        def turned(dst, src):
            for c in range(NC):
                for t in range(NS):
                    last = t_.transpose(dst[:, c * 256 + t * P:c * 256 + (t + 1) * P], src[:, t, c * P:(c + 1) * P], ident[:])
            return last

        def stage_a(i):
            t0_ready.wait(pe, i, 1)
            hhT_ready.wait_before(pe, i, 1)
            px_written.sig(turned(px, t0))
            t0T_ready.wait(pe, i, 1)
            for t in range(NS):
                for c in range(NC):
                    last = t_.matmul(px[:, t * K:(t + 1) * K], t0T[:, c, t * P:(t + 1) * P], cT[:, c, :], start=(c == 0), stop=(c == NC - 1))
            px_written.sig(last)
            aff_ready.wait(pe, i, 1)
            for c in range(NC):
                for t in range(NS):
                    t_.matmul(px[:, c * K:(c + 1) * K], t0[:, t, c * P:(c + 1) * P], aff[:, t, :], start=(t == 0), stop=(t == NS - 1))
            for t in range(NS):
                last = t_.transpose(px[0:K, 256 + t * P:256 + (t + 1) * P], aff[:, t, :], ident[:])
            px_written.sig(last)
            ut_ready.wait(pe, i, 1)
            for c in range(NC):
                last = t_.matmul(px[0:K, 0:256], ut[:, c, :], wvo[:, c, :], start=(c == 0), stop=(c == NC - 1))
            px_written.sig(last)
            z_ready.wait(pe, i, 1)
            for t in range(NS):
                last = t_.matmul(px[:, t * 256:(t + 1) * 256], affT[:, t * P:(t + 1) * P], zs, start=True, stop=True)
            px_written.sig(last)
            hn_ready.wait(pe, i, 1)
            px_written.sig(turned(px, t0))

        def stack_half(i, u, q, parts, with_max=False):
            slot_free(i, u)
            hi, lo = parts
            for k in range(4):
                s = 4 * (u % 2) + k
                src = (q * 2 + s // 4) * 256
                dst = big[:, u % 2, k * 256:(k + 1) * 256]
                t_.matmul(dst, sel[:, hi, s % 4, :], qk_hi[:, src:src + 256], start=True, stop=False)
                last = t_.matmul(dst, sel[:, lo, s % 4, :], qk_lo[:, src:src + 256], start=False, stop=not with_max)
                if with_max:
                    last = t_.matmul(dst, selm[:, s, :, :].rearrange("p r c -> p (r c)"), negmT, start=False, stop=True)
            big_written.sig(last)

        def scores(i, u, s, turned_):
            slot_free(i, u)
            for c in range(NS):
                for r in range(2):
                    rows = slice(64 * r, 64 * r + 64)
                    x, y = (kst, qst) if turned_ else (qst, kst)
                    dst = big[:, u % 2, r * 512 + c * 256:r * 512 + (c + 1) * 256]
                    last = t_.matmul(dst, x[rows, s, c * P:(c + 1) * P], y[rows, s, :], start=True, stop=True)
            big_written.sig(last)

        def context(i, s):
            big_act.wait(pe, i, 5 + s)
            for c in range(NS):
                for r in range(2):
                    h = 2 * s + r
                    j = h % 4
                    last = t_.matmul(acc[32 * j:32 * j + 32, h // 4, :], vext[:, c, h, :], pt[:, s % 2, r, c, :],
                                     start=(c == 0), stop=(c == NS - 1), tile_position=(0, 32 * j))
            pv_done.sig(last)

        def stage_b(i):
            hhT_ready.wait(pe, i, 1)
            slot_free(i, 0)
            for t in range(NS):
                for c in range(NC):
                    last = t_.matmul(big[:, 0, t * 256:(t + 1) * 256], hhT[:, c, t * P:(t + 1) * P], wv[:, c, :], start=(c == 0), stop=(c == NC - 1))
            big_written.sig(last)
            slot_free(i, 1)
            for q, w in enumerate((wq, wk_)):
                for o in range(NC):
                    for c in range(NC):
                        last = t_.matmul(big[:, 1, q * 512 + o * 256:q * 512 + (o + 1) * 256], w[:, c, o * P:(o + 1) * P], hhT[:, c, :],
                                         start=(c == 0), stop=(c == NC - 1))
            big_written.sig(last)
            big_dve.wait(pe, i, 1)
            stack_half(i, 2, 1, (0, 1))
            stack_half(i, 3, 1, (0, 1))
            stack_half(i, 4, 0, (2, 3))
            stack_half(i, 5, 0, (2, 3))
            big_act.wait(pe, i, 3)
            big_dve.wait(pe, i, 3)
            for s in range(8):
                scores(i, 6 + s, s, False)
            negm_ready.wait(pe, i, 1)
            ctx_ready.wait_before(pe, i, 1)
            for c in range(NS):
                last = t_.transpose(acc[0:32, 0, c * 64:(c + 1) * 64].bitcast(F16), neghl[:, c, :], ident16[:])
            negmT_psum.sig(last)
            negmT_ready.wait(pe, i, 1)
            stack_half(i, 14, 0, (2, 3), True)
            stack_half(i, 15, 0, (2, 3), True)
            big_act.wait(pe, i, 4)
            big_dve.wait(pe, i, 12)
            for s in range(8):
                scores(i, 16 + s, s, True)
                if s >= 1:
                    context(i, s - 1)
            context(i, 7)

        def stage_c(i):
            ctx_ready.wait(pe, i, 1)
            logit_read.wait_before(pe, i, 1)
            for t in range(NS):
                for k in range(4):
                    last = t_.matmul(py[:, t * 256:(t + 1) * 256], ctxn[:, k, t * P:(t + 1) * P], wop[:, k, :], start=(k == 0), stop=(k == 3))
            py_written.sig(last)
            m_ready.wait(pe, i, 1)
            py_written.sig(turned(py, m))
            mT_ready.wait(pe, i, 1)
            for t in range(NS):
                for c in range(NC):
                    last = t_.matmul(py[:, t * E:(t + 1) * E], mT[:, c, t * P:(t + 1) * P], wg[:, c, :], start=(c == 0), stop=(c == NC - 1))
            py_written.sig(last)

        with pe.Fori(0, B) as i:
            stage_a(i)
            stage_b(i)
            stage_c(i)
        py_written.wait(pe, B - 1, 3)
        pe.sem_inc(img_done_pe, 1)
        for c in (hot_used, xT_psum, up_done, down_done):
            c.open(pe)
        pe.wait_ge(tri_ready, 1)
        pe.wait_ge(r_dve, ROUTE_MASKS)
        t_.matmul(px[:, 0:NTL * E], tri[:], cmask, start=True, stop=True)
        t_.matmul(py[:, 0:NTL * E], ones[:], cmask, start=True, stop=True).then_inc(r_pe, 1)
        pe.wait_ge(r_dve, ROUTE_RANKS)
        t_.matmul(px[:, 0:2 * NCOL], zero16[:, 0:P], zero16[:, 0:2 * NCOL], start=True, stop=False)
        with pe.Fori(0, 2 * NTL // 8) as r:
            for half in range(2):
                hot_ready.wait(pe, r, half + 1)
                for n in range(4 * half, 4 * half + 4):
                    last = t_.matmul(px[:, 0:2 * NCOL], hotb[:, n, :], hota[:, n].rearrange("p v a -> p (v a)"), start=False, stop=False)
                hot_used.sig(last)
        t_.matmul(px[:, 0:2 * NCOL], zero16[:, 0:P], zero16[:, 0:2 * NCOL], start=False, stop=True).then_inc(r_pe, 1)

        pe.wait_ge(route_done, 1)

        def turn(j):
            x_in.wait(pe, j, 2)
            for c in range(NC):
                for t in range(2):
                    o = slice(c * 128 + t * 64, c * 128 + (t + 1) * 64)
                    t_.transpose(px[:, o].bitcast(F16), xg[:, t, c * P:(c + 1) * P], ident16[:])
                    last = t_.transpose(py[:, o].bitcast(BF16), xg[:, t, D + c * P:D + (c + 1) * P].bitcast(BF16), ident_bf[:])
            xT_psum.sig(last)

        def up(j, e):
            xT_hi_ready.wait(pe, j, 1)
            xT_lo_ready.wait(pe, j, 1)
            for half in range(2):
                gelu_done.wait_before(pe, j, half + 1)
                for k in range(FC // 2):
                    f = half * (FC // 2) + k
                    dst = big[:, half, k * TT:(k + 1) * TT]
                    for n, (w, x) in enumerate(((w1hi, xT_hi), (w1hi, xT_lo), (w1lo, xT_hi))):
                        for c in range(NC):
                            last = t_.matmul(dst, w[:, bass.ds(e * (NC * F) + (c * F + f * P), P)], x[:, c, :],
                                             start=(n == 0 and c == 0), stop=(n == 2 and c == NC - 1))
                up_done.sig(last)

        def down(j, e):
            y_ready.wait_before(pe, j, 1)
            split_done.wait(pe, j, 2)
            for t in range(2):
                for f in range(FC):
                    for n, (x, w) in enumerate(((h_hi, w2hi), (h_hi, w2lo), (h_lo, w2hi))):
                        last = t_.matmul(acc[:, 2 * t, :], x[:, f, t * P:(t + 1) * P], w[:, bass.ds(e * (FC * D) + f * D, D)],
                                         start=(f == 0 and n == 0), stop=(f == FC - 1 and n == 2))
            down_done.sig(last)

        turn(0)
        up(0, expert(pe, 0))
        turn(1)
        with pe.Fori(0, NT - 2) as j:
            up(j + 1, expert(pe, j + 1))
            turn(j + 2)
            down(j, expert(pe, j))
        up(NT - 1, expert(pe, NT - 1))
        down(NT - 2, expert(pe, NT - 2))
        down(NT - 1, expert(pe, NT - 1))


def kernel(**inputs):
    import numpy as np
    import concourse.bacc as bacc
    from concourse.bass_utils import run_bass_kernel_spmd

    nc = bacc.Bacc("TRN2", target_bir_lowering=False, num_devices=1)
    arrays, aps = {}, {}
    for name, value in inputs.items():
        arr = np.ascontiguousarray(value)
        arrays[f"in_{name}"] = arr
        aps[name] = nc.dram_tensor(f"in_{name}", arr.shape, mybir.dt.from_np(arr.dtype), kind="ExternalInput").ap()
    out = nc.dram_tensor("out_0", (B, S, D), F32, kind="ExternalOutput").ap()
    tower(nc, aps, out)
    r = run_bass_kernel_spmd(nc, [arrays], core_ids=[0])
    return r.results[0]["out_0"]
```

```python
from contextlib import ExitStack

import concourse.bass as bass
from concourse import mybir

ALU = mybir.AluOpType
ACT = mybir.ActivationFunctionType
F32 = mybir.dt.float32
F16 = mybir.dt.float16
BF16 = mybir.dt.bfloat16
I32 = mybir.dt.int32
U32 = mybir.dt.uint32
AX = mybir.AxisListType

P = 128
B = 16
S = 256
D = 256
T = B * S
H, DH = 16, 16
K = 16
E, F = 8, 1024
NC = D // P
NS = S // P
FC = F // P
TT = 256
NT = 2 * T // TT + E - 1
NSLOT = NT * TT
NCOL = NSLOT // P
EPS = 1e-5
WS = 64.0

G4 = 4
NG = B // G4
RB = P // G4
RROWS = S // RB


class Count:

    def __init__(self, sem, per, unit=1, opened=True):
        self.sem, self.per, self.unit, self.opened = sem, per, unit, opened

    def open(self, eng):
        eng.sem_inc(self.sem, self.per * self.unit)

    def sig(self, ins):
        ins.then_inc(self.sem, self.unit)

    def wait(self, eng, i, n, alone=None):
        self.await_(eng, (i + self.opened) * (self.per * self.unit) + n * self.unit, alone)

    def wait_before(self, eng, i, n, alone=None):
        self.await_(eng, i * (self.per * self.unit) + n * self.unit, alone)

    def await_(self, eng, value, alone):
        eng.wait_ge(self.sem, value)
        if alone:
            eng.sem_inc(alone, 1)


class Chain:

    def __init__(self, sem, per):
        self.c, self.n = Count(sem, per), 0

    def start(self, eng, i):
        self.eng, self.i, self.n = eng, i, 0

    def link(self, ins, alone=None):
        self.n += 1
        self.c.sig(ins)
        self.c.wait(self.eng, self.i, self.n, alone)

    def end(self):
        assert self.n == self.c.per, (self.n, self.c.per)


def tower(nc, a, out, dbg=None, upto=9):
    with ExitStack() as ctx:
        build(nc, ctx, a, out, dbg, upto)


def build(nc, ctx, a, out, dbg, upto):
    def sb(name, shape, dt=F32):
        return ctx.enter_context(nc.sbuf_tensor(name, shape, dt))

    def sem(name):
        return ctx.enter_context(nc.semaphore(name))

    def dram(name, shape, dt):
        return nc.dram_tensor(name, shape, dt).ap()

    rec_dram = dram("rec_rows", [T, D], F32)
    h2_dram = dram("h2_rows", [T, D], F32)
    x4_dram = dram("x4_rows", [T, D], F32)
    m_dram = dram("m_rows", [T, 2 * D], F16)
    y_dram = dram("y_rows", [2 * T + NSLOT, D], F32)

    big = ctx.enter_context(nc.psum_tensor("big", [P, 2, 1024], F32))
    acc = ctx.enter_context(nc.psum_tensor("acc", [P, 4, 256], F32))
    px = ctx.enter_context(nc.psum_tensor("px", [P, 512], F32))
    py = ctx.enter_context(nc.psum_tensor("py", [P, 512], F32))

    expert_w = sb("expert_w", [P, 4, E * NC * F], F16)
    w1hi = expert_w[:, 0, :]
    w1lo = expert_w[:, 1, :].bitcast(BF16)
    w2hi = expert_w[:, 2, :]
    w2lo = expert_w[:, 3, :].bitcast(BF16)
    arena1 = expert_w[:, :, :].rearrange("p a b -> p (a b)").bitcast(F32)
    used = [0]

    def a1(n):
        used[0] += n
        assert used[0] <= 2 * E * NC * F
        return arena1[:, used[0] - n:used[0]]

    X = RROWS * D
    xin = [a1(X), a1(X)]
    rec = [a1(X), a1(X)]
    col_s, col_d = a1(X // 2), a1(X // 2)
    det = {1: a1(3 * X // 4), 2: a1(3 * X // 16), 3: a1(3 * X // 64)}
    app = {1: a1(X // 4), 2: a1(X // 16), 3: a1(X // 64)}
    wdet = {1: a1(9 * X // 4), 2: a1(9 * X // 16), 3: a1(9 * X // 64)}
    wapp = a1(X // 64)
    junk = a1(3 * X // 4)
    part = a1(10)
    bias10, rscale = a1(10), a1(10)
    z10, e10, w10, nw10 = a1(10), a1(10), a1(10), a1(10)
    s3, r3 = a1(3), a1(3)

    NWORK = 13936
    work = sb("work", [P, NWORK])
    at = [0]

    def wk(n):
        at[0] += n
        assert at[0] <= NWORK, at[0]
        return work[:, at[0] - n:at[0]]

    v3 = lambda t, n: t.rearrange("p (a b) -> p a b", a=n)
    h_t = v3(wk(512), 2)
    t0 = v3(wk(512), 2)
    t0T = v3(wk(512), 2)
    h2 = v3(wk(512), 2)
    x3 = wk(1024)
    hhT = v3(wk(512), 2)
    qst = v3(wk(1024).bitcast(F16), 8)
    kst = v3(wk(1024).bitcast(F16), 8)
    vext = wk(1024).rearrange("p (c h e) -> p c h e", c=NS, h=H)
    pt = wk(2048).rearrange("p (b r c q) -> p b r c q", b=2, r=2, c=NS)
    qk_hi = pt[:, 0].rearrange("p r c q -> p (r c q)")[:, 0:512].bitcast(F16)
    qk_lo = pt[:, 0].rearrange("p r c q -> p (r c q)")[:, 512:1024].bitcast(F16)
    ctxn_w = wk(1024)
    ctxn = v3(ctxn_w, 4)
    probs = [pt[:, 0], pt[:, 1], ctxn_w.rearrange("p (r c q) -> p r c q", r=2, c=NS)]
    x4 = v3(wk(512), 2)
    m = v3(wk(512), 2)
    mhl = v3(wk(512).bitcast(F16), 2)
    mT = v3(wk(512), 2)
    cturn = pt[:, 1].rearrange("p r c q -> p (r c q)")
    ct3 = cturn.rearrange("p (n d) -> p n d", d=32)
    crec = ctxn[:, 0, 0:32]
    wraw = wk(1024)
    mid = at[0]
    st = wk(12).rearrange("p (t n) -> p t n", t=NS)
    mv = wk(4).rearrange("p (t n) -> p t n", t=NS)
    var, rstd = wk(2), wk(2)
    stc = wk(12).rearrange("p (t n) -> p t n", t=NS)
    mvc = wk(4).rearrange("p (t n) -> p t n", t=NS)
    varc, rstdc = wk(2), wk(2)
    tsq, affsum, affrec = wk(2), wk(2), wk(2)
    dist = v3(wk(32), 2)
    aff = v3(wk(32), 2)
    ut = v3(wk(32), 2)
    affT = wk(256)[0:K, :]
    zs = wk(256)[0:K, :]
    sqj = v3(wk(256).bitcast(BF16), 2)
    mx = v3(wk(32), 2)
    neghl = v3(wk(32).bitcast(F16), 2)
    negmT = wk(128).bitcast(F16)[0:32, :]

    ident = sb("ident", [P, P])
    ident16 = sb("ident16", [P, P], F16)
    blk = sb("blk", [P, P])
    ones = sb("ones", [P, P])
    tri = sb("tri", [P, P])
    halfneg = sb("halfneg", [P, 2])
    kone = sb("kone", [P, 1])
    wscale = sb("wscale", [P, 1])
    sel = sb("sel", [P, 4, 4, 128], F16)
    selm = sb("selm", [32, 8, 2, 64], F16)
    csq_b = sb("csq_b", [P, 2, K])
    wq, wk_, wv = (sb(n, [P, NC, D]) for n in ("wq", "wk", "wv"))
    wop = sb("wop", [P, 4, D])
    wvo = sb("wvo", [P, NC, D])
    g1, b1 = sb("g1", [P, NC]), sb("b1ln", [P, NC])
    g2b, b2b = sb("g2b", [P, D]), sb("b2b", [P, D])
    wg = sb("wg", [P, NC, E])
    cT = sb("cT", [P, NC, K])
    lall = sb("lall", [P, 2 * B, E])

    at[0] = 0
    rt = lambda n: wk(n)
    NTL = 2 * B
    te3 = lambda t: t.rearrange("p (t e) -> p t e", e=E)
    mask1, mask2, cmask, cand, lrest, ra, rb_, rank = (rt(NTL * E) for _ in range(8))
    mx1, mx2, pick = rt(NTL), rt(NTL), rt(NTL)
    wts = sb("wts", [P, 2, NTL])
    pos = rt(2 * NTL)
    pos_i, posa_i, posb_i = (rt(2 * NTL).bitcast(I32) for _ in range(3))
    posa, posb = rt(2 * NTL), rt(2 * NTL)
    ntile, tbase, tend = rt(E), rt(E), rt(E)
    cmp = rt(E * 16)
    tcmp = rt(NT * E)
    tef = rt(NT)
    iota_i = rt(P).bitcast(I32)
    iota_f = rt(P)
    iota_h = rt(P // 2).bitcast(F16)
    iota_p = rt(1)
    iota_pi = rt(1).bitcast(I32)
    jstep = rt(16)
    slot_i = rt(NCOL).bitcast(I32)
    slot_f = rt(NCOL)
    hotb = rt(8 * P // 2).bitcast(F16).rearrange("p (n b) -> p n b", n=8)
    hota = rt(8 * NCOL).bitcast(F16).rearrange("p (n v a) -> p n v a", n=8, v=2)
    zero16 = rt(P).bitcast(F16)
    cols1 = rt(2 * NTL)
    minus_p = rt(NCOL)
    tok, emp, dest = rt(NCOL), rt(NCOL), rt(NCOL)
    tex = sb("tex", [1, NT], I32)
    src_idx, dst_idx = sb("src_idx", [P, NCOL], U32), sb("dst_idx", [P, NCOL], U32)
    gidx, sidx = sb("gidx", [P, 2], U32), sb("sidx", [P, 2], U32)
    at[0] = 0
    b2e = wk(E * D)
    b1e = wk(E * FC)
    xg = v3(wk(512).bitcast(F16), 2)
    xT_hi = v3(wk(256).bitcast(F16), 2)
    xT_lo = v3(wk(256).bitcast(BF16), 2)
    hf = v3(wk(2048), FC)
    h_hi = v3(wk(1024).bitcast(F16), FC)
    h_lo = v3(wk(1024).bitcast(BF16), FC)
    ys = v3(wk(512), 2)
    at[0] = 0
    comb = [[v3(wk(512), 2) for _ in range(5)] for _ in range(2)]
    ident_bf = sb("ident_bf", [P, P], BF16)

    img = lambda d: d.rearrange("(i t p) d -> i p t d", t=NS, p=P)

    passed_dve, passed_pool, passed_sp = sem("passed_dve"), sem("passed_pool"), sem("passed_sp")

    const_ld, const_pool, const_dve = sem("const_ld"), sem("const_pool"), sem("const_dve")
    prep_pe, prep_dve, prep_act = sem("prep_pe"), sem("prep_dve"), sem("prep_act")
    dwt_w_ld = sem("dwt_w_ld")

    x_ld = [sem("x_ld0"), sem("x_ld1")]
    dwt_chain = Chain(sem("dwt_chain"), 32)
    part_ready = Count(sem("part_ready"), 1)
    part_sum = Count(sem("part_sum"), 1)
    dwt_logits = Count(sem("dwt_logits"), 1)
    band_logit = Count(sem("band_logit"), 1)
    band_exp = Count(sem("band_exp"), 2)
    rec_ready = Count(sem("rec_ready"), 1)
    rec_stored = Count(sem("rec_stored"), 1, 16)

    C = {}

    def cnt(name, per=1, unit=1):
        C[name] = Count(sem(name), per, unit)
        return C[name]

    h_ld = cnt("h_ld", 1, 16)
    var_a, rstd_a = cnt("var_a", 3), cnt("rstd_a", 3)
    t0_ready, tsq_ready = cnt("t0_ready"), cnt("tsq_ready")
    px_written = cnt("px_written", 6)
    t0T_ready, dist_ready, aff_exp = cnt("t0T_ready"), cnt("dist_ready"), cnt("aff_exp")
    aff_ready, ut_ready, z_ready = cnt("aff_ready"), cnt("ut_ready"), cnt("z_ready")
    h2_ready, h2_stored = cnt("h2_ready"), cnt("h2_stored", 1, 16)
    hn_ready, hhT_ready = cnt("hn_ready"), cnt("hhT_ready")
    big_written = cnt("big_written", 24)
    big_hi = cnt("big_hi", 1)
    big_act = cnt("big_act", 12)
    big_dve = cnt("big_dve", 12)
    negm_ready, negmT_psum, negmT_ready = cnt("negm_ready"), cnt("negmT_psum"), cnt("negmT_ready")
    pv_done, ctx_ready = cnt("pv_done", 8), cnt("ctx_ready")
    py_written = cnt("py_written", 3)
    x4_ready, x4_stored = cnt("x4_ready"), cnt("x4_stored", 1, 16)
    var_c, rstd_c, m0_ready, m_ready = cnt("var_c"), cnt("rstd_c"), cnt("m0_ready"), cnt("m_ready")
    mhl_ready, mhl_stored = cnt("mhl_ready"), cnt("mhl_stored", 1, 16)
    mT_ready, logit_read = cnt("mT_ready"), cnt("logit_read")
    w_ld, w_hi, w_lo = cnt("w_ld", 2, 16), cnt("w_hi", 4), cnt("w_lo", 2)
    dve_a, dve_b, dve_c = Chain(sem("dve_a"), 12), Chain(sem("dve_b"), 1), Chain(sem("dve_c"), 2)
    dve_ctx = Chain(sem("dve_ctx"), 3)
    pool_c = Chain(sem("pool_c"), 2)

    READER = ["D", "A", "D", "A", "D"] + ["D"] * 8 + ["A", "A", "D"] + ["A"] * 8
    assert len(READER) == 24
    order = [READER[:u].count(READER[u]) + 1 for u in range(24)]
    N_A, N_D = READER.count("A"), READER.count("D")
    assert (N_A, N_D) == (12, 12)

    def slot_free(i, u):
        before = C["big_act"] if READER[u - 2] == "A" else C["big_dve"]
        (before.wait if u >= 2 else before.wait_before)(nc.tensor, i, order[u - 2])

    tri_ready = sem("tri_ready")
    ROUTE_RANKS = 45
    img_done_act, img_done_pe = sem("img_done_act"), sem("img_done_pe")
    r_dve, r_pool, r_act, r_pe, r_ld = sem("r_dve"), sem("r_pool"), sem("r_act"), sem("r_pe"), sem("r_ld")
    hot_ready, hot_used = Count(sem("hot_ready"), 2), Count(sem("hot_used"), 2)
    route_done = sem("route_done")
    x_in = Count(sem("x_in"), 2, 16, opened=False)
    xT_psum, xT_hi_ready, xT_lo_ready = Count(sem("xT_psum"), 1), Count(sem("xT_hi_ready"), 1), Count(sem("xT_lo_ready"), 1)
    up_done, gelu_done, split_done = Count(sem("up_done"), 2), Count(sem("gelu_done"), 2), Count(sem("split_done"), 2)
    hi_chain = Count(sem("hi_chain"), 2)
    down_done, y_ready = Count(sem("down_done"), 1), Count(sem("y_ready"), 1)
    y_out = Count(sem("y_out"), 2, 16, opened=False)
    y_free = Count(sem("y_free"), 1)
    src_ready, dst_ready = Count(sem("src_ready"), 1), Count(sem("dst_ready"), 1)
    c_in = [Count(sem(f"c_in{k}"), 4, 16) for k in range(2)]
    c_sum, c_out, c_first = Count(sem("c_sum"), 2), [Count(sem(f"c_out{k}"), 1, 16) for k in range(2)], Count(sem("c_first"), 2)
    c_done, c_mid = Count(sem("c_done"), 2), Count(sem("c_mid"), 2)
    FILL = (2, 2, 2, 2, 2)
    ROUTE_MASKS = 15

    def expert(eng, j):
        return eng.value_load(tex[0:1, bass.ds(j, 1)], min_val=0, max_val=E - 1)

    def run_images(eng, image_round):
        image_round(0, c_=False)
        with eng.Fori(1, B - 1) as i:
            image_round(i)
        image_round(B - 1, a_=False)
        image_round(B, a_=False, b_=False)

    block = ctx.enter_context(nc.Block())

    @block.sync
    def _(sp):
        for c in (rec_stored, h_ld, h2_stored, x4_stored, mhl_stored, w_ld):
            c.open(sp)
        for lv, name, n in ((1, "L0_tok_Wd3", X // 4), (2, "L0_tok_Wd2", X // 16), (3, "L0_tok_Wd1", X // 64)):
            src = a[name].rearrange("(b r n) o -> r b (n o)", b=3, r=RB)
            dst = wdet[lv].rearrange("p (b n) -> p b n", b=3)
            for q in range(G4):
                sp.dma_start(dst[RB * q:RB * (q + 1)], src).then_inc(dwt_w_ld, 16)
        for q in range(G4):
            sp.dma_start(wapp[RB * q:RB * (q + 1)], a["L0_tok_Wa"].rearrange("(r n) o -> r (n o)", r=RB)).then_inc(dwt_w_ld, 16)
        for k, name in enumerate(("L0_tok_ba", "L0_tok_bd1", "L0_tok_bd2", "L0_tok_bd3")):
            dst = bias10[:, 0:1] if k == 0 else bias10[:, 3 * k - 2:3 * k + 1]
            sp.dma_start(dst, a[name].partition_broadcast(P)).then_inc(dwt_w_ld, 16)
        xg = a["x"].rearrange("(g b) (r h) w o -> g (b r) (h w o)", b=G4, r=RB)
        rg = rec_dram.rearrange("(g p h) d -> g p (h d)", g=NG, h=RROWS)

        def store_rec(g):
            rec_ready.wait(sp, g, 1)
            sp.dma_start(rg[g], rec[g % 2]).then_inc(rec_stored.sem, 16)

        for g in range(NG):
            if g >= 2:
                rec_ready.wait(sp, g, -1)
            sp.dma_start(xin[g % 2], xg[g]).then_inc(x_ld[g % 2], 16)
            if g >= 1:
                store_rec(g - 1)
        store_rec(NG - 1)

        rec_stored.wait(sp, NG - 1, 1)
        sp.wait_ge(prep_pe, 1)
        w1v = a["L0_ffn_W1"].rearrange("e (c p) f -> (e c) p f", p=P)
        w2v = a["L0_ffn_W2"].rearrange("e (n q p) d -> (e n) p q d", n=2, p=P)
        def store_h2(i):
            h2_ready.wait(sp, i, 1, alone=passed_sp)
            sp.dma_start(img(h2_dram)[i], h2).then_inc(h2_stored.sem, 16)

        def store_mhl(i):
            mhl_ready.wait(sp, i, 1, alone=passed_sp)
            sp.dma_start(img(m_dram)[i], mhl).then_inc(mhl_stored.sem, 16)

        def image_round(i, a_=True, b_=True, c_=True, m_=True):
            if a_:
                h2_ready.wait(sp, i, 1, alone=passed_sp)
                sp.dma_start(h_t, img(rec_dram)[i + 1]).then_inc(h_ld.sem, 16)
            if b_:
                w_lo.wait_before(sp, i, 2, alone=passed_sp)
                sp.dma_start(wraw, w1v[i]).then_inc(w_ld.sem, 16)
            if m_:
                store_mhl(i - 2)
            if b_:
                w_lo.wait(sp, i, 1, alone=passed_sp)
                sp.dma_start(wraw.rearrange("p (q d) -> p q d", q=4), w2v[i]).then_inc(w_ld.sem, 16)
            if c_:
                x4_ready.wait(sp, i - 1, 1, alone=passed_sp)
                sp.dma_start(img(x4_dram)[i - 1], x4).then_inc(x4_stored.sem, 16)
            if a_:
                store_h2(i + 1)

        sp.dma_start(h_t, img(rec_dram)[0]).then_inc(h_ld.sem, 16)
        store_h2(0)
        image_round(0, c_=False, m_=False)
        image_round(1, m_=False)
        with sp.Fori(2, B - 1) as i:
            image_round(i)
        image_round(B - 1, a_=False)
        image_round(B, a_=False, b_=False)
        store_mhl(B - 1)
        for c in (h2_stored, x4_stored, mhl_stored):
            c.wait(sp, B - 1, 1)
        sp.wait_ge(route_done, 1)
        for c in (*c_in, *c_out, y_free):
            c.open(sp)
        sp.dma_start(b2e, a["L0_ffn_b2"].rearrange("e d -> (e d)").partition_broadcast(P)).then_inc(r_ld, 16)
        sp.dma_start(b1e.rearrange("p (e c) -> p e c", e=E), a["L0_ffn_b1"].rearrange("e (c p) -> p e c", p=P),
                     allow_slow_non_contiguous=True).then_inc(r_ld, 16)
        with sp.Fori(0, NT) as j:
            y_out.wait(sp, j, 2)
            sp.sem_inc(y_free.sem, 1)
        y1v, y2v = img(y_dram[0:T]), img(y_dram[T:2 * T])
        with sp.Fori(0, B // 2) as r:
            for k in range(2):
                c_out[k].wait_before(sp, r, 1, alone=passed_sp)
                for buf, src in zip(comb[k], (img(h2_dram), img(x4_dram), y1v, y2v)):
                    sp.dma_start(buf, src[r * 2 + k]).then_inc(c_in[k].sem, 16)
            for k in range(2):
                c_done.wait(sp, r, k + 1, alone=passed_sp)
                sp.dma_start(out.rearrange("i (t p) d -> i p t d", p=P)[r * 2 + k], comb[k][4]).then_inc(c_out[k].sem, 16)
        for k in range(2):
            c_out[k].wait(sp, B // 2 - 1, 1)

    @block.gpsimd
    def _(pool):
        g = nc.gpsimd
        for c in (rstd_a, rstd_c, m_ready, mhl_ready, pool_c.c, w_hi, w_lo):
            c.open(pool)
        g.memset(ident[:], 0.0).then_inc(const_pool, 1)
        g.memset(blk[:], 0.0).then_inc(const_pool, 1)
        g.memset(ones[:], 1.0).then_inc(const_pool, 1)
        g.memset(halfneg[:], -0.5).then_inc(const_pool, 1)
        g.memset(wop[:], 0.0).then_inc(const_pool, 1)
        g.memset(vext, 1.0).then_inc(const_pool, 1)
        g.memset(sel[:], 0.0).then_inc(const_pool, 1)
        g.memset(selm[:], 0.0).then_inc(const_pool, 1)
        g.memset(wscale[:], WS).then_inc(const_pool, 1)
        pool.wait_ge(const_pool, 9)
        g.affine_select(out=ident[:], in_=ident[:], compare_op=ALU.not_equal, fill=1.0, base=0,
                        pattern=[[-1, P]], channel_multiplier=1).then_inc(const_pool, 1)
        pool.wait_ge(const_pool, 10)
        g.affine_select(out=tri[:], in_=ones[:], compare_op=ALU.is_gt, fill=0.0, base=0,
                        pattern=[[1, P]], channel_multiplier=-1).then_inc(tri_ready, 1)
        pool.wait_ge(tri_ready, 1)
        for q in range(G4):
            g.memset(blk[RB * q:RB * (q + 1), RB * q:RB * (q + 1)], 1.0).then_inc(const_pool, 1)
        pool.wait_ge(const_pool, 10 + G4)
        n = 0
        for dst, src in (
            (wq[:], a["L0_ffn_Wq"].rearrange("(c p) n -> p c n", p=P)),
            (wk_[:], a["L0_ffn_Wk"].rearrange("(c p) n -> p c n", p=P)),
            (wv[:], a["L0_ffn_Wv"].rearrange("(c p) n -> p c n", p=P)),
            (wg[:], a["L0_ffn_Wg"].rearrange("(c p) n -> p c n", p=P)),
            (h_t, a["L0_attn_W_v"].rearrange("(c p) n -> p c n", p=P)),
            (t0, a["L0_attn_W_o"].rearrange("(c p) n -> p c n", p=P)),
            (zs, a["L0_attn_splat_centers"]),
            (affT[:, 0:1], a["L0_attn_splat_log_scales"].rearrange("(k o) -> k o", o=1)),
            (g1[:], a["L0_ffn_ln1_g"].rearrange("(c p) -> p c", p=P)),
            (b1[:], a["L0_ffn_ln1_b"].rearrange("(c p) -> p c", p=P)),
            (g2b[:], a["L0_ffn_ln2_g"].partition_broadcast(P)),
            (b2b[:], a["L0_ffn_ln2_b"].partition_broadcast(P)),
        ):
            pool.dma_start(dst, src, allow_slow_non_contiguous=True).then_inc(const_ld, 16)
            n += 1
        wo_rows = a["L0_ffn_Wo"].rearrange("(g j d) n -> j d g n", g=4, j=4)
        for j in range(4):
            pool.dma_start(wop[32 * j:32 * j + DH], wo_rows[j]).then_inc(const_ld, 16)
            n += 1
        assert n == 16

        def inv_std(i, ln):
            var_a.wait(pool, i, ln + 1)
            g.tensor_tensor(rstd, var, halfneg[:], ALU.pow).then_inc(rstd_a.sem, 1)

        def expert_inputs(i):
            var_c.wait(pool, i, 1)
            g.tensor_tensor(rstdc, varc, halfneg[:], ALU.pow).then_inc(rstd_c.sem, 1)
            pool_c.start(pool, i)
            m0_ready.wait(pool, i, 1)
            pool_c.link(g.tensor_tensor(m, m, g2b[:].unsqueeze(1).broadcast_to([P, NS, D]), ALU.mult))
            g.tensor_tensor(m, m, b2b[:].unsqueeze(1).broadcast_to([P, NS, D]), ALU.add).then_inc(m_ready.sem, 1)
            m_ready.wait(pool, i, 1)
            mhl_stored.wait_before(pool, i, 1, alone=passed_pool)
            pool_c.link(g.tensor_copy(mhl[:, :, 0:D], m))
            g.tensor_tensor(mhl[:, :, D:2 * D].bitcast(BF16), m, mhl[:, :, 0:D], ALU.subtract).then_inc(mhl_ready.sem, 1)
            pool_c.end()

        def weights(i, n, hi, lo):
            w_ld.wait(pool, i, n)
            part_ = bass.ds(i * 1024, 1024)
            g.tensor_tensor(wraw, wraw, wscale[:].broadcast_to([P, 1024]), ALU.mult).then_inc(w_hi.sem, 1)
            w_hi.wait(pool, i, 2 * n - 1, alone=passed_pool)
            g.tensor_copy(hi[:, part_], wraw).then_inc(w_hi.sem, 1)
            w_hi.wait(pool, i, 2 * n, alone=passed_pool)
            g.tensor_tensor(lo[:, part_], wraw, hi[:, part_], ALU.subtract).then_inc(w_lo.sem, 1)

        def image_round(i, a_=True, b_=True, c_=True):
            if a_:
                inv_std(i + 1, 0)
            if b_:
                weights(i, 1, w1hi, w1lo)
                weights(i, 2, w2hi, w2lo)
            if a_:
                inv_std(i + 1, 1)
                inv_std(i + 1, 2)
            if c_:
                expert_inputs(i - 1)

        for ln in range(3):
            inv_std(0, ln)
        run_images(pool, image_round)
        pool.wait_ge(img_done_pe, 1)
        pool.wait_ge(img_done_act, 1)
        mhl_stored.wait(pool, B - 1, 1)
        x4_stored.wait(pool, B - 1, 1)
        g.iota(iota_i, pattern=[[1, P]], base=0, channel_multiplier=0).then_inc(r_pool, 1)
        g.iota(iota_pi, pattern=[[0, 1]], base=0, channel_multiplier=1).then_inc(r_pool, 1)
        g.iota(slot_i, pattern=[[P, NCOL]], base=2 * T + P, channel_multiplier=1).then_inc(r_pool, 1)
        g.memset(zero16, 0.0).then_inc(r_pool, 1)
        for c in (src_ready, dst_ready):
            c.open(pool)

        def gather(j):
            xT_psum.wait_before(pool, j, 1)
            g.tensor_copy(gidx[:], src_idx[:, bass.ds(j * 2, 2)]).then_inc(src_ready.sem, 1)
            src_ready.wait(pool, j, 1, alone=passed_pool)
            for t in range(2):
                g.indirect_dma_start(xg[:, t, :], None, m_dram, bass.IndirectOffsetOnAxis(ap=gidx[:, t:t + 1], axis=0)).then_inc(x_in.sem, 16)

        def scatter(j):
            y_ready.wait(pool, j, 1)
            g.tensor_copy(sidx[:], dst_idx[:, bass.ds(j * 2, 2)]).then_inc(dst_ready.sem, 1)
            dst_ready.wait(pool, j, 1, alone=passed_pool)
            for t in range(2):
                g.indirect_dma_start(y_dram, bass.IndirectOffsetOnAxis(ap=sidx[:, t:t + 1], axis=0), ys[:, t, :], None).then_inc(y_out.sem, 16)

        pool.wait_ge(route_done, 1)
        for j in range(3):
            gather(j)
        with pool.Fori(0, NT - 3) as j:
            gather(j + 3)
            scatter(j)
        for j in range(NT - 3, NT):
            scatter(j)
        c_first.open(pool)
        with pool.Fori(0, B // 2) as r:
            for k in range(2):
                c_in[k].wait(pool, r, 4)
                c_out[k].wait_before(pool, r, 1)
                g.tensor_tensor(comb[k][4], comb[k][0], comb[k][1], ALU.add).then_inc(c_first.sem, 1)

    @block.scalar
    def _(act):
        s = nc.scalar
        for c in (band_exp, tsq_ready, t0T_ready, aff_exp, ut_ready, z_ready, hhT_ready, big_hi, big_act,
                  negmT_ready, mT_ready, logit_read):
            c.open(act)
        act.wait_ge(const_ld, 256)
        s.activation(affT[:, 1:2], affT[:, 0:1], ACT.Exp).then_inc(prep_act, 1)
        s.activation(sqj[0:K, 0, :], zs, ACT.Square, accum_out=affT[:, 2:3]).then_inc(prep_act, 1)
        for g in range(NG):
            band_logit.wait(act, g, 1)
            s.activation(e10[:, 1:10], z10[:, 1:10], ACT.Exp).then_inc(band_exp.sem, 1)
            s.activation(e10[:, 0:1], z10[:, 0:1], ACT.Exp, scale=-1.0).then_inc(band_exp.sem, 1)

        def token_squares(i):
            t0_ready.wait(act, i, 1)
            for t in range(NS):
                last = s.activation(sqj[:, t, :], t0[:, t, :], ACT.Square, accum_out=tsq[:, t:t + 1])
            tsq_ready.sig(last)

        def splat_tokens(i):
            px_written.wait(act, i, 1)
            s.copy(t0T.rearrange("p a b -> p (a b)"), px[:]).then_inc(t0T_ready.sem, 1)

        def splat_exp(i):
            dist_ready.wait(act, i, 1)
            s.activation(aff, dist, ACT.Exp).then_inc(aff_exp.sem, 1)

        def splat_sums(i):
            px_written.wait(act, i, 3)
            s.copy(ut, px[:, 0:32].rearrange("p (a b) -> p a b", a=2))
            s.copy(affT, px[0:K, 256:512]).then_inc(ut_ready.sem, 1)

        def splat_states(i):
            px_written.wait(act, i, 4)
            s.copy(zs, px[0:K, 0:256]).then_inc(z_ready.sem, 1)

        def attention_input(i):
            px_written.wait(act, i, 6)
            big_written.wait_before(act, i, 14)
            for c in range(NC):
                last = s.activation(hhT[:, c, :], px[:, c * 256:(c + 1) * 256], ACT.Identity,
                                    bias=b1[:, c:c + 1], scale=g1[:, c:c + 1])
            hhT_ready.sig(last)

        def high_parts(i):
            big_written.wait(act, i, 1)
            s.copy(qk_hi, big[:, 0, :]).then_inc(big_hi.sem, 1)

        def first_stacks(i):
            big_written.wait(act, i, 2)
            s.activation(kst[:, 0:4].rearrange("p a b -> p (a b)"), big[:, 1, :], ACT.Identity, bias=kone[:, 0:1]).then_inc(big_act.sem, 1)
            big_written.wait(act, i, 4)
            s.copy(qst[:, 0:4].rearrange("p a b -> p (a b)"), big[:, 1, :]).then_inc(big_act.sem, 1)

        def values(i):
            big_written.wait(act, i, 14)
            s.copy(vext[:, :, :, 0:DH], big[:, 1, 0:512].rearrange("p (c h e) -> p c h e", c=NS, h=H)).then_inc(big_act.sem, 1)

        def maximum_rows(i):
            negmT_psum.wait(act, i, 1)
            s.copy(negmT, acc[0:32, 0, 0:128].bitcast(F16)).then_inc(negmT_ready.sem, 1)

        def second_stack(i):
            big_written.wait(act, i, 15)
            s.copy(qst[:, 0:4].rearrange("p a b -> p (a b)"), big[:, 0, :]).then_inc(big_act.sem, 1)

        def probabilities(i, u):
            big_written.wait(act, i, 17 + u)
            if u < 3:
                pv_done.wait_before(act, i, 8)
            else:
                pv_done.wait(act, i, u - 2)
            s.activation(probs[u % 3].rearrange("p r c q -> p (r c q)"), big[:, u % 2, :], ACT.Exp,
                         scale=float(DH) ** -0.5).then_inc(big_act.sem, 1)

        def router_tokens(i):
            py_written.wait(act, i, 2)
            s.copy(mT.rearrange("p a b -> p (a b)"), py[:]).then_inc(mT_ready.sem, 1)

        def router_logits(i):
            py_written.wait(act, i, 3)
            s.copy(lall[:].rearrange("p t e -> p (t e)")[:, bass.ds(i * 2 * E, 2 * E)], py[:, 0:2 * E]).then_inc(logit_read.sem, 1)

        def image_round(i, a_=True, b_=True, c_=True):
            if a_:
                token_squares(i + 1)
                splat_tokens(i + 1)
            if b_:
                first_stacks(i)
            if a_:
                splat_exp(i + 1)
                splat_sums(i + 1)
            if b_:
                values(i)
            if a_:
                splat_states(i + 1)
            if b_:
                maximum_rows(i)
                second_stack(i)
                for u in range(6):
                    probabilities(i, u)
            if a_:
                attention_input(i + 1)
            if b_:
                for u in (6, 7):
                    probabilities(i, u)
            if c_:
                router_tokens(i - 1)
            if a_:
                high_parts(i + 1)
            if c_:
                router_logits(i - 1)

        token_squares(0)
        splat_tokens(0)
        splat_exp(0)
        splat_sums(0)
        splat_states(0)
        attention_input(0)
        high_parts(0)
        run_images(act, image_round)
        logit_read.wait(act, B - 1, 1)
        act.sem_inc(img_done_act, 1)
        act.wait_ge(r_dve, ROUTE_MASKS)
        s.activation(wts[:, 1, :], mx2, ACT.Exp).then_inc(r_act, 1)
        act.wait_ge(route_done, 1)
        for c in (xT_hi_ready, gelu_done):
            c.open(act)
        act.wait_ge(r_ld, 32)

        def rows_in(j):
            xT_psum.wait(act, j, 1)
            up_done.wait_before(act, j, 2)
            s.activation(xT_hi.rearrange("p a b -> p (a b)"), px[:, 0:256].bitcast(F16), ACT.Copy).then_inc(xT_hi_ready.sem, 1)

        def hidden_half(j, e, half):
            up_done.wait(act, j, half + 1)
            split_done.wait_before(act, j, half + 1)
            for k in range(FC // 2):
                f = half * (FC // 2) + k
                last = s.activation(hf[:, f, :], big[:, half, k * TT:(k + 1) * TT], ACT.Gelu_apprx_tanh,
                                    bias=b1e[:, bass.ds(e * FC + f, 1)], scale=1.0 / WS)
            gelu_done.sig(last)

        def hidden(j):
            e = expert(act, j)
            hidden_half(j, e, 0)
            hidden_half(j, e, 1)

        rows_in(0)
        hidden(0)
        rows_in(1)
        with act.Fori(0, NT - 2) as j:
            hidden(j + 1)
            rows_in(j + 2)
        hidden(NT - 1)

    @block.vector
    def _(dve):
        v = nc.vector
        for c in (dwt_chain.c, dwt_logits, part_ready, band_logit, rec_ready, var_a, t0_ready, dist_ready, aff_ready, h2_ready,
                  hn_ready, big_dve, negm_ready, ctx_ready, x4_ready, var_c, m0_ready, dve_a.c, dve_b.c, dve_c.c, dve_ctx.c):
            c.open(dve)
        steps = [0]

        def step(ins):
            steps[0] += 1
            ins.then_inc(prep_dve, 1)
            dve.wait_ge(prep_dve, steps[0])

        step(v.memset(rscale[:, 0:4], 1.0 / 64))
        step(v.memset(rscale[:, 4:7], 1.0 / 16))
        step(v.memset(rscale[:, 7:10], 1.0 / 4))
        dve.wait_ge(dwt_w_ld, 16 * (4 * G4 + 4))

        def dwt_group(g):
            ch = dwt_chain
            ch.start(dve, g)
            rec_ready.wait_before(dve, g, 1)
            dve.wait_ge(x_ld[g % 2], 16 * (g // 2 + 1))
            cur = xin[g % 2]
            n = X
            rows, cols = RROWS, D
            for lv in (1, 2, 3):
                q = n // 4
                xv = cur.rearrange("p (r two) -> p r two", two=2)
                v.tensor_tensor(col_s[:, 0:n // 2], xv[:, :, 0], xv[:, :, 1], ALU.add)
                ch.link(v.tensor_tensor(col_d[:, 0:n // 2], xv[:, :, 0], xv[:, :, 1], ALU.subtract))
                w = cols // 2
                sv = col_s[:, 0:n // 2].rearrange("p (r two c) -> p r two c", two=2, c=w)
                dv = col_d[:, 0:n // 2].rearrange("p (r two c) -> p r two c", two=2, c=w)
                o = lambda t: t.rearrange("p (r c) -> p r c", c=w)
                v.tensor_tensor(o(app[lv]), sv[:, :, 0], sv[:, :, 1], ALU.add)
                v.tensor_tensor(o(det[lv][:, 0:q]), sv[:, :, 0], sv[:, :, 1], ALU.subtract)
                v.tensor_tensor(o(det[lv][:, q:2 * q]), dv[:, :, 0], dv[:, :, 1], ALU.add)
                ch.link(v.tensor_tensor(o(det[lv][:, 2 * q:3 * q]), dv[:, :, 0], dv[:, :, 1], ALU.subtract))
                cur, n, rows, cols = app[lv], q, rows // 2, w
            ch.link(v.tensor_tensor_reduce(junk[:, 0:X // 64], app[3], wapp, 0.125, 0.0, ALU.mult, ALU.add, part[:, 0:1]))
            for k, lv in ((1, 3), (4, 2), (7, 1)):
                n = 3 * X // 4 ** lv
                for o in range(3):
                    wv_o = wdet[lv].rearrange("p (n o) -> p n o", o=3)[:, :, o]
                    ins = v.tensor_tensor_reduce(junk[:, 0:n], det[lv], wv_o, 0.5 ** lv, 0.0, ALU.mult, ALU.add,
                                                 part[:, k + o:k + o + 1])
                    if (k, o) == (7, 2):
                        part_ready.sig(ins)
                    else:
                        ch.link(ins)
            part_sum.wait(dve, g, 1)
            v.tensor_tensor(z10, px[:, 0:10], bias10, ALU.add).then_inc(dwt_logits.sem, 1)
            dwt_logits.wait(dve, g, 1)
            z3 = z10[:, 1:10].rearrange("p (l o) -> p l o", o=3)
            ch.link(v.tensor_reduce(s3, z3, AX.X, ALU.max))
            v.tensor_tensor(z3, z3, s3.unsqueeze(2).broadcast_to([P, 3, 3]), ALU.subtract).then_inc(band_logit.sem, 1)
            band_exp.wait(dve, g, 2)
            e3 = e10[:, 1:10].rearrange("p (l o) -> p l o", o=3)
            ch.link(v.tensor_reduce(s3, e3, AX.X, ALU.add))
            ch.link(v.reciprocal(r3, s3))
            ch.link(v.tensor_tensor(w10[:, 1:10].rearrange("p (l o) -> p l o", o=3), e3, r3.unsqueeze(2).broadcast_to([P, 3, 3]), ALU.mult))
            ch.link(v.tensor_scalar(e10[:, 0:1], e10[:, 0:1], 1.0, None, ALU.add))
            ch.link(v.reciprocal(w10[:, 0:1], e10[:, 0:1]))
            ch.link(v.tensor_tensor(w10, w10, rscale, ALU.mult))
            ch.link(v.tensor_scalar(nw10, w10, -1.0, None, ALU.mult))
            ch.link(v.tensor_scalar(app[3], app[3], w10[:, 0:1], None, ALU.mult))
            low = app[3]
            for k, lv in ((1, 3), (4, 2), (7, 1)):
                n = X // 4 ** lv
                w = D // 2 ** lv
                hb, vb, db = (det[lv][:, j * n:(j + 1) * n].rearrange("p (r c) -> p r c", c=w) for j in range(3))
                lowv = low.rearrange("p (r c) -> p r c", c=w)
                sv = col_s[:, 0:2 * n].rearrange("p (r two c) -> p r two c", two=2, c=w)
                dv = col_d[:, 0:2 * n].rearrange("p (r two c) -> p r two c", two=2, c=w)
                v.scalar_tensor_tensor(sv[:, :, 0], hb, w10[:, k:k + 1], lowv, ALU.mult, ALU.add)
                v.scalar_tensor_tensor(sv[:, :, 1], hb, nw10[:, k:k + 1], lowv, ALU.mult, ALU.add)
                ch.link(v.tensor_scalar(vb, vb, w10[:, k + 1:k + 2], None, ALU.mult))
                v.scalar_tensor_tensor(dv[:, :, 0], db, w10[:, k + 2:k + 3], vb, ALU.mult, ALU.add)
                ch.link(v.scalar_tensor_tensor(dv[:, :, 1], db, nw10[:, k + 2:k + 3], vb, ALU.mult, ALU.add))
                if lv == 1:
                    if g >= 2:
                        rec_stored.wait(dve, g, -1)
                    dst = rec[g % 2]
                else:
                    dst = app[lv - 1]
                ov = dst.rearrange("p (n two) -> p n two", two=2)
                v.tensor_tensor(ov[:, :, 0], col_s[:, 0:2 * n], col_d[:, 0:2 * n], ALU.add)
                ins = v.tensor_tensor(ov[:, :, 1], col_s[:, 0:2 * n], col_d[:, 0:2 * n], ALU.subtract)
                if lv == 1:
                    rec_ready.sig(ins)
                else:
                    ch.link(ins)
                low = dst
            ch.end()

        for g in range(NG):
            dwt_group(g)

        dve.wait_ge(const_pool, 10 + G4)
        step(v.tensor_copy(ident16[:], ident[:]))
        src = ident16[:].rearrange("p (s r d) -> p s r d", s=4, r=2)
        stk = lambda n: sel[:, n].rearrange("p s (r b d) -> p s r b d", r=2, b=4)
        for n, b in ((0, 0), (0, 2), (1, 1), (2, 0), (2, 1), (3, 2)):
            for sl in range(4):
                step(v.tensor_copy(stk(n)[:, sl, :, b, :], src[:, sl]))
        for part_, base in ((0, 0), (1, 16)):
            step(v.tensor_copy(selm[:, :, :, 48 + part_], ident16[0:32, base:base + 16].rearrange("p (s r) -> p s r", r=2)))
        step(v.tensor_reduce(kone[:], ident[:].rearrange("p (r c) -> p r c", r=2)[:, :, 48:50], AX.XY, ALU.add))
        dve.wait_ge(prep_act, 2)
        step(v.tensor_scalar(affT[:, 1:2], affT[:, 1:2], 0.1, 2.0, ALU.max, ALU.min))
        step(v.tensor_tensor(affT[:, 3:4], affT[:, 1:2], affT[:, 1:2], ALU.mult))
        step(v.reciprocal(affT[:, 4:5], affT[:, 3:4]))
        step(v.tensor_scalar(affT[:, 4:5], affT[:, 4:5], -0.5, None, ALU.mult))
        step(v.tensor_scalar(affT[:, 16:32], ident[0:K, 0:K], affT[:, 2:3], None, ALU.mult))
        step(v.tensor_scalar(affT[:, 32:48], ident[0:K, 0:K], affT[:, 4:5], None, ALU.mult))
        v.memset(x4[:, 0, 0:1], 0.0).then_inc(const_dve, 1)
        dve.wait_ge(prep_pe, 1)
        step(v.tensor_copy(csq_b[:].rearrange("p a b -> p (a b)"), py[:, 0:32]))
        step(v.tensor_copy(cT[:].rearrange("p a b -> p (a b)"), py[:, 32:64]))
        v.tensor_copy(t0T.rearrange("p a b -> p (a b)"), px[:]).then_inc(const_dve, 1)
        dve.wait_ge(prep_pe, 2)
        v.tensor_copy(wvo[:].rearrange("p a b -> p (a b)"), py[:]).then_inc(const_dve, 1)
        dve.wait_ge(const_dve, 3)

        def stats(ch, src, st_, mv_, var_, ready):
            for t in range(NS):
                last = v.bn_stats(st_[:, t, :], src[:, t, :])
            ch.link(last, alone=passed_dve)
            for t in range(NS):
                last = v.bn_aggr(mv_[:, t, :], st_[:, t, :])
            ch.link(last)
            v.tensor_scalar(var_, mv_[:, :, 1], EPS, None, ALU.add).then_inc(ready.sem, 1)

        def normed(dst, src, mv_, rstd_):
            for t in range(NS):
                last = v.tensor_scalar(dst[:, t, :], src[:, t, :], mv_[:, t, 0:1], rstd_[:, t:t + 1], ALU.subtract, ALU.mult)
            return last

        def x3_of(i):
            return v3(x3[:, bass.ds((i % 2) * 512, 512)], 2)

        def token_stats(i):
            dve_a.start(dve, i)
            h_ld.wait(dve, i, 1, alone=passed_dve)
            stats(dve_a, h_t, st, mv, var, var_a)

        def normed_tokens(i):
            rstd_a.wait(dve, i, 1)
            px_written.wait_before(dve, i, 6)
            t0_ready.sig(normed(t0, h_t, mv, rstd))

        def distances(i):
            px_written.wait(dve, i, 2)
            tsq_ready.wait(dve, i, 1)
            dve_a.link(v.scalar_tensor_tensor(dist, px[:, 0:32].rearrange("p (a b) -> p a b", a=2), -2.0,
                                              csq_b[:, 0:1, :].broadcast_to([P, NS, K]), ALU.mult, ALU.add))
            dve_a.link(v.tensor_tensor(dist, dist, tsq.unsqueeze(2).broadcast_to([P, NS, K]), ALU.add))
            v.scalar_tensor_tensor(dist, dist, 0.0, csq_b[:, 1:2, :].broadcast_to([P, NS, K]), ALU.max, ALU.mult).then_inc(dist_ready.sem, 1)

        def affinities(i):
            aff_exp.wait(dve, i, 1)
            dve_a.link(v.tensor_reduce(affsum, aff, AX.X, ALU.add))
            dve_a.link(v.tensor_scalar(affsum, affsum, 1e-8, None, ALU.add))
            dve_a.link(v.reciprocal(affrec, affsum))
            v.tensor_tensor(aff, aff, affrec.unsqueeze(2).broadcast_to([P, NS, K]), ALU.mult).then_inc(aff_ready.sem, 1)

        def splat_residual(i):
            px_written.wait(dve, i, 5)
            h2_stored.wait_before(dve, i, 1)
            v.tensor_tensor(h2.rearrange("p a b -> p (a b)"), h_t.rearrange("p a b -> p (a b)"), px[:], ALU.add).then_inc(h2_ready.sem, 1)
            h2_ready.wait(dve, i, 1, alone=passed_dve)
            stats(dve_a, h2, st, mv, var, var_a)

        def normed_residual(i):
            rstd_a.wait(dve, i, 2)
            dve_a.link(normed(x3_of(i), h2, mv, rstd), alone=passed_dve)
            stats(dve_a, x3_of(i), st, mv, var, var_a)

        def attention_input(i):
            rstd_a.wait(dve, i, 3)
            hn_ready.sig(normed(t0, x3_of(i), mv, rstd))
            dve_a.end()

        def low_parts(i):
            big_hi.wait(dve, i, 1)
            v.tensor_tensor(qk_lo, big[:, 0, :], qk_hi, ALU.subtract).then_inc(big_dve.sem, 1)

        def first_k_stack(i):
            big_written.wait(dve, i, 3)
            v.tensor_scalar(kst[:, 4:8].rearrange("p a b -> p (a b)"), big[:, 0, :], kone[:, 0:1], None, ALU.add).then_inc(big_dve.sem, 1)

        def q_stack(i, u):
            big_written.wait(dve, i, u)
            v.tensor_copy(qst[:, 4:8].rearrange("p a b -> p (a b)"), big[:, (u + 1) % 2, :]).then_inc(big_dve.sem, 1)

        def maxima(i, us):
            for u in us:
                big_written.wait(dve, i, 6 + u)
                v.tensor_reduce(mx[:, :, 2 * u:2 * u + 2].rearrange("p c r -> p r c"),
                                big[:, (u + 1) % 2, :].rearrange("p (r c k) -> p r c k", r=2, c=NS), AX.X, ALU.max,
                                negate=True).then_inc(big_dve.sem, 1)

        def maximum_parts(i):
            dve_b.start(dve, i)
            big_dve.wait(dve, i, 11)
            dve_b.link(v.tensor_copy(neghl[:, :, 0:H], mx))
            v.tensor_tensor(neghl[:, :, H:2 * H], mx, neghl[:, :, 0:H], ALU.subtract).then_inc(negm_ready.sem, 1)
            dve_b.end()

        def context(i):
            dve_ctx.start(dve, i)
            pv_done.wait(dve, i, 8)
            dve_ctx.link(v.transpose(cturn, acc[:].rearrange("p a b -> p (a b)")))
            py_written.wait_before(dve, i, 1)
            dve_ctx.link(v.reciprocal(crec, ct3[:, :, DH]))
            dve_ctx.link(v.tensor_tensor(ct3[:, :, 0:DH], ct3[:, :, 0:DH], crec.unsqueeze(2).broadcast_to([P, 32, DH]), ALU.mult))
            v.transpose(ctxn.rearrange("p a b -> p (a b)"), cturn).then_inc(ctx_ready.sem, 1)
            dve_ctx.end()

        def residual(i):
            dve_c.start(dve, i)
            py_written.wait(dve, i, 1)
            x4_stored.wait_before(dve, i, 1)
            v.tensor_tensor(x4, x3_of(i), py[:].rearrange("p (a b) -> p a b", a=2), ALU.add).then_inc(x4_ready.sem, 1)

        def residual_stats(i):
            x4_ready.wait(dve, i, 1, alone=passed_dve)
            stats(dve_c, x4, stc, mvc, varc, var_c)

        def expert_input(i):
            rstd_c.wait(dve, i, 1)
            py_written.wait_before(dve, i, 2)
            mhl_ready.wait_before(dve, i, 1)
            m0_ready.sig(normed(m, x4, mvc, rstdc))
            dve_c.end()

        def image_round(i, a_=True, b_=True, c_=True):
            if a_:
                token_stats(i + 1)
            if c_:
                context(i - 1)
            if a_:
                normed_tokens(i + 1)
            if b_:
                low_parts(i)
                first_k_stack(i)
                q_stack(i, 5)
            if a_:
                distances(i + 1)
            if b_:
                maxima(i, range(0, 2))
            if a_:
                affinities(i + 1)
            if b_:
                maxima(i, range(2, 8))
                maximum_parts(i)
            if c_:
                residual(i - 1)
            if a_:
                splat_residual(i + 1)
            if b_:
                q_stack(i, 16)
            if a_:
                normed_residual(i + 1)
            if c_:
                residual_stats(i - 1)
            if a_:
                attention_input(i + 1)
            if c_:
                expert_input(i - 1)

        token_stats(0)
        normed_tokens(0)
        distances(0)
        affinities(0)
        splat_residual(0)
        normed_residual(0)
        attention_input(0)
        run_images(dve, image_round)

        m0_ready.wait(dve, B - 1, 1)
        dve.wait_ge(img_done_act, 1)
        dve.wait_ge(img_done_pe, 1)
        mhl_stored.wait(dve, B - 1, 1)
        x4_stored.wait(dve, B - 1, 1)
        dve.wait_ge(r_pool, 4)
        rsteps = [0]

        def rstep(ins):
            rsteps[0] += 1
            ins.then_inc(r_dve, 1)
            dve.wait_ge(r_dve, rsteps[0])

        row = lambda t: t.unsqueeze(2).broadcast_to([P, NTL, E])
        v.tensor_copy(iota_f, iota_i)
        v.tensor_copy(iota_p, iota_pi)
        v.tensor_copy(slot_f, slot_i)
        rstep(v.tensor_copy(ident_bf[:], ident[:]))
        experts = iota_f[:, 0:E].unsqueeze(1).broadcast_to([P, NTL, E])
        v.memset(minus_p, -float(P))
        v.tensor_scalar(cols1, iota_f[:, 0:2 * NTL], 1.0, None, ALU.add)
        v.tensor_scalar(jstep, iota_f[:, 0:16], float(TT), None, ALU.mult)
        rstep(v.tensor_copy(iota_h, iota_f))

        def choose(l, mx_, mask):
            rstep(v.tensor_reduce(mx_, l, AX.X, ALU.max))
            rstep(v.tensor_tensor(te3(cand), l, row(mx_), ALU.is_lt))
            rstep(v.scalar_tensor_tensor(te3(cand), te3(cand), 16.0, experts, ALU.mult, ALU.add))
            rstep(v.tensor_reduce(pick, te3(cand), AX.X, ALU.min))
            rstep(v.tensor_tensor(te3(mask), experts, row(pick), ALU.is_equal))

        choose(lall[:], mx1, mask1)
        rstep(v.scalar_tensor_tensor(te3(lrest), te3(mask1), -1e30, lall[:], ALU.mult, ALU.add))
        choose(te3(lrest), mx2, mask2)
        rstep(v.tensor_tensor(mx2, mx2, mx1, ALU.subtract))
        rstep(v.tensor_tensor(cmask, mask1, mask2, ALU.add))
        assert rsteps[0] == ROUTE_MASKS
        dve.wait_ge(r_act, 1)
        rstep(v.tensor_scalar(mx1, wts[:, 1, :], 1.0, None, ALU.add))
        rstep(v.reciprocal(wts[:, 0, :], mx1))
        rstep(v.tensor_tensor(wts[:, 1, :], wts[:, 1, :], wts[:, 0, :], ALU.mult))
        dve.wait_ge(r_pe, 1)
        rstep(v.tensor_copy(ra, py[:, 0:NTL * E]))
        x, y = ra, rb_
        for s_ in (1, 2, 4, 8, 16):
            v.tensor_tensor(te3(y)[:, s_:], te3(x)[:, s_:], te3(x)[:, :NTL - s_], ALU.add)
            rstep(v.tensor_copy(te3(y)[:, :s_], te3(x)[:, :s_]))
            x, y = y, x
        count = te3(x)[:, NTL - 1, :]
        rstep(v.tensor_tensor(rank, x, py[:, 0:NTL * E], ALU.subtract))
        rstep(v.tensor_tensor(rank, rank, px[:, 0:NTL * E], ALU.add))
        cm3 = cmp.rearrange("p (e j) -> p e j", e=E)
        rstep(v.tensor_tensor(cm3, count.unsqueeze(2).broadcast_to([P, E, 16]), jstep.unsqueeze(1).broadcast_to([P, E, 16]), ALU.is_gt))
        rstep(v.tensor_reduce(ntile, cm3, AX.X, ALU.add))
        sq = cmp[:, 0:E * E].rearrange("p (e j) -> p e j", e=E)
        ie = iota_f[:, 0:E]
        rstep(v.tensor_tensor(sq, ie.unsqueeze(2).broadcast_to([P, E, E]), ie.unsqueeze(1).broadcast_to([P, E, E]), ALU.is_gt))
        rstep(v.tensor_tensor(sq, sq, ntile.unsqueeze(1).broadcast_to([P, E, E]), ALU.mult))
        rstep(v.tensor_reduce(tbase, sq, AX.X, ALU.add))
        rstep(v.tensor_tensor(tend, tbase, ntile, ALU.add))
        t3 = tcmp.rearrange("p (j e) -> p j e", e=E)
        rstep(v.tensor_tensor(t3, tend.unsqueeze(1).broadcast_to([P, NT, E]), iota_f[:, 0:NT].unsqueeze(2).broadcast_to([P, NT, E]), ALU.is_le))
        rstep(v.tensor_reduce(tef, t3, AX.X, ALU.add))
        rstep(v.tensor_scalar(tef, tef, float(E - 1), None, ALU.min))
        rstep(v.tensor_copy(tex[:], tef[0:1, :]))
        rstep(v.tensor_scalar(tbase, tbase, float(TT), None, ALU.mult))
        rstep(v.tensor_tensor(te3(rank), te3(rank), tbase.unsqueeze(1).broadcast_to([P, NTL, E]), ALU.add))
        for k, mask in enumerate((mask1, mask2)):
            rstep(v.tensor_tensor(mask, mask, rank, ALU.mult))
            rstep(v.tensor_reduce(pos[:, k * NTL:(k + 1) * NTL], te3(mask), AX.X, ALU.add))
        rstep(v.tensor_copy(pos_i, pos))
        v.tensor_scalar(posb_i, pos_i, P - 1, None, ALU.bitwise_and)
        rstep(v.tensor_scalar(posa_i, pos_i, 7, None, ALU.logical_shift_right))
        v.tensor_copy(posa, posa_i)
        rstep(v.tensor_copy(posb, posb_i))
        assert rsteps[0] == ROUTE_RANKS, rsteps[0]
        hot_ready.open(dve)
        with dve.Fori(0, 2 * NTL // 8) as r:
            for half in range(2):
                hot_used.wait_before(dve, r, half + 1)
                for k in range(4):
                    n = 4 * half + k
                    col = r * 8 + n
                    v.tensor_scalar(hotb[:, n, :], iota_h, posb[:, bass.ds(col, 1)], None, ALU.is_equal)
                    v.tensor_scalar(hota[:, n, 0, :], iota_h[:, 0:NCOL], posa[:, bass.ds(col, 1)], iota_p, ALU.is_equal, ALU.mult)
                    last = v.tensor_scalar(hota[:, n, 1, :], iota_h[:, 0:NCOL], posa[:, bass.ds(col, 1)], cols1[:, bass.ds(col, 1)], ALU.is_equal, ALU.mult)
                hot_ready.sig(last)
        dve.wait_ge(r_pe, 2)
        rstep(v.scalar_tensor_tensor(tok, px[:, NCOL:2 * NCOL], float(P), minus_p, ALU.mult, ALU.add))
        rstep(v.tensor_tensor(tok, tok, px[:, 0:NCOL], ALU.add))
        rstep(v.tensor_scalar(emp, tok, -0.5, None, ALU.is_lt))
        rstep(v.tensor_tensor(emp, emp, slot_f, ALU.mult))
        rstep(v.tensor_tensor(dest, tok, emp, ALU.add))
        rstep(v.tensor_copy(dst_idx[:], dest))
        rstep(v.tensor_scalar(emp, tok, float(T), -float(T), ALU.is_ge, ALU.mult))
        rstep(v.tensor_tensor(tok, tok, emp, ALU.add))
        rstep(v.tensor_scalar(tok, tok, 0.0, None, ALU.max))
        v.tensor_copy(src_idx[:], tok).then_inc(route_done, 1)
        dve.wait_ge(route_done, 1)

        for c in (xT_lo_ready, split_done, y_ready, hi_chain):
            c.open(dve)
        dve.wait_ge(r_ld, 32)

        def split(j, half):
            sl = slice(half * (FC // 2), (half + 1) * (FC // 2))
            gelu_done.wait(dve, j, half + 1)
            down_done.wait_before(dve, j, 1)
            v.tensor_copy(h_hi[:, sl], hf[:, sl]).then_inc(hi_chain.sem, 1)
            hi_chain.wait(dve, j, half + 1)
            v.tensor_tensor(h_lo[:, sl], hf[:, sl], h_hi[:, sl], ALU.subtract).then_inc(split_done.sem, 1)

        def rows_in(j):
            xT_psum.wait(dve, j, 1)
            up_done.wait_before(dve, j, 2)
            v.tensor_copy(xT_lo.rearrange("p a b -> p (a b)"), py[:, 0:256].bitcast(BF16)).then_inc(xT_lo_ready.sem, 1)

        def rows_out(j, e):
            down_done.wait(dve, j, 1)
            y_free.wait_before(dve, j, 1)
            for t in range(2):
                last = v.scalar_tensor_tensor(ys[:, t, :], acc[:, 2 * t, :], 1.0 / WS, b2e[:, bass.ds(e * D, D)], ALU.mult, ALU.add)
            y_ready.sig(last)

        rows_in(0)
        rows_in(1)
        with dve.Fori(0, NT - 2) as j:
            split(j, 0)
            split(j, 1)
            rows_in(j + 2)
            rows_out(j, expert(dve, j))
        for j in (NT - 2, NT - 1):
            split(j, 0)
            split(j, 1)
            rows_out(j, expert(dve, j))

        c_done.open(dve)
        c_mid.open(dve)
        with dve.Fori(0, B // 2) as r:
            for k in range(2):
                c_first.wait(dve, r, k + 1)
                for n in range(2):
                    for t in range(NS):
                        o = comb[k][4][:, t, :]
                        last = v.scalar_tensor_tensor(o, comb[k][2 + n][:, t, :], wts[:, n, :][:, bass.ds(r * 4 + 2 * k + t, 1)], o, ALU.mult, ALU.add)
                    if n == 0:
                        c_mid.sig(last)
                        c_mid.wait(dve, r, k + 1)
                c_done.sig(last)

    @block.tensor
    def _(pe):
        t_ = nc.tensor
        for c in (part_sum, px_written, big_written, negmT_psum, pv_done, py_written):
            c.open(pe)
        pe.wait_ge(const_pool, 10 + G4)
        for g in range(NG):
            part_ready.wait(pe, g, 1)
            t_.matmul(px[:, 0:10], blk[:], part, start=True, stop=True).then_inc(part_sum.sem, 1)
        pe.wait_ge(const_dve, 1)
        dwt_logits.wait(pe, NG - 1, 1)
        t_.matmul(py[:, 0:32], ones[0:K, :], affT[:, 16:48], start=True, stop=True)
        for c in range(NC):
            t_.transpose(py[:, 32 + 16 * c:48 + 16 * c], zs[:, c * P:(c + 1) * P], ident[0:K, 0:K])
        for c in range(NC):
            for k in range(NC):
                last = t_.transpose(px[:, k * 256 + c * P:k * 256 + (c + 1) * P], h_t[:, c, k * P:(k + 1) * P], ident[:])
        last.then_inc(prep_pe, 1)
        pe.wait_ge(const_dve, 2)
        for c in range(NC):
            for k in range(NC):
                last = t_.matmul(py[:, c * 256:(c + 1) * 256], t0T[:, k, c * P:(c + 1) * P], t0[:, k, :], start=(k == 0), stop=(k == NC - 1))
        last.then_inc(prep_pe, 1)
        pe.wait_ge(const_dve, 3)

        def turned(dst, src):
            for c in range(NC):
                for t in range(NS):
                    last = t_.transpose(dst[:, c * 256 + t * P:c * 256 + (t + 1) * P], src[:, t, c * P:(c + 1) * P], ident[:])
            return last

        def splat_tokens(i):
            t0_ready.wait(pe, i, 1)
            hhT_ready.wait_before(pe, i, 1)
            px_written.sig(turned(px, t0))

        def splat_products(i):
            t0T_ready.wait(pe, i, 1)
            for t in range(NS):
                for c in range(NC):
                    last = t_.matmul(px[:, t * K:(t + 1) * K], t0T[:, c, t * P:(t + 1) * P], cT[:, c, :], start=(c == 0), stop=(c == NC - 1))
            px_written.sig(last)

        def splat_sums(i):
            aff_ready.wait(pe, i, 1)
            for c in range(NC):
                for t in range(NS):
                    t_.matmul(px[:, c * K:(c + 1) * K], t0[:, t, c * P:(c + 1) * P], aff[:, t, :], start=(t == 0), stop=(t == NS - 1))
            for t in range(NS):
                last = t_.transpose(px[0:K, 256 + t * P:256 + (t + 1) * P], aff[:, t, :], ident[:])
            px_written.sig(last)

        def splat_states(i):
            ut_ready.wait(pe, i, 1)
            for c in range(NC):
                last = t_.matmul(px[0:K, 0:256], ut[:, c, :], wvo[:, c, :], start=(c == 0), stop=(c == NC - 1))
            px_written.sig(last)

        def splat_output(i):
            z_ready.wait(pe, i, 1)
            for t in range(NS):
                last = t_.matmul(px[:, t * 256:(t + 1) * 256], affT[:, t * P:(t + 1) * P], zs, start=True, stop=True)
            px_written.sig(last)

        def attention_input(i):
            hn_ready.wait(pe, i, 1)
            px_written.sig(turned(px, t0))

        def stack_half(i, u, half, q, parts, with_max=False):
            slot_free(i, u)
            hi, lo = parts
            for k in range(4):
                s = 4 * half + k
                src = (q * 2 + s // 4) * 256
                dst = big[:, u % 2, k * 256:(k + 1) * 256]
                t_.matmul(dst, sel[:, hi, s % 4, :], qk_hi[:, src:src + 256], start=True, stop=False)
                last = t_.matmul(dst, sel[:, lo, s % 4, :], qk_lo[:, src:src + 256], start=False, stop=not with_max)
                if with_max:
                    last = t_.matmul(dst, selm[:, s, :, :].rearrange("p r c -> p (r c)"), negmT, start=False, stop=True)
            big_written.sig(last)

        def scores(i, u, s, turned_):
            slot_free(i, u)
            for c in range(NS):
                for r in range(2):
                    rows = slice(64 * r, 64 * r + 64)
                    x, y = (kst, qst) if turned_ else (qst, kst)
                    dst = big[:, u % 2, r * 512 + c * 256:r * 512 + (c + 1) * 256]
                    last = t_.matmul(dst, x[rows, s, c * P:(c + 1) * P], y[rows, s, :], start=True, stop=True)
            big_written.sig(last)

        def context(i, s):
            big_act.wait(pe, i, 5 + s)
            for c in range(NS):
                for r in range(2):
                    h = 2 * s + r
                    j = h % 4
                    last = t_.matmul(acc[32 * j:32 * j + 32, h // 4, :], vext[:, c, h, :], probs[s % 3][:, r, c, :],
                                     start=(c == 0), stop=(c == NS - 1), tile_position=(0, 32 * j))
            pv_done.sig(last)

        def projections(i):
            hhT_ready.wait(pe, i, 1)
            slot_free(i, 0)
            for q, w in enumerate((wq, wk_)):
                for o in range(NC):
                    for c in range(NC):
                        last = t_.matmul(big[:, 0, q * 512 + o * 256:q * 512 + (o + 1) * 256], w[:, c, o * P:(o + 1) * P], hhT[:, c, :],
                                         start=(c == 0), stop=(c == NC - 1))
            big_written.sig(last)

        def values(i):
            slot_free(i, 13)
            for t in range(NS):
                for c in range(NC):
                    last = t_.matmul(big[:, 1, t * 256:(t + 1) * 256], hhT[:, c, t * P:(t + 1) * P], wv[:, c, :], start=(c == 0), stop=(c == NC - 1))
            big_written.sig(last)

        def first_stacks(i):
            big_dve.wait(pe, i, 1)
            stack_half(i, 1, 0, 1, (0, 1))
            stack_half(i, 2, 1, 1, (0, 1))
            stack_half(i, 3, 0, 0, (2, 3))
            stack_half(i, 4, 1, 0, (2, 3))

        def keep_clock(n):
            for _ in range(n):
                t_.matmul(acc[:, 3, :], ident16[:], sel[:, 0, 0:2, :].rearrange("p a b -> p (a b)"), start=True, stop=True)

        def first_scores(i, ss):
            for s in ss:
                keep_clock(FILL[0])
                if s == 0:
                    big_act.wait(pe, i, 2)
                    big_dve.wait(pe, i, 3)
                scores(i, 5 + s, s, False)

        def maximum_rows(i):
            negm_ready.wait(pe, i, 1)
            ctx_ready.wait_before(pe, i, 1)
            for c in range(NS):
                last = t_.transpose(acc[0:32, 0, c * 64:(c + 1) * 64].bitcast(F16), neghl[:, c, :], ident16[:])
            negmT_psum.sig(last)

        def second_stacks(i):
            negmT_ready.wait(pe, i, 1)
            stack_half(i, 14, 0, 0, (2, 3), True)
            stack_half(i, 15, 1, 0, (2, 3), True)

        def attention(i, ss):
            for s in ss:
                if s == 0:
                    big_act.wait(pe, i, 4)
                    big_dve.wait(pe, i, 12)
                scores(i, 16 + s, s, True)
                if s >= 2:
                    context(i, s - 2)

        def output_projection(i, t):
            if t == 0:
                ctx_ready.wait(pe, i, 1)
                logit_read.wait_before(pe, i, 1)
            for k in range(4):
                last = t_.matmul(py[:, t * 256:(t + 1) * 256], ctxn[:, k, t * P:(t + 1) * P], wop[:, k, :], start=(k == 0), stop=(k == 3))
            if t == 1:
                py_written.sig(last)

        def router_tokens(i):
            m_ready.wait(pe, i, 1)
            py_written.sig(turned(py, m))

        def router_logits(i):
            mT_ready.wait(pe, i, 1)
            for t in range(NS):
                for c in range(NC):
                    last = t_.matmul(py[:, t * E:(t + 1) * E], mT[:, c, t * P:(t + 1) * P], wg[:, c, :], start=(c == 0), stop=(c == NC - 1))
            py_written.sig(last)

        def image_round(i, a_=True, b_=True, c_=True):
            if a_:
                splat_tokens(i + 1)
            if c_:
                output_projection(i - 1, 0)
            if b_:
                keep_clock(FILL[3])
                first_stacks(i)
            if a_:
                splat_products(i + 1)
            if b_:
                first_scores(i, range(0, 2))
            if c_:
                output_projection(i - 1, 1)
            if b_:
                first_scores(i, range(2, 5))
            if a_:
                splat_sums(i + 1)
            if b_:
                first_scores(i, range(5, 8))
                values(i)
            if a_:
                splat_states(i + 1)
            if b_:
                keep_clock(FILL[1])
                maximum_rows(i)
                keep_clock(FILL[2])
            if a_:
                splat_output(i + 1)
            if b_:
                second_stacks(i)
                keep_clock(FILL[4])
                attention(i, range(0, 6))
            if a_:
                attention_input(i + 1)
            if b_:
                attention(i, range(6, 8))
            if c_:
                router_tokens(i - 1)
            if b_:
                context(i, 6)
                context(i, 7)
            if a_:
                projections(i + 1)
            if c_:
                router_logits(i - 1)

        splat_tokens(0)
        splat_products(0)
        splat_sums(0)
        splat_states(0)
        splat_output(0)
        attention_input(0)
        projections(0)
        run_images(pe, image_round)
        py_written.wait(pe, B - 1, 3)
        pe.sem_inc(img_done_pe, 1)
        for c in (hot_used, xT_psum, up_done, down_done):
            c.open(pe)
        pe.wait_ge(tri_ready, 1)
        pe.wait_ge(r_dve, ROUTE_MASKS)
        t_.matmul(px[:, 0:NTL * E], tri[:], cmask, start=True, stop=True)
        t_.matmul(py[:, 0:NTL * E], ones[:], cmask, start=True, stop=True).then_inc(r_pe, 1)
        pe.wait_ge(r_dve, ROUTE_RANKS)
        t_.matmul(px[:, 0:2 * NCOL], zero16[:, 0:P], zero16[:, 0:2 * NCOL], start=True, stop=False)
        with pe.Fori(0, 2 * NTL // 8) as r:
            for half in range(2):
                hot_ready.wait(pe, r, half + 1)
                for n in range(4 * half, 4 * half + 4):
                    last = t_.matmul(px[:, 0:2 * NCOL], hotb[:, n, :], hota[:, n].rearrange("p v a -> p (v a)"), start=False, stop=False)
                hot_used.sig(last)
        t_.matmul(px[:, 0:2 * NCOL], zero16[:, 0:P], zero16[:, 0:2 * NCOL], start=False, stop=True).then_inc(r_pe, 1)

        pe.wait_ge(route_done, 1)

        def turn(j):
            x_in.wait(pe, j, 2)
            for c in range(NC):
                for t in range(2):
                    o = slice(c * 128 + t * 64, c * 128 + (t + 1) * 64)
                    t_.transpose(px[:, o].bitcast(F16), xg[:, t, c * P:(c + 1) * P], ident16[:])
                    last = t_.transpose(py[:, o].bitcast(BF16), xg[:, t, D + c * P:D + (c + 1) * P].bitcast(BF16), ident_bf[:])
            xT_psum.sig(last)

        def up(j, e):
            xT_hi_ready.wait(pe, j, 1)
            xT_lo_ready.wait(pe, j, 1)
            for half in range(2):
                gelu_done.wait_before(pe, j, half + 1)
                for k in range(FC // 2):
                    f = half * (FC // 2) + k
                    dst = big[:, half, k * TT:(k + 1) * TT]
                    for n, (w, x) in enumerate(((w1hi, xT_hi), (w1hi, xT_lo), (w1lo, xT_hi))):
                        for c in range(NC):
                            last = t_.matmul(dst, w[:, bass.ds(e * (NC * F) + (c * F + f * P), P)], x[:, c, :],
                                             start=(n == 0 and c == 0), stop=(n == 2 and c == NC - 1))
                up_done.sig(last)

        def down(j, e):
            y_ready.wait_before(pe, j, 1)
            split_done.wait(pe, j, 2)
            for t in range(2):
                for f in range(FC):
                    for n, (x, w) in enumerate(((h_hi, w2hi), (h_hi, w2lo), (h_lo, w2hi))):
                        last = t_.matmul(acc[:, 2 * t, :], x[:, f, t * P:(t + 1) * P], w[:, bass.ds(e * (FC * D) + f * D, D)],
                                         start=(f == 0 and n == 0), stop=(f == FC - 1 and n == 2))
            down_done.sig(last)

        turn(0)
        up(0, expert(pe, 0))
        turn(1)
        with pe.Fori(0, NT - 2) as j:
            up(j + 1, expert(pe, j + 1))
            turn(j + 2)
            down(j, expert(pe, j))
        up(NT - 1, expert(pe, NT - 1))
        down(NT - 2, expert(pe, NT - 2))
        down(NT - 1, expert(pe, NT - 1))


def kernel(**inputs):
    import numpy as np
    import concourse.bacc as bacc
    from concourse.bass_utils import run_bass_kernel_spmd

    nc = bacc.Bacc("TRN2", target_bir_lowering=False, num_devices=1)
    arrays, aps = {}, {}
    for name, value in inputs.items():
        arr = np.ascontiguousarray(value)
        arrays[f"in_{name}"] = arr
        aps[name] = nc.dram_tensor(f"in_{name}", arr.shape, mybir.dt.from_np(arr.dtype), kind="ExternalInput").ap()
    out = nc.dram_tensor("out_0", (B, S, D), F32, kind="ExternalOutput").ap()
    tower(nc, aps, out)
    r = run_bass_kernel_spmd(nc, [arrays], core_ids=[0])
    return r.results[0]["out_0"]
```

```python
from contextlib import ExitStack

import concourse.bass as bass
from concourse import mybir

ALU = mybir.AluOpType
ACT = mybir.ActivationFunctionType
F32 = mybir.dt.float32
F16 = mybir.dt.float16
BF16 = mybir.dt.bfloat16
I32 = mybir.dt.int32
U32 = mybir.dt.uint32
AX = mybir.AxisListType

P = 128
B = 16
S = 256
D = 256
T = B * S
H, DH = 16, 16
K = 16
E, F = 8, 1024
NC = D // P
NS = S // P
FC = F // P
TT = 256
NT = 2 * T // TT + E - 1
NSLOT = NT * TT
NCOL = NSLOT // P
EPS = 1e-5
WS = 64.0

G4 = 4
NG = B // G4
RB = P // G4
RROWS = S // RB


class Count:

    def __init__(self, sem, per, unit=1, opened=True):
        self.sem, self.per, self.unit, self.opened = sem, per, unit, opened

    def open(self, eng):
        eng.sem_inc(self.sem, self.per * self.unit)

    def sig(self, ins):
        ins.then_inc(self.sem, self.unit)

    def wait(self, eng, i, n, alone=None):
        self.await_(eng, (i + self.opened) * (self.per * self.unit) + n * self.unit, alone)

    def wait_before(self, eng, i, n, alone=None):
        self.await_(eng, i * (self.per * self.unit) + n * self.unit, alone)

    def await_(self, eng, value, alone):
        eng.wait_ge(self.sem, value)
        if alone:
            eng.sem_inc(alone, 1)


class Chain:

    def __init__(self, sem, per):
        self.c, self.n = Count(sem, per), 0

    def start(self, eng, i):
        self.eng, self.i, self.n = eng, i, 0

    def link(self, ins, alone=None):
        self.n += 1
        self.c.sig(ins)
        self.c.wait(self.eng, self.i, self.n, alone)

    def end(self):
        assert self.n == self.c.per, (self.n, self.c.per)


def tower(nc, a, out):
    with ExitStack() as ctx:
        build(nc, ctx, a, out)


def build(nc, ctx, a, out):
    def sb(name, shape, dt=F32):
        return ctx.enter_context(nc.sbuf_tensor(name, shape, dt))

    def sem(name):
        return ctx.enter_context(nc.semaphore(name))

    def dram(name, shape, dt):
        return nc.dram_tensor(name, shape, dt).ap()

    rec_dram = dram("rec_rows", [T, D], F32)
    h2_dram = dram("h2_rows", [T, D], F32)
    x4_dram = dram("x4_rows", [T, D], F32)
    m_dram = dram("m_rows", [T, 2 * D], F16)
    y_dram = dram("y_rows", [2 * T + NSLOT, D], F32)

    big = ctx.enter_context(nc.psum_tensor("big", [P, 2, 1024], F32))
    acc = ctx.enter_context(nc.psum_tensor("acc", [P, 4, 256], F32))
    px = ctx.enter_context(nc.psum_tensor("px", [P, 512], F32))
    py = ctx.enter_context(nc.psum_tensor("py", [P, 512], F32))

    expert_w = sb("expert_w", [P, 4, E * NC * F], F16)
    w1hi = expert_w[:, 0, :]
    w1lo = expert_w[:, 1, :].bitcast(BF16)
    w2hi = expert_w[:, 2, :]
    w2lo = expert_w[:, 3, :].bitcast(BF16)
    arena1 = expert_w[:, :, :].rearrange("p a b -> p (a b)").bitcast(F32)
    used = [0]

    def a1(n):
        used[0] += n
        assert used[0] <= 2 * E * NC * F
        return arena1[:, used[0] - n:used[0]]

    X = RROWS * D
    xin = a1(X)
    rec = a1(X)
    col_s, col_d = a1(X // 2), a1(X // 2)
    det = {1: a1(3 * X // 4), 2: a1(3 * X // 16), 3: a1(3 * X // 64)}
    app = {1: a1(X // 4), 2: a1(X // 16), 3: a1(X // 64)}
    wdet = {1: a1(9 * X // 4), 2: a1(9 * X // 16), 3: a1(9 * X // 64)}
    wapp = a1(X // 64)
    junk = a1(3 * X // 4)
    product = a1(3 * X // 4)
    part = a1(10)
    bias10, rscale = a1(10), a1(10)
    z10, e10, w10, nw10 = a1(10), a1(10), a1(10), a1(10)
    s3, r3 = a1(3), a1(3)

    NWORK = 13936
    work = sb("work", [P, NWORK])
    at = [0]

    def wk(n):
        at[0] += n
        assert at[0] <= NWORK, at[0]
        return work[:, at[0] - n:at[0]]

    v3 = lambda t, n: t.rearrange("p (a b) -> p a b", a=n)
    h_t = v3(wk(512), 2)
    t0 = v3(wk(512), 2)
    t0T = v3(wk(512), 2)
    h2 = v3(wk(512), 2)
    x3 = wk(1024)
    hhT = v3(wk(512), 2)
    qst = v3(wk(1024).bitcast(F16), 8)
    kst = v3(wk(1024).bitcast(F16), 8)
    vext = wk(1024).rearrange("p (c h e) -> p c h e", c=NS, h=H)
    pt = wk(2048).rearrange("p (b r c q) -> p b r c q", b=2, r=2, c=NS)
    qk_hi = pt[:, 0].rearrange("p r c q -> p (r c q)")[:, 0:512].bitcast(F16)
    qk_lo = pt[:, 0].rearrange("p r c q -> p (r c q)")[:, 512:1024].bitcast(F16)
    ctxn_w = wk(1024)
    ctxn = v3(ctxn_w[:, 0:512], 2)
    probs = [pt[:, 0], pt[:, 1], ctxn_w.rearrange("p (r c q) -> p r c q", r=2, c=NS)]
    at_x4 = at[0]
    x4 = v3(wk(512), 2)
    m = v3(wk(512), 2)
    mhl = v3(wk(512).bitcast(F16), 2)
    mT = v3(wk(512), 2)
    cturns = [t0T.rearrange("p a b -> p (a b)"), pt[:, 1].rearrange("p r c q -> p (r c q)")[:, 0:512]]
    wraw = wk(1024)
    st = wk(12).rearrange("p (t n) -> p t n", t=NS)
    mv = wk(4).rearrange("p (t n) -> p t n", t=NS)
    var, rstd = wk(2), wk(2)
    stc = wk(12).rearrange("p (t n) -> p t n", t=NS)
    mvc = wk(4).rearrange("p (t n) -> p t n", t=NS)
    varc, rstdc = wk(2), wk(2)
    tsq, affsum, affrec = wk(2), wk(2), wk(2)
    dist = v3(wk(32), 2)
    aff = v3(wk(32), 2)
    ut = v3(wk(32), 2)
    packs = [wk(256), wk(256)]
    affT, zs = packs[0][0:K, :], packs[1][0:K, :]
    sqj = v3(wk(256).bitcast(BF16), 2)
    mx = v3(wk(32), 2)
    neghl = v3(wk(32).bitcast(F16), 2)
    negmT = wk(128).bitcast(F16)[0:32, :]

    ident = sb("ident", [P, P])
    ident16 = sb("ident16", [P, P], F16)
    blk = sb("blk", [P, P])
    ones = sb("ones", [P, P])
    tri = sb("tri", [P, P])
    halfneg = sb("halfneg", [P, 2])
    kone = sb("kone", [P, 1])
    wscale = sb("wscale", [P, 1])
    sel = sb("sel", [P, 4, 4, 128], F16)
    selm = sb("selm", [32, 8, 2, 64], F16)
    csq_b = sb("csq_b", [P, 2, K])
    mats = sb("mats", [P, 2560])
    wq, wk_, wv = (v3(mats[:, n * 512:(n + 1) * 512], NC) for n in range(3))
    wop = v3(mats[:, 1536:2048], 2)
    wvo = v3(mats[:, 2048:2560], NC)
    g1, b1 = sb("g1", [P, NC]), sb("b1ln", [P, NC])
    g2b, b2b = sb("g2b", [P, D]), sb("b2b", [P, D])
    wg = sb("wg", [P, NC, E])
    cT = sb("cT", [P, NC, K])
    lall = sb("lall", [P, 2 * B, E])

    at[0] = 0
    b2e = wk(E * D)
    b1e = wk(E * FC)
    rt = lambda n: wk(n)
    NTL = 2 * B
    te3 = lambda t: t.rearrange("p (t e) -> p t e", e=E)
    mask1, mask2, cmask, cand, lrest, ra, rb_, rank = (rt(NTL * E) for _ in range(8))
    mx1, mx2, pick = rt(NTL), rt(NTL), rt(NTL)
    wts = sb("wts", [P, 2, NTL])
    pos = rt(2 * NTL)
    pos_i, posa_i, posb_i = (rt(2 * NTL).bitcast(I32) for _ in range(3))
    posa, posb = rt(2 * NTL), rt(2 * NTL)
    ntile, tbase, tend = rt(E), rt(E), rt(E)
    cmp = rt(E * 16)
    tcmp = rt(NT * E)
    tef = rt(NT)
    iota_i = rt(P).bitcast(I32)
    iota_f = rt(P)
    iota_h = rt(P // 2).bitcast(F16)
    iota_p = rt(1)
    iota_pi = rt(1).bitcast(I32)
    jstep = rt(16)
    slot_i = rt(NCOL).bitcast(I32)
    slot_f = rt(NCOL)
    HB = 8
    hotb = rt(HB * P).bitcast(F16).rearrange("p (u n b) -> p u n b", u=2, n=HB)
    hot1 = rt(HB * NCOL).bitcast(F16).rearrange("p (u n a) -> p u n a", u=2, n=HB)
    hota = rt(2 * HB * NCOL).bitcast(F16).rearrange("p (u n v a) -> p u n v a", u=2, n=HB, v=2)
    zero16 = rt(P).bitcast(F16)
    cols1 = rt(2 * NTL)
    minus_p = rt(NCOL)
    tok, emp, dest = rt(NCOL), rt(NCOL), rt(NCOL)
    tex = sb("tex", [1, NT], I32)
    src_idx, dst_idx = sb("src_idx", [P, NCOL], U32), sb("dst_idx", [P, NCOL], U32)
    gidx, sidx = sb("gidx", [P, 2], U32), sb("sidx", [P, 2], U32)
    assert at[0] <= at_x4
    at[0] = E * D + E * FC
    xg = v3(wk(512).bitcast(F16), 2)
    xT_hi = v3(wk(256).bitcast(F16), 2)
    xT_lo = v3(wk(256).bitcast(BF16), 2)
    hf = v3(wk(2048), FC)
    h_hi = v3(wk(1024).bitcast(F16), FC)
    h_lo = v3(wk(1024).bitcast(BF16), FC)
    ys = v3(wk(512), 2)
    NRA = (NWORK - at[0]) // D // 8 * 8
    NRB = 2 * B - NRA
    res_a, res_b = wk(NRA * D), mats[:, 0:NRB * D]
    res_h2 = mats[:, NRB * D:(NRB + 1) * D]
    at[0] = 0
    CK = 4
    yb = [[v3(wk(512), 2) for _ in range(2)] for _ in range(CK)]
    ident_bf = sb("ident_bf", [P, P], BF16)

    img = lambda d: d.rearrange("(i t p) d -> i p t d", t=NS, p=P)

    passed_dve, passed_pool, passed_sp = sem("passed_dve"), sem("passed_pool"), sem("passed_sp")

    const_ld, const_pool, const_dve = sem("const_ld"), sem("const_pool"), sem("const_dve")
    prep_pe, prep_dve, prep_act = sem("prep_pe"), sem("prep_dve"), sem("prep_act")
    dwt_w_ld = sem("dwt_w_ld")

    x_ld = Count(sem("x_ld"), 1, 16)
    dwt_chain = Chain(sem("dwt_chain"), 31)
    product_ready, product_sum = Count(sem("product_ready"), 1), Count(sem("product_sum"), 1)
    part_ready = Count(sem("part_ready"), 1)
    part_sum = Count(sem("part_sum"), 1)
    dwt_logits = Count(sem("dwt_logits"), 1)
    band_logit = Count(sem("band_logit"), 1)
    band_exp = Count(sem("band_exp"), 2)
    rec_ready = Count(sem("rec_ready"), 1)
    rec_stored = Count(sem("rec_stored"), 1, 16)

    C = {}

    def cnt(name, per=1, unit=1):
        C[name] = Count(sem(name), per, unit)
        return C[name]

    h_ld = cnt("h_ld", 1, 16)
    var_a, rstd_a = cnt("var_a", 3), cnt("rstd_a", 3)
    t0_ready, tsq_ready = cnt("t0_ready"), cnt("tsq_ready")
    px_written = cnt("px_written", 6)
    t0T_ready, dist_ready, aff_exp = cnt("t0T_ready"), cnt("dist_ready"), cnt("aff_exp")
    aff_ready, ut_ready, z_ready = cnt("aff_ready"), cnt("ut_ready"), cnt("z_ready")
    h2_ready, h2_stored = cnt("h2_ready"), cnt("h2_stored", 1, 16)
    hn_ready, hhT_ready = cnt("hn_ready"), cnt("hhT_ready")
    big_written = cnt("big_written", 22)
    k_projected, k_hi, k_lo, q_hi = cnt("k_projected"), cnt("k_hi"), cnt("k_lo"), cnt("q_hi")
    big_act = cnt("big_act", 11)
    big_dve = cnt("big_dve", 11)
    k_in_acc, k_taken = cnt("k_in_acc"), cnt("k_taken")
    v_in_acc, v_taken = cnt("v_in_acc"), cnt("v_taken")
    negm_ready, negmT_psum, negmT_ready = cnt("negm_ready"), cnt("negmT_psum"), cnt("negmT_ready")
    pv_done, ctx_ready = cnt("pv_done", 8), cnt("ctx_ready")
    py_written = cnt("py_written", 3)
    x4_ready, x4_stored = cnt("x4_ready"), cnt("x4_stored", 1, 16)
    var_c, rstd_c, m0_ready, m_ready = cnt("var_c"), cnt("rstd_c"), cnt("m0_ready"), cnt("m_ready")
    mhl_ready, mhl_stored = cnt("mhl_ready"), cnt("mhl_stored", 1, 16)
    mT_ready, logit_read = cnt("mT_ready"), cnt("logit_read")
    w_ld, w_hi, w_lo = cnt("w_ld", 2, 16), cnt("w_hi", 4), cnt("w_lo", 2)
    dve_a, dve_b, dve_c = Chain(sem("dve_a"), 12), Chain(sem("dve_b"), 1), Chain(sem("dve_c"), 2)
    dve_ctx = Chain(sem("dve_ctx"), 7)
    pool_c = Chain(sem("pool_c"), 2)

    READER = ["D", "A", "A", "D"] + ["D"] * 8 + ["A", "D"] + ["A"] * 8
    FIRST, SECOND = 4, 14
    order = [READER[:u].count(READER[u]) + 1 for u in range(len(READER))]
    assert len(READER) == 22 and READER.count("A") == 11

    def slot_free(i, u):
        before = C["big_act"] if READER[u - 2] == "A" else C["big_dve"]
        (before.wait if u >= 2 else before.wait_before)(nc.tensor, i, order[u - 2])

    tri_ready = sem("tri_ready")
    ROUTE_RANKS = 45
    img_done_act, img_done_pe = sem("img_done_act"), sem("img_done_pe")
    r_dve, r_pool, r_act, r_pe, r_ld = sem("r_dve"), sem("r_pool"), sem("r_act"), sem("r_pe"), sem("r_ld")
    hot_ready, hot_cols = Count(sem("hot_ready"), 2), Count(sem("hot_cols"), 2)
    hot_rows, hot_used = Count(sem("hot_rows"), 2), Count(sem("hot_used"), 2)
    route_done = sem("route_done")
    x_in = Count(sem("x_in"), 2, 16, opened=False)
    xT_psum, xT_hi_ready, xT_lo_ready = Count(sem("xT_psum"), 1), Count(sem("xT_hi_ready"), 1), Count(sem("xT_lo_ready"), 1)
    up_done, gelu_done, split_done = Count(sem("up_done"), 2), Count(sem("gelu_done"), 2), Count(sem("split_done"), 2)
    hi_chain = Count(sem("hi_chain"), 2)
    down_done, y_ready = Count(sem("down_done"), 1), Count(sem("y_ready"), 1)
    y_out = Count(sem("y_out"), 2, 16, opened=False)
    y_free = Count(sem("y_free"), 1)
    src_ready, dst_ready = Count(sem("src_ready"), 1), Count(sem("dst_ready"), 1)
    res_in, res_done = Count(sem("res_in"), 2, 16), Count(sem("res_done"), 1)
    c_in = [Count(sem(f"c_in{k}"), 2, 16) for k in range(CK)]
    c_mid, c_done = Count(sem("c_mid"), CK), Count(sem("c_done"), CK)
    c_out = sem("c_out")
    ROUTE_MASKS = 15

    def expert(eng, j):
        return eng.value_load(tex[0:1, bass.ds(j, 1)], min_val=0, max_val=E - 1)

    def run_images(eng, image_round):
        image_round(0, c_=False)
        with eng.Fori(1, B - 1) as i:
            image_round(i)
        image_round(B - 1, a_=False)
        image_round(B, a_=False, b_=False)

    def run_images_late(eng, image_round):
        image_round(0, c_=False, m_=False)
        image_round(1, m_=False)
        with eng.Fori(2, B - 1) as i:
            image_round(i)
        image_round(B - 1, a_=False)
        image_round(B, a_=False, b_=False)
        image_round(B + 1, a_=False, b_=False, c_=False)

    block = ctx.enter_context(nc.Block())

    @block.sync
    def _(sp):
        for c in (x_ld, rec_stored, h_ld, h2_stored, x4_stored, mhl_stored, w_ld):
            c.open(sp)
        xg = a["x"].rearrange("(g b) (r h) w o -> g (b r) (h w o)", b=G4, r=RB)
        rg = rec_dram.rearrange("(g p h) d -> g p (h d)", g=NG, h=RROWS)

        def load_x(g):
            sp.dma_start(xin, xg[g]).then_inc(x_ld.sem, 16)

        def store_rec(g):
            rec_ready.wait(sp, g, 1, alone=passed_sp)
            sp.dma_start(rg[g], rec).then_inc(rec_stored.sem, 16)

        load_x(0)
        for lv, name, n in ((3, "L0_tok_Wd1", X // 64), (2, "L0_tok_Wd2", X // 16), (1, "L0_tok_Wd3", X // 4)):
            src = a[name].rearrange("(b r n) o -> r b (n o)", b=3, r=RB)
            dst = wdet[lv].rearrange("p (b n) -> p b n", b=3)
            for q in range(G4):
                sp.dma_start(dst[RB * q:RB * (q + 1)], src).then_inc(dwt_w_ld, 16)
        for q in range(G4):
            sp.dma_start(wapp[RB * q:RB * (q + 1)], a["L0_tok_Wa"].rearrange("(r n) o -> r (n o)", r=RB)).then_inc(dwt_w_ld, 16)
        for k, name in enumerate(("L0_tok_ba", "L0_tok_bd1", "L0_tok_bd2", "L0_tok_bd3")):
            dst = bias10[:, 0:1] if k == 0 else bias10[:, 3 * k - 2:3 * k + 1]
            sp.dma_start(dst, a[name].partition_broadcast(P)).then_inc(dwt_w_ld, 16)
        with sp.Fori(0, NG - 1) as g:
            dwt_chain.c.wait(sp, g, 1, alone=passed_sp)
            load_x(g + 1)
            store_rec(g)
        sp.wait_ge(prep_pe, 1)
        rec_stored.wait(sp, 0, 1)
        sp.dma_start(h_t, img(rec_dram)[0]).then_inc(h_ld.sem, 16)
        store_rec(NG - 1)
        rec_stored.wait(sp, NG - 1, 1)
        w1v = a["L0_ffn_W1"].rearrange("e (c p) f -> (e c) p f", p=P)
        w2v = a["L0_ffn_W2"].rearrange("e (n q p) d -> (e n) p q d", n=2, p=P)
        def store_h2(i):
            h2_ready.wait(sp, i, 1, alone=passed_sp)
            sp.dma_start(img(h2_dram)[i], h2).then_inc(h2_stored.sem, 16)

        def store_mhl(i):
            mhl_ready.wait(sp, i, 1, alone=passed_sp)
            sp.dma_start(img(m_dram)[i], mhl).then_inc(mhl_stored.sem, 16)

        def image_round(i, a_=True, b_=True, c_=True, m_=True):
            if a_:
                h2_ready.wait(sp, i, 1, alone=passed_sp)
                sp.dma_start(h_t, img(rec_dram)[i + 1]).then_inc(h_ld.sem, 16)
            if b_:
                w_lo.wait_before(sp, i, 2, alone=passed_sp)
                sp.dma_start(wraw, w1v[i]).then_inc(w_ld.sem, 16)
            if m_:
                store_mhl(i - 2)
            if b_:
                w_lo.wait(sp, i, 1, alone=passed_sp)
                sp.dma_start(wraw.rearrange("p (q d) -> p q d", q=4), w2v[i]).then_inc(w_ld.sem, 16)
            if c_:
                x4_ready.wait(sp, i - 1, 1, alone=passed_sp)
                sp.dma_start(img(x4_dram)[i - 1], x4).then_inc(x4_stored.sem, 16)
            if a_:
                store_h2(i + 1)

        store_h2(0)
        run_images_late(sp, image_round)
        for c in (*c_in, y_free, res_in):
            c.open(sp)
        sp.wait_ge(img_done_pe, 1)
        sp.wait_ge(img_done_act, 1)
        m0_ready.wait(sp, B - 1, 1)
        sp.dma_start(b2e, a["L0_ffn_b2"].rearrange("e d -> (e d)").partition_broadcast(P)).then_inc(r_ld, 16)
        sp.dma_start(b1e.rearrange("p (e c) -> p e c", e=E), a["L0_ffn_b1"].rearrange("e (c p) -> p e c", p=P),
                     allow_slow_non_contiguous=True).then_inc(r_ld, 16)
        for c in (h2_stored, x4_stored, mhl_stored):
            c.wait(sp, B - 1, 1)
        sp.wait_ge(route_done, 1)
        h2v, x4v = (d.rearrange("(j p) d -> j p d", p=P) for d in (h2_dram, x4_dram))

        def load_residual(j, region, first):
            res_done.wait_before(sp, j, 1, alone=passed_sp)
            sp.dma_start(res_h2, h2v[j]).then_inc(res_in.sem, 16)
            sp.dma_start(region[:, bass.ds((j - first) * D, D)], x4v[j]).then_inc(res_in.sem, 16)

        def rows_stored(j):
            y_out.wait(sp, j, 2)
            sp.sem_inc(y_free.sem, 1)

        with sp.Fori(0, NRA) as j:
            load_residual(j, res_a, 0)
            rows_stored(j)
        with sp.Fori(NRA, 2 * B) as j:
            load_residual(j, res_b, NRA)
            rows_stored(j)
        with sp.Fori(2 * B, NT) as j:
            rows_stored(j)
        yv = [img(y_dram[0:T]), img(y_dram[T:2 * T])]
        outv = img(out.rearrange("i s d -> (i s) d"))

        def load_rows(r, k):
            for n in range(2):
                sp.dma_start(yb[k][n], yv[n][r * CK + k]).then_inc(c_in[k].sem, 16)

        def store_out(r, k, region, first):
            c_done.wait(sp, r, k + 1, alone=passed_sp)
            rows = region[:, bass.ds((r * (2 * CK) + 2 * k - first) * D, NS * D)]
            sp.dma_start(outv[r * CK + k], v3(rows, NS)).then_inc(c_out, 16)

        for k in range(CK):
            load_rows(0, k)
        with sp.Fori(0, NRA // (2 * CK)) as r:
            for k in range(CK):
                store_out(r, k, res_a, 0)
                load_rows(r + 1, k)
        for k in range(CK):
            store_out(B // CK - 1, k, res_b, NRA)
        sp.wait_ge(c_out, 16 * B)

    @block.gpsimd
    def _(pool):
        g = nc.gpsimd
        for c in (rstd_a, rstd_c, m_ready, mhl_ready, pool_c.c, w_hi, w_lo, product_ready):
            c.open(pool)
        g.memset(ident[:], 0.0).then_inc(const_pool, 1)
        g.memset(blk[:], 0.0).then_inc(const_pool, 1)
        g.memset(ones[:], 1.0).then_inc(const_pool, 1)
        g.memset(halfneg[:], -0.5).then_inc(const_pool, 1)
        g.memset(vext, 1.0).then_inc(const_pool, 1)
        g.memset(sel[:], 0.0).then_inc(const_pool, 1)
        g.memset(selm[:], 0.0).then_inc(const_pool, 1)
        g.memset(wscale[:], WS).then_inc(const_pool, 1)
        pool.wait_ge(const_pool, 8)
        g.affine_select(out=ident[:], in_=ident[:], compare_op=ALU.not_equal, fill=1.0, base=0,
                        pattern=[[-1, P]], channel_multiplier=1).then_inc(const_pool, 1)
        pool.wait_ge(const_pool, 9)
        g.affine_select(out=tri[:], in_=ones[:], compare_op=ALU.is_gt, fill=0.0, base=0,
                        pattern=[[1, P]], channel_multiplier=-1).then_inc(tri_ready, 1)
        pool.wait_ge(tri_ready, 1)
        for q in range(G4):
            g.memset(blk[RB * q:RB * (q + 1), RB * q:RB * (q + 1)], 1.0).then_inc(const_pool, 1)
        pool.wait_ge(const_pool, 9 + G4)
        n = 0
        for dst, src in (
            (wq[:], a["L0_ffn_Wq"].rearrange("(c p) n -> p c n", p=P)),
            (wk_[:], a["L0_ffn_Wk"].rearrange("(c p) n -> p c n", p=P)),
            (wv[:], a["L0_ffn_Wv"].rearrange("(c p) n -> p c n", p=P)),
            (wg[:], a["L0_ffn_Wg"].rearrange("(c p) n -> p c n", p=P)),
            (h_t, a["L0_attn_W_v"].rearrange("(c p) n -> p c n", p=P)),
            (t0, a["L0_attn_W_o"].rearrange("(c p) n -> p c n", p=P)),
            (zs, a["L0_attn_splat_centers"]),
            (affT[:, 0:1], a["L0_attn_splat_log_scales"].rearrange("(k o) -> k o", o=1)),
            (g1[:], a["L0_ffn_ln1_g"].rearrange("(c p) -> p c", p=P)),
            (b1[:], a["L0_ffn_ln1_b"].rearrange("(c p) -> p c", p=P)),
            (g2b[:], a["L0_ffn_ln2_g"].partition_broadcast(P)),
            (b2b[:], a["L0_ffn_ln2_b"].partition_broadcast(P)),
        ):
            pool.dma_start(dst, src, allow_slow_non_contiguous=True).then_inc(const_ld, 16)
            n += 1
        wo_rows = a["L0_ffn_Wo"].rearrange("(n e j d) w -> j e d n w", n=2, e=2, j=4)
        for j in range(4):
            for e in range(2):
                row = 32 * j + DH * e
                pool.dma_start(wop[row:row + DH], wo_rows[j, e]).then_inc(const_ld, 16)
                n += 1
        assert n == 20

        def inv_std(i, ln):
            var_a.wait(pool, i, ln + 1)
            g.tensor_tensor(rstd, var, halfneg[:], ALU.pow).then_inc(rstd_a.sem, 1)

        def expert_inputs(i):
            var_c.wait(pool, i, 1)
            g.tensor_tensor(rstdc, varc, halfneg[:], ALU.pow).then_inc(rstd_c.sem, 1)
            pool_c.start(pool, i)
            m0_ready.wait(pool, i, 1)
            pool_c.link(g.tensor_tensor(m, m, g2b[:].unsqueeze(1).broadcast_to([P, NS, D]), ALU.mult))
            g.tensor_tensor(m, m, b2b[:].unsqueeze(1).broadcast_to([P, NS, D]), ALU.add).then_inc(m_ready.sem, 1)
            m_ready.wait(pool, i, 1)
            mhl_stored.wait_before(pool, i, 1, alone=passed_pool)
            pool_c.link(g.tensor_copy(mhl[:, :, 0:D], m))
            g.tensor_tensor(mhl[:, :, D:2 * D].bitcast(BF16), m, mhl[:, :, 0:D], ALU.subtract).then_inc(mhl_ready.sem, 1)
            pool_c.end()

        def weights(i, n, hi, lo):
            w_ld.wait(pool, i, n)
            part_ = bass.ds(i * 1024, 1024)
            g.tensor_tensor(wraw, wraw, wscale[:].broadcast_to([P, 1024]), ALU.mult).then_inc(w_hi.sem, 1)
            w_hi.wait(pool, i, 2 * n - 1, alone=passed_pool)
            g.tensor_copy(hi[:, part_], wraw).then_inc(w_hi.sem, 1)
            w_hi.wait(pool, i, 2 * n, alone=passed_pool)
            g.tensor_tensor(lo[:, part_], wraw, hi[:, part_], ALU.subtract).then_inc(w_lo.sem, 1)

        def image_round(i, a_=True, b_=True, c_=True):
            if a_:
                inv_std(i + 1, 0)
            if b_:
                weights(i, 1, w1hi, w1lo)
                weights(i, 2, w2hi, w2lo)
            if a_:
                inv_std(i + 1, 1)
                inv_std(i + 1, 2)
            if c_:
                expert_inputs(i - 1)

        pool.wait_ge(dwt_w_ld, 16 * (4 * G4 + 4))

        def band_product(g):
            dwt_chain.c.wait(pool, g, 2)
            product_sum.wait_before(pool, g, 1, alone=passed_pool)
            nc.gpsimd.tensor_tensor(product, det[1], wdet[1].rearrange("p (n o) -> p n o", o=3)[:, :, 2], ALU.mult).then_inc(product_ready.sem, 1)

        with pool.Fori(0, NG - 1) as group:
            band_product(group)
        band_product(NG - 1)
        for ln in range(3):
            inv_std(0, ln)
        rec_stored.wait(pool, NG - 1, 1)
        run_images(pool, image_round)
        pool.wait_ge(img_done_pe, 1)
        pool.wait_ge(img_done_act, 1)
        g.iota(iota_i, pattern=[[1, P]], base=0, channel_multiplier=0).then_inc(r_pool, 1)
        g.iota(iota_pi, pattern=[[0, 1]], base=0, channel_multiplier=1).then_inc(r_pool, 1)
        g.iota(slot_i, pattern=[[P, NCOL]], base=2 * T + P, channel_multiplier=1).then_inc(r_pool, 1)
        g.memset(zero16, 0.0).then_inc(r_pool, 1)
        for c in (src_ready, dst_ready, hot_cols):
            c.open(pool)
        with pool.Fori(0, 2 * NTL // (2 * HB)) as r:
            for u in range(2):
                hot_ready.wait(pool, r, u + 1, alone=passed_pool)
                g.tensor_tensor(hota[:, u, :, 1, :], hot1[:, u], cols1[:, bass.ds((r * 2 + u) * HB, HB)].unsqueeze(2).broadcast_to([P, HB, NCOL]),
                                ALU.mult).then_inc(hot_cols.sem, 1)

        def gather(j):
            xT_psum.wait_before(pool, j, 1)
            g.tensor_copy(gidx[:], src_idx[:, bass.ds(j * 2, 2)]).then_inc(src_ready.sem, 1)
            src_ready.wait(pool, j, 1, alone=passed_pool)
            for t in range(2):
                g.indirect_dma_start(xg[:, t, :], None, m_dram, bass.IndirectOffsetOnAxis(ap=gidx[:, t:t + 1], axis=0)).then_inc(x_in.sem, 16)

        def scatter(j):
            y_ready.wait(pool, j, 1)
            g.tensor_copy(sidx[:], dst_idx[:, bass.ds(j * 2, 2)]).then_inc(dst_ready.sem, 1)
            dst_ready.wait(pool, j, 1, alone=passed_pool)
            for t in range(2):
                g.indirect_dma_start(y_dram, bass.IndirectOffsetOnAxis(ap=sidx[:, t:t + 1], axis=0), ys[:, t, :], None).then_inc(y_out.sem, 16)

        pool.wait_ge(route_done, 1)
        mhl_stored.wait(pool, B - 1, 1)
        for j in range(3):
            gather(j)
        res_done.open(pool)

        def residual(j, region, first):
            rows = region[:, bass.ds((j - first) * D, D)]
            res_in.wait(pool, j, 2, alone=passed_pool)
            g.tensor_tensor(rows, rows, res_h2, ALU.add).then_inc(res_done.sem, 1)

        with pool.Fori(0, NRA) as j:
            gather(j + 3)
            residual(j, res_a, 0)
            scatter(j)
        with pool.Fori(NRA, 2 * B) as j:
            gather(j + 3)
            residual(j, res_b, NRA)
            scatter(j)
        with pool.Fori(2 * B, NT - 3) as j:
            gather(j + 3)
            scatter(j)
        for j in range(NT - 3, NT):
            scatter(j)

    @block.scalar
    def _(act):
        s = nc.scalar
        for c in (product_sum, v_taken, band_exp, tsq_ready, t0T_ready, aff_exp, ut_ready, z_ready, hhT_ready, k_hi, q_hi, big_act,
                  negmT_ready, mT_ready, logit_read):
            c.open(act)
        act.wait_ge(const_ld, 16 * 20)
        s.activation(affT[:, 1:2], affT[:, 0:1], ACT.Exp).then_inc(prep_act, 1)
        s.activation(sqj[0:K, 0, :], zs, ACT.Square, accum_out=affT[:, 2:3]).then_inc(prep_act, 1)

        def band_exps(g):
            band_logit.wait(act, g, 1)
            s.activation(e10[:, 1:10], z10[:, 1:10], ACT.Exp).then_inc(band_exp.sem, 1)
            s.activation(e10[:, 0:1], z10[:, 0:1], ACT.Exp, scale=-1.0).then_inc(band_exp.sem, 1)

        def band_sum(g):
            product_ready.wait(act, g, 1)
            part_sum.wait_before(act, g, 1)
            s.activation(product, product, ACT.Copy, scale=0.5, accum_out=part[:, 9:10]).then_inc(product_sum.sem, 1)

        with act.Fori(0, NG - 1) as g:
            band_sum(g)
            band_exps(g)

        def token_squares(i):
            t0_ready.wait(act, i, 1)
            for t in range(NS):
                last = s.activation(sqj[:, t, :], t0[:, t, :], ACT.Square, accum_out=tsq[:, t:t + 1])
            tsq_ready.sig(last)

        def splat_tokens(i):
            px_written.wait(act, i, 1)
            s.copy(t0T.rearrange("p a b -> p (a b)"), px[:]).then_inc(t0T_ready.sem, 1)

        def splat_exp(i):
            dist_ready.wait(act, i, 1)
            s.activation(aff, dist, ACT.Exp).then_inc(aff_exp.sem, 1)

        def splat_sums(i):
            px_written.wait(act, i, 3)
            s.copy(ut, px[:, 0:32].rearrange("p (a b) -> p a b", a=2))
            s.copy(affT, px[0:K, 256:512]).then_inc(ut_ready.sem, 1)

        def splat_states(i):
            px_written.wait(act, i, 4)
            s.copy(zs, px[0:K, 0:256]).then_inc(z_ready.sem, 1)

        def attention_input(i):
            px_written.wait(act, i, 6)
            v_in_acc.wait_before(act, i, 1)
            for c in range(NC):
                last = s.activation(hhT[:, c, :], px[:, c * 256:(c + 1) * 256], ACT.Identity,
                                    bias=b1[:, c:c + 1], scale=g1[:, c:c + 1])
            hhT_ready.sig(last)

        def high_parts(i):
            k_projected.wait(act, i, 1)
            s.copy(qk_hi[:, 512:1024], big[:, 0, 512:1024]).then_inc(k_hi.sem, 1)
            big_written.wait(act, i, 1)
            s.copy(qk_hi[:, 0:512], big[:, 0, 0:512]).then_inc(q_hi.sem, 1)

        def first_stacks(i):
            big_written.wait(act, i, 2)
            s.activation(kst[:, 0:4].rearrange("p a b -> p (a b)"), big[:, 1, :], ACT.Identity, bias=kone[:, 0:1]).then_inc(big_act.sem, 1)
            big_written.wait(act, i, 3)
            s.copy(qst[:, 0:4].rearrange("p a b -> p (a b)"), big[:, 0, :]).then_inc(big_act.sem, 1)

        def values(i):
            v_in_acc.wait(act, i, 1)
            s.copy(vext[:, :, :, 0:DH], acc[:, 0:2, :].rearrange("p c (h e) -> p c h e", h=H)).then_inc(v_taken.sem, 1)

        def maximum_rows(i):
            negmT_psum.wait(act, i, 1)
            s.copy(negmT, acc[0:32, 0, 0:128].bitcast(F16)).then_inc(negmT_ready.sem, 1)

        def second_stack(i):
            big_written.wait(act, i, FIRST + 9)
            s.copy(qst[:, 0:4].rearrange("p a b -> p (a b)"), big[:, 0, :]).then_inc(big_act.sem, 1)

        def probabilities(i, u):
            big_written.wait(act, i, SECOND + 1 + u)
            if u < 3:
                pv_done.wait_before(act, i, 8)
            else:
                pv_done.wait(act, i, u - 2)
            s.activation(probs[u % 3].rearrange("p r c q -> p (r c q)"), big[:, u % 2, :], ACT.Exp,
                         scale=float(DH) ** -0.5).then_inc(big_act.sem, 1)

        def router_tokens(i):
            py_written.wait(act, i, 2)
            s.copy(mT.rearrange("p a b -> p (a b)"), py[:]).then_inc(mT_ready.sem, 1)

        def router_logits(i):
            py_written.wait(act, i, 3)
            s.copy(lall[:].rearrange("p t e -> p (t e)")[:, bass.ds(i * 2 * E, 2 * E)], py[:, 0:2 * E]).then_inc(logit_read.sem, 1)

        def image_round(i, a_=True, b_=True, c_=True, m_=True):
            if b_:
                first_stacks(i)
            if m_:
                router_logits(i - 2)
            if a_:
                token_squares(i + 1)
                splat_tokens(i + 1)
            if a_:
                splat_exp(i + 1)
            if b_:
                values(i)
            if a_:
                splat_sums(i + 1)
                splat_states(i + 1)
            if b_:
                maximum_rows(i)
                second_stack(i)
                for u in range(6):
                    probabilities(i, u)
            if a_:
                attention_input(i + 1)
            if b_:
                for u in (6, 7):
                    probabilities(i, u)
            if c_:
                router_tokens(i - 1)
            if a_:
                high_parts(i + 1)

        band_sum(NG - 1)
        token_squares(0)
        band_exps(NG - 1)
        splat_tokens(0)
        splat_exp(0)
        splat_sums(0)
        splat_states(0)
        attention_input(0)
        high_parts(0)
        run_images_late(act, image_round)
        logit_read.wait(act, B - 1, 1)
        act.sem_inc(img_done_act, 1)
        act.wait_ge(r_dve, ROUTE_MASKS)
        s.activation(wts[:, 1, :], mx2, ACT.Exp).then_inc(r_act, 1)
        hot_rows.open(act)
        with act.Fori(0, 2 * NTL // (2 * HB)) as r:
            for u in range(2):
                hot_ready.wait(act, r, u + 1)
                s.activation(hota[:, u, :, 0, :], hot1[:, u], ACT.Copy, scale=iota_p).then_inc(hot_rows.sem, 1)
        act.wait_ge(route_done, 1)
        for c in (xT_hi_ready, gelu_done):
            c.open(act)
        act.wait_ge(r_ld, 32)

        def rows_in(j):
            xT_psum.wait(act, j, 1)
            up_done.wait_before(act, j, 2)
            s.activation(xT_hi.rearrange("p a b -> p (a b)"), px[:, 0:256].bitcast(F16), ACT.Copy).then_inc(xT_hi_ready.sem, 1)

        def hidden_half(j, e, half):
            up_done.wait(act, j, half + 1)
            split_done.wait_before(act, j, half + 1)
            for k in range(FC // 2):
                f = half * (FC // 2) + k
                last = s.activation(hf[:, f, :], big[:, half, k * TT:(k + 1) * TT], ACT.Gelu_apprx_tanh,
                                    bias=b1e[:, bass.ds(e * FC + f, 1)], scale=1.0 / WS)
            gelu_done.sig(last)

        def hidden(j):
            e = expert(act, j)
            hidden_half(j, e, 0)
            hidden_half(j, e, 1)

        rows_in(0)
        hidden(0)
        rows_in(1)
        with act.Fori(0, NT - 2) as j:
            hidden(j + 1)
            rows_in(j + 2)
        hidden(NT - 1)

    @block.vector
    def _(dve):
        v = nc.vector
        for c in (dwt_chain.c, dwt_logits, part_ready, band_logit, rec_ready, var_a, t0_ready, dist_ready, aff_ready, h2_ready,
                  hn_ready, big_dve, k_taken, k_lo, negm_ready, ctx_ready, x4_ready, var_c, m0_ready, dve_a.c, dve_b.c, dve_c.c, dve_ctx.c):
            c.open(dve)
        steps = [0]

        def step(ins):
            steps[0] += 1
            ins.then_inc(prep_dve, 1)
            dve.wait_ge(prep_dve, steps[0])

        step(v.memset(rscale[:, 0:4], 1.0 / 64))
        step(v.memset(rscale[:, 4:7], 1.0 / 16))
        step(v.memset(rscale[:, 7:10], 1.0 / 4))
        dve.wait_ge(const_pool, 9 + G4)
        step(v.tensor_copy(ident16[:], ident[:]))
        src = ident16[:].rearrange("p (s r d) -> p s r d", s=4, r=2)
        stk = lambda n: sel[:, n].rearrange("p s (r b d) -> p s r b d", r=2, b=4)
        for n, b in ((0, 0), (0, 2), (1, 1), (2, 0), (2, 1), (3, 2)):
            for sl in range(4):
                step(v.tensor_copy(stk(n)[:, sl, :, b, :], src[:, sl]))
        for part_, base in ((0, 0), (1, 16)):
            step(v.tensor_copy(selm[:, :, :, 48 + part_], ident16[0:32, base:base + 16].rearrange("p (s r) -> p s r", r=2)))
        step(v.tensor_reduce(kone[:], ident[:].rearrange("p (r c) -> p r c", r=2)[:, :, 48:50], AX.XY, ALU.add))

        def haar_down(g):
            ch = dwt_chain
            ch.start(dve, g)
            rec_ready.wait_before(dve, g, 1)
            x_ld.wait(dve, g, 1)
            cur = xin
            n = X
            cols = D
            for lv in (1, 2, 3):
                q = n // 4
                xv = cur.rearrange("p (r two) -> p r two", two=2)
                v.tensor_tensor(col_s[:, 0:n // 2], xv[:, :, 0], xv[:, :, 1], ALU.add)
                ch.link(v.tensor_tensor(col_d[:, 0:n // 2], xv[:, :, 0], xv[:, :, 1], ALU.subtract))
                w = cols // 2
                sv = col_s[:, 0:n // 2].rearrange("p (r two c) -> p r two c", two=2, c=w)
                dv = col_d[:, 0:n // 2].rearrange("p (r two c) -> p r two c", two=2, c=w)
                o = lambda t: t.rearrange("p (r c) -> p r c", c=w)
                v.tensor_tensor(o(app[lv]), sv[:, :, 0], sv[:, :, 1], ALU.add)
                v.tensor_tensor(o(det[lv][:, 0:q]), sv[:, :, 0], sv[:, :, 1], ALU.subtract)
                v.tensor_tensor(o(det[lv][:, q:2 * q]), dv[:, :, 0], dv[:, :, 1], ALU.add)
                ch.link(v.tensor_tensor(o(det[lv][:, 2 * q:3 * q]), dv[:, :, 0], dv[:, :, 1], ALU.subtract))
                cur, n, cols = app[lv], q, w

        def band_dots(lv, k):
            n = 3 * X // 4 ** lv
            for o in range(3 if lv > 1 else 2):
                wv_o = wdet[lv].rearrange("p (n o) -> p n o", o=3)[:, :, o]
                ins = v.tensor_tensor_reduce(junk[:, 0:n], det[lv], wv_o, 0.5 ** lv, 0.0, ALU.mult, ALU.add,
                                             part[:, k + o:k + o + 1])
                if (k, o) == (7, 1):
                    part_ready.sig(ins)
                else:
                    dwt_chain.link(ins)

        def small_dots():
            dve.wait_ge(dwt_w_ld, 16 * (4 * G4 + 4))
            dwt_chain.link(v.tensor_tensor_reduce(junk[:, 0:X // 64], app[3], wapp, 0.125, 0.0, ALU.mult, ALU.add, part[:, 0:1]))
            band_dots(3, 1)
            band_dots(2, 4)

        def band_weights(g):
            ch = dwt_chain
            part_sum.wait(dve, g, 1)
            v.tensor_tensor(z10, px[:, 0:10], bias10, ALU.add).then_inc(dwt_logits.sem, 1)
            dwt_logits.wait(dve, g, 1)
            z3 = z10[:, 1:10].rearrange("p (l o) -> p l o", o=3)
            ch.link(v.tensor_reduce(s3, z3, AX.X, ALU.max))
            v.tensor_tensor(z3, z3, s3.unsqueeze(2).broadcast_to([P, 3, 3]), ALU.subtract).then_inc(band_logit.sem, 1)
            band_exp.wait(dve, g, 2)
            e3 = e10[:, 1:10].rearrange("p (l o) -> p l o", o=3)
            ch.link(v.tensor_reduce(s3, e3, AX.X, ALU.add))
            ch.link(v.reciprocal(r3, s3))
            ch.link(v.tensor_tensor(w10[:, 1:10].rearrange("p (l o) -> p l o", o=3), e3, r3.unsqueeze(2).broadcast_to([P, 3, 3]), ALU.mult))
            ch.link(v.tensor_scalar(e10[:, 0:1], e10[:, 0:1], 1.0, None, ALU.add))
            ch.link(v.reciprocal(w10[:, 0:1], e10[:, 0:1]))
            ch.link(v.tensor_tensor(w10, w10, rscale, ALU.mult))
            ch.link(v.tensor_scalar(nw10, w10, -1.0, None, ALU.mult))
            ch.link(v.tensor_scalar(app[3], app[3], w10[:, 0:1], None, ALU.mult))

        def haar_up(g, lv, k):
            ch = dwt_chain
            n = X // 4 ** lv
            w = D // 2 ** lv
            hb, vb, db = (det[lv][:, j * n:(j + 1) * n].rearrange("p (r c) -> p r c", c=w) for j in range(3))
            lowv = app[lv].rearrange("p (r c) -> p r c", c=w)
            sv = col_s[:, 0:2 * n].rearrange("p (r two c) -> p r two c", two=2, c=w)
            dv = col_d[:, 0:2 * n].rearrange("p (r two c) -> p r two c", two=2, c=w)
            v.scalar_tensor_tensor(sv[:, :, 0], hb, w10[:, k:k + 1], lowv, ALU.mult, ALU.add)
            v.scalar_tensor_tensor(sv[:, :, 1], hb, nw10[:, k:k + 1], lowv, ALU.mult, ALU.add)
            ch.link(v.tensor_scalar(vb, vb, w10[:, k + 1:k + 2], None, ALU.mult))
            v.scalar_tensor_tensor(dv[:, :, 0], db, w10[:, k + 2:k + 3], vb, ALU.mult, ALU.add)
            ch.link(v.scalar_tensor_tensor(dv[:, :, 1], db, nw10[:, k + 2:k + 3], vb, ALU.mult, ALU.add))
            if lv == 1:
                rec_stored.wait_before(dve, g, 1)
            ov = (rec if lv == 1 else app[lv - 1]).rearrange("p (n two) -> p n two", two=2)
            v.tensor_tensor(ov[:, :, 0], col_s[:, 0:2 * n], col_d[:, 0:2 * n], ALU.add)
            ins = v.tensor_tensor(ov[:, :, 1], col_s[:, 0:2 * n], col_d[:, 0:2 * n], ALU.subtract)
            if lv == 1:
                rec_ready.sig(ins)
                ch.end()
            else:
                ch.link(ins)

        with dve.Fori(0, NG - 1) as g:
            haar_down(g)
            small_dots()
            band_dots(1, 7)
            band_weights(g)
            haar_up(g, 3, 1)
            haar_up(g, 2, 4)
            haar_up(g, 1, 7)

        def splat_constants():
            dve.wait_ge(prep_act, 2)
            step(v.tensor_scalar(affT[:, 1:2], affT[:, 1:2], 0.1, 2.0, ALU.max, ALU.min))
            step(v.tensor_tensor(affT[:, 3:4], affT[:, 1:2], affT[:, 1:2], ALU.mult))
            step(v.reciprocal(affT[:, 4:5], affT[:, 3:4]))
            step(v.tensor_scalar(affT[:, 4:5], affT[:, 4:5], -0.5, None, ALU.mult))
            step(v.tensor_scalar(affT[:, 16:32], ident[0:K, 0:K], affT[:, 2:3], None, ALU.mult))
            step(v.tensor_scalar(affT[:, 32:48], ident[0:K, 0:K], affT[:, 4:5], None, ALU.mult))
            v.memset(x4[:, 0, 0:1], 0.0).then_inc(const_dve, 1)

        def turned_constants():
            dve.wait_ge(prep_pe, 1)
            step(v.tensor_copy(csq_b[:].rearrange("p a b -> p (a b)"), py[:, 0:32]))
            step(v.tensor_copy(cT[:].rearrange("p a b -> p (a b)"), py[:, 32:64]))
            v.tensor_copy(t0T.rearrange("p a b -> p (a b)"), px[:]).then_inc(const_dve, 1)

        def product_constant():
            dve.wait_ge(prep_pe, 2)
            v.tensor_copy(wvo[:].rearrange("p a b -> p (a b)"), py[:]).then_inc(const_dve, 1)
            dve.wait_ge(const_dve, 3)

        def stats(ch, src, st_, mv_, var_, ready):
            for t in range(NS):
                last = v.bn_stats(st_[:, t, :], src[:, t, :])
            ch.link(last, alone=passed_dve)
            for t in range(NS):
                last = v.bn_aggr(mv_[:, t, :], st_[:, t, :])
            ch.link(last)
            v.tensor_scalar(var_, mv_[:, :, 1], EPS, None, ALU.add).then_inc(ready.sem, 1)

        def normed(dst, src, mv_, rstd_):
            for t in range(NS):
                last = v.tensor_scalar(dst[:, t, :], src[:, t, :], mv_[:, t, 0:1], rstd_[:, t:t + 1], ALU.subtract, ALU.mult)
            return last

        def x3_of(i):
            return v3(x3[:, bass.ds((i % 2) * 512, 512)], 2)

        def token_stats(i):
            dve_a.start(dve, i)
            h_ld.wait(dve, i, 1, alone=passed_dve)
            stats(dve_a, h_t, st, mv, var, var_a)

        def normed_tokens(i):
            rstd_a.wait(dve, i, 1)
            px_written.wait_before(dve, i, 6)
            t0_ready.sig(normed(t0, h_t, mv, rstd))

        def distances(i):
            px_written.wait(dve, i, 2)
            tsq_ready.wait(dve, i, 1)
            dve_a.link(v.scalar_tensor_tensor(dist, px[:, 0:32].rearrange("p (a b) -> p a b", a=2), -2.0,
                                              csq_b[:, 0:1, :].broadcast_to([P, NS, K]), ALU.mult, ALU.add))
            dve_a.link(v.tensor_tensor(dist, dist, tsq.unsqueeze(2).broadcast_to([P, NS, K]), ALU.add))
            v.scalar_tensor_tensor(dist, dist, 0.0, csq_b[:, 1:2, :].broadcast_to([P, NS, K]), ALU.max, ALU.mult).then_inc(dist_ready.sem, 1)

        def affinities(i):
            aff_exp.wait(dve, i, 1)
            dve_a.link(v.tensor_reduce(affsum, aff, AX.X, ALU.add))
            dve_a.link(v.tensor_scalar(affsum, affsum, 1e-8, None, ALU.add))
            dve_a.link(v.reciprocal(affrec, affsum))
            v.tensor_tensor(aff, aff, affrec.unsqueeze(2).broadcast_to([P, NS, K]), ALU.mult).then_inc(aff_ready.sem, 1)

        def splat_residual(i):
            px_written.wait(dve, i, 5)
            h2_stored.wait_before(dve, i, 1)
            v.tensor_tensor(h2.rearrange("p a b -> p (a b)"), h_t.rearrange("p a b -> p (a b)"), px[:], ALU.add).then_inc(h2_ready.sem, 1)
            h2_ready.wait(dve, i, 1, alone=passed_dve)
            stats(dve_a, h2, st, mv, var, var_a)

        def normed_residual(i):
            rstd_a.wait(dve, i, 2)
            dve_a.link(normed(x3_of(i), h2, mv, rstd), alone=passed_dve)
            stats(dve_a, x3_of(i), st, mv, var, var_a)

        def attention_input(i):
            rstd_a.wait(dve, i, 3)
            hn_ready.sig(normed(t0, x3_of(i), mv, rstd))
            dve_a.end()

        def low_parts(i):
            k_hi.wait(dve, i, 1)
            v.tensor_tensor(qk_lo[:, 512:1024], big[:, 0, 512:1024], qk_hi[:, 512:1024], ALU.subtract).then_inc(k_lo.sem, 1)
            q_hi.wait(dve, i, 1)
            v.tensor_tensor(qk_lo[:, 0:512], big[:, 0, 0:512], qk_hi[:, 0:512], ALU.subtract).then_inc(big_dve.sem, 1)

        def first_k_stack(i):
            k_in_acc.wait(dve, i, 1)
            v.tensor_scalar(kst[:, 4:8], acc[:], kone[:, 0:1], None, ALU.add).then_inc(k_taken.sem, 1)

        def q_stack(i, u):
            big_written.wait(dve, i, u)
            v.tensor_copy(qst[:, 4:8].rearrange("p a b -> p (a b)"), big[:, 1, :]).then_inc(big_dve.sem, 1)

        def maxima(i, us):
            for u in us:
                big_written.wait(dve, i, FIRST + 1 + u)
                v.tensor_reduce(mx[:, :, 2 * u:2 * u + 2].rearrange("p c r -> p r c"),
                                big[:, u % 2, :].rearrange("p (r c k) -> p r c k", r=2, c=NS), AX.X, ALU.max,
                                negate=True).then_inc(big_dve.sem, 1)

        def maximum_parts(i):
            dve_b.start(dve, i)
            big_dve.wait(dve, i, 10)
            dve_b.link(v.tensor_copy(neghl[:, :, 0:H], mx))
            v.tensor_tensor(neghl[:, :, H:2 * H], mx, neghl[:, :, 0:H], ALU.subtract).then_inc(negm_ready.sem, 1)
            dve_b.end()

        def context(i, half):
            turned_, where = cturns[half], slice(2 * half, 2 * half + 2)
            ct4 = turned_.rearrange("p (e n d) -> p e n d", e=2, d=32)
            crec = dist.rearrange("p a b -> p (a b)")[:, 16 * half:16 * half + 16].rearrange("p (e n) -> p e n", e=2)
            packed = packs[half]
            if half == 0:
                dve_ctx.start(dve, i)
            pv_done.wait(dve, i, 4 + 4 * half)
            dve_ctx.link(v.transpose(turned_, acc[:, where].rearrange("p a b -> p (a b)")))
            dve_ctx.link(v.reciprocal(crec, ct4[:, :, :, DH]))
            for e in range(2):
                last = v.tensor_tensor(packed.rearrange("p (n e d) -> p e n d", e=2, d=DH)[:, e], ct4[:, e, :, 0:DH],
                                       crec[:, e].unsqueeze(2).broadcast_to([P, 8, DH]), ALU.mult)
            dve_ctx.link(last)
            if half == 0:
                pv_done.wait(dve, i, 6)
            last = v.transpose(ctxn[:, half], packed)
            if half == 0:
                dve_ctx.link(last)
            else:
                ctx_ready.sig(last)
                dve_ctx.end()

        def residual(i):
            dve_c.start(dve, i)
            py_written.wait(dve, i, 1)
            x4_stored.wait_before(dve, i, 1)
            v.tensor_tensor(x4, x3_of(i), py[:].rearrange("p (a b) -> p a b", a=2), ALU.add).then_inc(x4_ready.sem, 1)

        def residual_stats(i):
            x4_ready.wait(dve, i, 1, alone=passed_dve)
            stats(dve_c, x4, stc, mvc, varc, var_c)

        def expert_input(i):
            rstd_c.wait(dve, i, 1)
            py_written.wait_before(dve, i, 2)
            mhl_ready.wait_before(dve, i, 1)
            m0_ready.sig(normed(m, x4, mvc, rstdc))
            dve_c.end()

        def image_round(i, a_=True, b_=True, c_=True):
            if a_:
                token_stats(i + 1)
            if c_:
                context(i - 1, 0)
                context(i - 1, 1)
            if b_:
                low_parts(i)
            if a_:
                normed_tokens(i + 1)
            if b_:
                first_k_stack(i)
                q_stack(i, 4)
                maxima(i, range(0, 3))
            if a_:
                distances(i + 1)
            if b_:
                maxima(i, range(3, 5))
            if a_:
                affinities(i + 1)
            if b_:
                maxima(i, range(5, 8))
                maximum_parts(i)
            if c_:
                residual(i - 1)
            if a_:
                splat_residual(i + 1)
            if b_:
                q_stack(i, FIRST + 10)
            if a_:
                normed_residual(i + 1)
            if c_:
                residual_stats(i - 1)
            if a_:
                attention_input(i + 1)
            if c_:
                expert_input(i - 1)

        last_g = NG - 1
        splat_constants()
        haar_down(last_g)
        turned_constants()
        small_dots()
        product_constant()
        token_stats(0)
        band_dots(1, 7)
        normed_tokens(0)
        band_weights(last_g)
        distances(0)
        haar_up(last_g, 3, 1)
        affinities(0)
        haar_up(last_g, 2, 4)
        haar_up(last_g, 1, 7)
        splat_residual(0)
        normed_residual(0)
        attention_input(0)
        run_images(dve, image_round)

        m0_ready.wait(dve, B - 1, 1)
        dve.wait_ge(img_done_act, 1)
        dve.wait_ge(img_done_pe, 1)
        dve.wait_ge(r_pool, 4)
        rsteps = [0]

        def rstep(ins):
            rsteps[0] += 1
            ins.then_inc(r_dve, 1)
            dve.wait_ge(r_dve, rsteps[0])

        row = lambda t: t.unsqueeze(2).broadcast_to([P, NTL, E])
        v.tensor_copy(iota_f, iota_i)
        v.tensor_copy(iota_p, iota_pi)
        v.tensor_copy(slot_f, slot_i)
        rstep(v.tensor_copy(ident_bf[:], ident[:]))
        experts = iota_f[:, 0:E].unsqueeze(1).broadcast_to([P, NTL, E])
        v.memset(minus_p, -float(P))
        v.tensor_scalar(cols1, iota_f[:, 0:2 * NTL], 1.0, None, ALU.add)
        v.tensor_scalar(jstep, iota_f[:, 0:16], float(TT), None, ALU.mult)
        rstep(v.tensor_copy(iota_h, iota_f))

        def choose(l, mx_, mask):
            rstep(v.tensor_reduce(mx_, l, AX.X, ALU.max))
            rstep(v.tensor_tensor(te3(cand), l, row(mx_), ALU.is_lt))
            rstep(v.scalar_tensor_tensor(te3(cand), te3(cand), 16.0, experts, ALU.mult, ALU.add))
            rstep(v.tensor_reduce(pick, te3(cand), AX.X, ALU.min))
            rstep(v.tensor_tensor(te3(mask), experts, row(pick), ALU.is_equal))

        choose(lall[:], mx1, mask1)
        rstep(v.scalar_tensor_tensor(te3(lrest), te3(mask1), -1e30, lall[:], ALU.mult, ALU.add))
        choose(te3(lrest), mx2, mask2)
        rstep(v.tensor_tensor(mx2, mx2, mx1, ALU.subtract))
        rstep(v.tensor_tensor(cmask, mask1, mask2, ALU.add))
        assert rsteps[0] == ROUTE_MASKS
        dve.wait_ge(r_act, 1)
        rstep(v.tensor_scalar(mx1, wts[:, 1, :], 1.0, None, ALU.add))
        rstep(v.reciprocal(wts[:, 0, :], mx1))
        rstep(v.tensor_tensor(wts[:, 1, :], wts[:, 1, :], wts[:, 0, :], ALU.mult))
        dve.wait_ge(r_pe, 1)
        rstep(v.tensor_copy(ra, py[:, 0:NTL * E]))
        x, y = ra, rb_
        for s_ in (1, 2, 4, 8, 16):
            v.tensor_tensor(te3(y)[:, s_:], te3(x)[:, s_:], te3(x)[:, :NTL - s_], ALU.add)
            rstep(v.tensor_copy(te3(y)[:, :s_], te3(x)[:, :s_]))
            x, y = y, x
        count = te3(x)[:, NTL - 1, :]
        rstep(v.tensor_tensor(rank, x, py[:, 0:NTL * E], ALU.subtract))
        rstep(v.tensor_tensor(rank, rank, px[:, 0:NTL * E], ALU.add))
        cm3 = cmp.rearrange("p (e j) -> p e j", e=E)
        rstep(v.tensor_tensor(cm3, count.unsqueeze(2).broadcast_to([P, E, 16]), jstep.unsqueeze(1).broadcast_to([P, E, 16]), ALU.is_gt))
        rstep(v.tensor_reduce(ntile, cm3, AX.X, ALU.add))
        sq = cmp[:, 0:E * E].rearrange("p (e j) -> p e j", e=E)
        ie = iota_f[:, 0:E]
        rstep(v.tensor_tensor(sq, ie.unsqueeze(2).broadcast_to([P, E, E]), ie.unsqueeze(1).broadcast_to([P, E, E]), ALU.is_gt))
        rstep(v.tensor_tensor(sq, sq, ntile.unsqueeze(1).broadcast_to([P, E, E]), ALU.mult))
        rstep(v.tensor_reduce(tbase, sq, AX.X, ALU.add))
        rstep(v.tensor_tensor(tend, tbase, ntile, ALU.add))
        t3 = tcmp.rearrange("p (j e) -> p j e", e=E)
        rstep(v.tensor_tensor(t3, tend.unsqueeze(1).broadcast_to([P, NT, E]), iota_f[:, 0:NT].unsqueeze(2).broadcast_to([P, NT, E]), ALU.is_le))
        rstep(v.tensor_reduce(tef, t3, AX.X, ALU.add))
        rstep(v.tensor_scalar(tef, tef, float(E - 1), None, ALU.min))
        rstep(v.tensor_copy(tex[:], tef[0:1, :]))
        rstep(v.tensor_scalar(tbase, tbase, float(TT), None, ALU.mult))
        rstep(v.tensor_tensor(te3(rank), te3(rank), tbase.unsqueeze(1).broadcast_to([P, NTL, E]), ALU.add))
        for k, mask in enumerate((mask1, mask2)):
            rstep(v.tensor_tensor(mask, mask, rank, ALU.mult))
            rstep(v.tensor_reduce(pos[:, k * NTL:(k + 1) * NTL], te3(mask), AX.X, ALU.add))
        rstep(v.tensor_copy(pos_i, pos))
        v.tensor_scalar(posb_i, pos_i, P - 1, None, ALU.bitwise_and)
        rstep(v.tensor_scalar(posa_i, pos_i, 7, None, ALU.logical_shift_right))
        v.tensor_copy(posa, posa_i)
        rstep(v.tensor_copy(posb, posb_i))
        assert rsteps[0] == ROUTE_RANKS, rsteps[0]
        hot_ready.open(dve)
        with dve.Fori(0, 2 * NTL // (2 * HB)) as r:
            for u in range(2):
                where = bass.ds((r * 2 + u) * HB, HB)
                spread = lambda t, n: t[:, where].unsqueeze(2).broadcast_to([P, HB, n])
                hot_used.wait_before(dve, r, u + 1, alone=passed_dve)
                v.tensor_tensor(hotb[:, u], iota_h.unsqueeze(1).broadcast_to([P, HB, P]), spread(posb, P), ALU.is_equal)
                v.tensor_tensor(hot1[:, u], iota_h[:, 0:NCOL].unsqueeze(1).broadcast_to([P, HB, NCOL]), spread(posa, NCOL),
                                ALU.is_equal).then_inc(hot_ready.sem, 1)
        dve.wait_ge(r_pe, 2)
        rstep(v.scalar_tensor_tensor(tok, px[:, NCOL:2 * NCOL], float(P), minus_p, ALU.mult, ALU.add))
        rstep(v.tensor_tensor(tok, tok, px[:, 0:NCOL], ALU.add))
        rstep(v.tensor_scalar(emp, tok, -0.5, None, ALU.is_lt))
        rstep(v.tensor_tensor(emp, emp, slot_f, ALU.mult))
        rstep(v.tensor_tensor(dest, tok, emp, ALU.add))
        rstep(v.tensor_copy(dst_idx[:], dest))
        rstep(v.tensor_scalar(emp, tok, float(T), -float(T), ALU.is_ge, ALU.mult))
        rstep(v.tensor_tensor(tok, tok, emp, ALU.add))
        rstep(v.tensor_scalar(tok, tok, 0.0, None, ALU.max))
        v.tensor_copy(src_idx[:], tok).then_inc(route_done, 1)
        dve.wait_ge(route_done, 1)

        for c in (xT_lo_ready, split_done, y_ready, hi_chain):
            c.open(dve)
        dve.wait_ge(r_ld, 32)

        def split(j, half):
            sl = slice(half * (FC // 2), (half + 1) * (FC // 2))
            gelu_done.wait(dve, j, half + 1)
            down_done.wait_before(dve, j, 1)
            v.tensor_copy(h_hi[:, sl], hf[:, sl]).then_inc(hi_chain.sem, 1)
            hi_chain.wait(dve, j, half + 1)
            v.tensor_tensor(h_lo[:, sl], hf[:, sl], h_hi[:, sl], ALU.subtract).then_inc(split_done.sem, 1)

        def rows_in(j):
            xT_psum.wait(dve, j, 1)
            up_done.wait_before(dve, j, 2)
            v.tensor_copy(xT_lo.rearrange("p a b -> p (a b)"), py[:, 0:256].bitcast(BF16)).then_inc(xT_lo_ready.sem, 1)

        def rows_out(j, e):
            down_done.wait(dve, j, 1)
            y_free.wait_before(dve, j, 1)
            for t in range(2):
                last = v.scalar_tensor_tensor(ys[:, t, :], acc[:, 2 * t, :], 1.0 / WS, b2e[:, bass.ds(e * D, D)], ALU.mult, ALU.add)
            y_ready.sig(last)

        rows_in(0)
        rows_in(1)
        with dve.Fori(0, NT - 2) as j:
            split(j, 0)
            split(j, 1)
            rows_in(j + 2)
            rows_out(j, expert(dve, j))
        for j in (NT - 2, NT - 1):
            split(j, 0)
            split(j, 1)
            rows_out(j, expert(dve, j))

        c_done.open(dve)
        c_mid.open(dve)

        def combine(r, region, first):
            for k in range(CK):
                c_in[k].wait(dve, r, 2, alone=passed_dve)
                for n in range(2):
                    for t in range(NS):
                        tile = r * (2 * CK) + (2 * k + t)
                        o = region[:, bass.ds((tile - first) * D, D)]
                        last = v.scalar_tensor_tensor(o, yb[k][n][:, t, :], wts[:, n, :][:, bass.ds(tile, 1)], o, ALU.mult, ALU.add)
                    if n == 0:
                        c_mid.sig(last)
                        c_mid.wait(dve, r, k + 1, alone=passed_dve)
                c_done.sig(last)

        res_done.wait(dve, 2 * B - 1, 1)
        with dve.Fori(0, NRA // (2 * CK)) as r:
            combine(r, res_a, 0)
        combine(B // CK - 1, res_b, NRA)

    @block.tensor
    def _(pe):
        t_ = nc.tensor
        for c in (part_sum, px_written, big_written, negmT_psum, pv_done, py_written, k_projected, k_in_acc, v_in_acc):
            c.open(pe)
        pe.wait_ge(const_pool, 9 + G4)
        def part_sums(g):
            part_ready.wait(pe, g, 1)
            product_sum.wait(pe, g, 1)
            t_.matmul(px[:, 0:10], blk[:], part, start=True, stop=True).then_inc(part_sum.sem, 1)
        with pe.Fori(0, NG - 1) as g:
            part_sums(g)
        pe.wait_ge(const_dve, 1)
        dwt_logits.wait(pe, NG - 2, 1)
        t_.matmul(py[:, 0:32], ones[0:K, :], affT[:, 16:48], start=True, stop=True)
        for c in range(NC):
            t_.transpose(py[:, 32 + 16 * c:48 + 16 * c], zs[:, c * P:(c + 1) * P], ident[0:K, 0:K])
        for c in range(NC):
            for k in range(NC):
                last = t_.transpose(px[:, k * 256 + c * P:k * 256 + (c + 1) * P], h_t[:, c, k * P:(k + 1) * P], ident[:])
        last.then_inc(prep_pe, 1)
        pe.wait_ge(const_dve, 2)
        for c in range(NC):
            for k in range(NC):
                last = t_.matmul(py[:, c * 256:(c + 1) * 256], t0T[:, k, c * P:(c + 1) * P], t0[:, k, :], start=(k == 0), stop=(k == NC - 1))
        last.then_inc(prep_pe, 1)
        pe.wait_ge(const_dve, 3)
        part_sums(NG - 1)
        dwt_logits.wait(pe, NG - 1, 1)

        def turned(dst, src):
            for c in range(NC):
                for t in range(NS):
                    last = t_.transpose(dst[:, c * 256 + t * P:c * 256 + (t + 1) * P], src[:, t, c * P:(c + 1) * P], ident[:])
            return last

        def splat_tokens(i):
            t0_ready.wait(pe, i, 1)
            hhT_ready.wait_before(pe, i, 1)
            px_written.sig(turned(px, t0))

        def splat_products(i):
            t0T_ready.wait(pe, i, 1)
            for t in range(NS):
                for c in range(NC):
                    last = t_.matmul(px[:, t * K:(t + 1) * K], t0T[:, c, t * P:(t + 1) * P], cT[:, c, :], start=(c == 0), stop=(c == NC - 1))
            px_written.sig(last)

        def splat_sums(i):
            aff_ready.wait(pe, i, 1)
            for c in range(NC):
                for t in range(NS):
                    t_.matmul(px[:, c * K:(c + 1) * K], t0[:, t, c * P:(c + 1) * P], aff[:, t, :], start=(t == 0), stop=(t == NS - 1))
            for t in range(NS):
                last = t_.transpose(px[0:K, 256 + t * P:256 + (t + 1) * P], aff[:, t, :], ident[:])
            px_written.sig(last)

        def splat_states(i):
            ut_ready.wait(pe, i, 1)
            for c in range(NC):
                last = t_.matmul(px[0:K, 0:256], ut[:, c, :], wvo[:, c, :], start=(c == 0), stop=(c == NC - 1))
            px_written.sig(last)

        def splat_output(i):
            z_ready.wait(pe, i, 1)
            for t in range(NS):
                last = t_.matmul(px[:, t * 256:(t + 1) * 256], affT[:, t * P:(t + 1) * P], zs, start=True, stop=True)
            px_written.sig(last)

        def attention_input(i):
            hn_ready.wait(pe, i, 1)
            px_written.sig(turned(px, t0))

        def stack_half(dst, half, q, parts, with_max=False):
            hi, lo = parts
            for k in range(4):
                s = 4 * half + k
                src = (q * 2 + s // 4) * 256
                to = dst[:, k * 256:(k + 1) * 256]
                t_.matmul(to, sel[:, hi, s % 4, :], qk_hi[:, src:src + 256], start=True, stop=False)
                last = t_.matmul(to, sel[:, lo, s % 4, :], qk_lo[:, src:src + 256], start=False, stop=not with_max)
                if with_max:
                    last = t_.matmul(to, selm[:, s, :, :].rearrange("p r c -> p (r c)"), negmT, start=False, stop=True)
            return last

        def ring_half(i, u, half, q, parts, with_max=False):
            slot_free(i, u)
            big_written.sig(stack_half(big[:, u % 2, :], half, q, parts, with_max))

        def scores(i, u, s, turned_):
            slot_free(i, u)
            for c in range(NS):
                for r in range(2):
                    rows = slice(64 * r, 64 * r + 64)
                    x, y = (kst, qst) if turned_ else (qst, kst)
                    dst = big[:, u % 2, r * 512 + c * 256:r * 512 + (c + 1) * 256]
                    last = t_.matmul(dst, x[rows, s, c * P:(c + 1) * P], y[rows, s, :], start=True, stop=True)
            big_written.sig(last)

        def context(i, s):
            big_act.wait(pe, i, 4 + s)
            for c in range(NS):
                for r in range(2):
                    h = 2 * s + r
                    j = h % 4
                    last = t_.matmul(acc[32 * j:32 * j + 32, h // 4, :], vext[:, c, h, :], probs[s % 3][:, r, c, :],
                                     start=(c == 0), stop=(c == NS - 1), tile_position=(0, 32 * j))
            pv_done.sig(last)

        def projections(i):
            hhT_ready.wait(pe, i, 1)
            slot_free(i, 0)
            for q, w in ((1, wk_), (0, wq)):
                for o in range(NC):
                    for c in range(NC):
                        last = t_.matmul(big[:, 0, q * 512 + o * 256:q * 512 + (o + 1) * 256], w[:, c, o * P:(o + 1) * P], hhT[:, c, :],
                                         start=(c == 0), stop=(c == NC - 1))
                if q == 1:
                    k_projected.sig(last)
            big_written.sig(last)

        def values(i, t):
            if t == 0:
                k_taken.wait(pe, i, 1)
            for c in range(NC):
                last = t_.matmul(acc[:, t, :], hhT[:, c, t * P:(t + 1) * P], wv[:, c, :], start=(c == 0), stop=(c == NC - 1))
            if t == 1:
                v_in_acc.sig(last)

        def first_stacks(i):
            k_lo.wait(pe, i, 1)
            ring_half(i, 1, 0, 1, (0, 1))
            ctx_ready.wait_before(pe, i, 1)
            k_in_acc.sig(stack_half(acc[:].rearrange("p a b -> p (a b)"), 1, 1, (0, 1)))
            big_dve.wait(pe, i, 1)
            ring_half(i, 2, 0, 0, (2, 3))
            ring_half(i, 3, 1, 0, (2, 3))

        def keep_clock(n):
            for _ in range(n):
                t_.matmul(acc[:, 3, :], ident16[:], sel[:, 0, 0:2, :].rearrange("p a b -> p (a b)"), start=True, stop=True)

        def first_scores(i, ss):
            for s in ss:
                if s == 0:
                    big_act.wait(pe, i, 2)
                if s == 4:
                    big_dve.wait(pe, i, 2)
                    k_taken.wait(pe, i, 1)
                scores(i, FIRST + s, s, False)

        def maximum_rows(i):
            negm_ready.wait(pe, i, 1)
            v_taken.wait(pe, i, 1)
            for c in range(NS):
                last = t_.transpose(acc[0:32, 0, c * 64:(c + 1) * 64].bitcast(F16), neghl[:, c, :], ident16[:])
            negmT_psum.sig(last)

        def second_stacks(i):
            negmT_ready.wait(pe, i, 1)
            ring_half(i, SECOND - 2, 0, 0, (2, 3), True)
            ring_half(i, SECOND - 1, 1, 0, (2, 3), True)

        def attention(i, ss):
            for s in ss:
                if s == 0:
                    big_act.wait(pe, i, 3)
                if s == 4:
                    big_dve.wait(pe, i, 11)
                scores(i, SECOND + s, s, True)
                if s >= 2:
                    context(i, s - 2)

        def output_projection(i, t, ks):
            if (t, ks[0]) == (0, 0):
                ctx_ready.wait(pe, i, 1)
                logit_read.wait_before(pe, i, 1)
            for k in ks:
                last = t_.matmul(py[:, t * 256:(t + 1) * 256], ctxn[:, k, t * P:(t + 1) * P], wop[:, k, :], start=(k == 0), stop=(k == 1))
            if (t, k) == (1, 1):
                py_written.sig(last)

        def router_tokens(i):
            m_ready.wait(pe, i, 1)
            py_written.sig(turned(py, m))

        def router_logits(i):
            mT_ready.wait(pe, i, 1)
            for t in range(NS):
                for c in range(NC):
                    last = t_.matmul(py[:, t * E:(t + 1) * E], mT[:, c, t * P:(t + 1) * P], wg[:, c, :], start=(c == 0), stop=(c == NC - 1))
            py_written.sig(last)

        def image_round(i, a_=True, b_=True, c_=True, m_=True):
            if b_:
                ctx_ready.wait_before(pe, i, 1)
                first_stacks(i)
            if m_:
                router_logits(i - 2)
            if a_:
                splat_tokens(i + 1)
            if b_:
                first_scores(i, (0,))
            if b_:
                first_scores(i, (1,))
                values(i, 0)
                first_scores(i, (2,))
            if a_:
                splat_products(i + 1)
            if b_:
                first_scores(i, (3,))
                values(i, 1)
            if b_:
                first_scores(i, (4,))
            if c_:
                output_projection(i - 1, 0, (0, 1))
            if b_:
                first_scores(i, (5,))
            if c_:
                output_projection(i - 1, 1, (0, 1))
            if b_:
                first_scores(i, (6,))
            if a_:
                splat_sums(i + 1)
            if b_:
                first_scores(i, (7,))
            if a_:
                splat_states(i + 1)
            if b_:
                keep_clock(2)
                maximum_rows(i)
                keep_clock(2)
            if a_:
                splat_output(i + 1)
            if b_:
                second_stacks(i)
                attention(i, range(0, 6))
            if a_:
                attention_input(i + 1)
            if b_:
                attention(i, range(6, 8))
            if c_:
                router_tokens(i - 1)
            if b_:
                context(i, 6)
                context(i, 7)
            if a_:
                projections(i + 1)

        splat_tokens(0)
        splat_products(0)
        splat_sums(0)
        splat_states(0)
        splat_output(0)
        attention_input(0)
        projections(0)
        run_images_late(pe, image_round)
        py_written.wait(pe, B - 1, 3)
        pe.sem_inc(img_done_pe, 1)
        for c in (hot_used, xT_psum, up_done, down_done):
            c.open(pe)
        pe.wait_ge(tri_ready, 1)
        pe.wait_ge(r_dve, ROUTE_MASKS)
        t_.matmul(px[:, 0:NTL * E], tri[:], cmask, start=True, stop=True)
        t_.matmul(py[:, 0:NTL * E], ones[:], cmask, start=True, stop=True).then_inc(r_pe, 1)
        pe.wait_ge(r_dve, ROUTE_RANKS)
        t_.matmul(px[:, 0:2 * NCOL], zero16[:, 0:P], zero16[:, 0:2 * NCOL], start=True, stop=False)
        with pe.Fori(0, 2 * NTL // (2 * HB)) as r:
            for u in range(2):
                hot_rows.wait(pe, r, u + 1)
                hot_cols.wait(pe, r, u + 1)
                for n in range(HB):
                    last = t_.matmul(px[:, 0:2 * NCOL], hotb[:, u, n, :], hota[:, u, n].rearrange("p v a -> p (v a)"), start=False, stop=False)
                hot_used.sig(last)
        t_.matmul(px[:, 0:2 * NCOL], zero16[:, 0:P], zero16[:, 0:2 * NCOL], start=False, stop=True).then_inc(r_pe, 1)

        pe.wait_ge(route_done, 1)

        def turn(j):
            x_in.wait(pe, j, 2)
            for c in range(NC):
                for t in range(2):
                    o = slice(c * 128 + t * 64, c * 128 + (t + 1) * 64)
                    t_.transpose(px[:, o].bitcast(F16), xg[:, t, c * P:(c + 1) * P], ident16[:])
                    last = t_.transpose(py[:, o].bitcast(BF16), xg[:, t, D + c * P:D + (c + 1) * P].bitcast(BF16), ident_bf[:])
            xT_psum.sig(last)

        def up(j, e):
            xT_hi_ready.wait(pe, j, 1)
            xT_lo_ready.wait(pe, j, 1)
            for half in range(2):
                gelu_done.wait_before(pe, j, half + 1)
                for k in range(FC // 2):
                    f = half * (FC // 2) + k
                    dst = big[:, half, k * TT:(k + 1) * TT]
                    for n, (w, x) in enumerate(((w1hi, xT_hi), (w1hi, xT_lo), (w1lo, xT_hi))):
                        for c in range(NC):
                            last = t_.matmul(dst, w[:, bass.ds(e * (NC * F) + (c * F + f * P), P)], x[:, c, :],
                                             start=(n == 0 and c == 0), stop=(n == 2 and c == NC - 1))
                up_done.sig(last)

        def down(j, e):
            y_ready.wait_before(pe, j, 1)
            split_done.wait(pe, j, 2)
            for t in range(2):
                for f in range(FC):
                    for n, (x, w) in enumerate(((h_hi, w2hi), (h_hi, w2lo), (h_lo, w2hi))):
                        last = t_.matmul(acc[:, 2 * t, :], x[:, f, t * P:(t + 1) * P], w[:, bass.ds(e * (FC * D) + f * D, D)],
                                         start=(f == 0 and n == 0), stop=(f == FC - 1 and n == 2))
            down_done.sig(last)

        turn(0)
        up(0, expert(pe, 0))
        turn(1)
        with pe.Fori(0, NT - 2) as j:
            up(j + 1, expert(pe, j + 1))
            turn(j + 2)
            down(j, expert(pe, j))
        up(NT - 1, expert(pe, NT - 1))
        down(NT - 2, expert(pe, NT - 2))
        down(NT - 1, expert(pe, NT - 1))


def kernel(**inputs):
    import numpy as np
    import concourse.bacc as bacc
    from concourse.bass_utils import run_bass_kernel_spmd

    nc = bacc.Bacc("TRN2", target_bir_lowering=False, num_devices=1)
    arrays, aps = {}, {}
    for name, value in inputs.items():
        arr = np.ascontiguousarray(value)
        arrays[f"in_{name}"] = arr
        aps[name] = nc.dram_tensor(f"in_{name}", arr.shape, mybir.dt.from_np(arr.dtype), kind="ExternalInput").ap()
    out = nc.dram_tensor("out_0", (B, S, D), F32, kind="ExternalOutput").ap()
    tower(nc, aps, out)
    r = run_bass_kernel_spmd(nc, [arrays], core_ids=[0])
    return r.results[0]["out_0"]
```
